# Optimizing a Trainium2 kernel written in Bass

```python
import numpy as np
import jax
import jax.numpy as jnp

def _softmax(x, axis=-1):
    return jax.nn.softmax(x, axis=axis)

def _gelu(x):
    return jax.nn.gelu(x, approximate=True)

def _silu(x):
    return jax.nn.silu(x)

def _sigmoid(x):
    return jax.nn.sigmoid(x)

def _layernorm(x, axis=-1, eps=1e-05):
    m = jnp.mean(x, axis=axis, keepdims=True)
    v = jnp.var(x, axis=axis, keepdims=True)
    return (x - m) / jnp.sqrt(v + eps)

def _scatter_add(tgt, idx, src, axis=0):
    return tgt.at[idx].add(src)

def _segment_sum(src, seg, n):
    return jax.ops.segment_sum(src, seg, n)
kernel_name = 'mk_vit_tower_cls_d1_tok_img2048_r4_21a9fa'

def setup_inputs(seed: int=0):
    np.random.seed(seed)
    _w = jnp.asarray

    def _rec_inputs():
        import jax
        import jax.numpy as jnp
        _rk = jax.random.key(seed)
        x = -0.00340659 + 1.00146 * jax.random.normal(jax.random.fold_in(_rk, 1), (16, 256, 64, 2), jnp.float32)
        cls_tok = 0.02 * jax.random.normal(jax.random.fold_in(_rk, 5), (1, 1, 512), jnp.float32)
        return (x, cls_tok)
    x, cls_tok = _rec_inputs()

    def _L0_tok_setup():
        import jax, jax.numpy as jnp
        import numpy as np
        CH, H, N, N_SSM, SEQ_L = (1, 256, 64, 256, 512)

        def _kernel(C_ri, log_dt, B_ri, inv_A_real, A_imag, L):
            C = C_ri[..., 0] + 1j * C_ri[..., 1]
            B = B_ri[..., 0] + 1j * B_ri[..., 1]
            A = -jnp.exp(inv_A_real) + 1j * A_imag
            rep = log_dt.shape[0] // inv_A_real.shape[0]
            B = jnp.tile(B, (rep, 1))
            A = jnp.tile(A, (rep, 1))
            dt = jnp.exp(log_dt)
            dtA = A * dt[:, None]
            Ct = B[None] * C / (1.0 - dtA / 2) * dt[:, None]
            dA = (1.0 + dtA / 2) / (1.0 - dtA / 2)
            dA_log = jnp.log(dA)
            l = jnp.arange(L, dtype=jnp.float32)
            V = jnp.exp(dA_log[:, :, None] * l)
            K = 2.0 * jnp.einsum('chn,hnl->chl', Ct, V).real
            return K
        key = jax.random.key(seed)
        ks = jax.random.split(key, 5)
        return {'C_ri': jax.random.normal(ks[0], (CH, H, N, 2), dtype=jnp.float32), 'log_dt': jax.random.normal(ks[1], (H,), dtype=jnp.float32), 'B_ri': jax.random.normal(ks[2], (N_SSM, N, 2), dtype=jnp.float32), 'inv_A_real': jax.random.normal(ks[3], (N_SSM, N), dtype=jnp.float32), 'A_imag': jax.random.normal(ks[4], (N_SSM, N), dtype=jnp.float32), 'L': SEQ_L}
    _L0_tok_all = _L0_tok_setup()
    _L0_tok_in = {k: v for k, v in _L0_tok_all.items() if k in ('log_dt', 'B_ri', 'inv_A_real', 'A_imag')}
    del _L0_tok_all

    def _L0_attn_setup():
        import jax, jax.numpy as jnp
        from jax import lax
        import numpy as np
        B, L, D_MODEL = (1, 256, 512)
        H, P, G, S = (32, 64, 8, 32)
        D_SSM = H * P
        CONV_DIM = D_SSM + 2 * G * S
        PROJ_DIM = 2 * D_SSM + 2 * G * S + H
        K = 4
        EPS = 1e-05

        def _forward(hidden_states, W_in, b_in, conv_w, conv_b, A_log, D_param, dt_bias, norm_w, W_out, b_out, mup_vector):
            Bb, Ll, _ = hidden_states.shape
            zxbcdt = (hidden_states @ W_in + b_in) * mup_vector
            z = zxbcdt[..., :D_SSM]
            xBC = zxbcdt[..., D_SSM:D_SSM + CONV_DIM]
            dt = zxbcdt[..., D_SSM + CONV_DIM:]
            xBC_t = jnp.transpose(xBC, (0, 2, 1))
            conv = lax.conv_general_dilated(xBC_t, conv_w[:, None, :], (1,), [(K - 1, 0)], dimension_numbers=('NCH', 'OIH', 'NCH'), feature_group_count=CONV_DIM)
            xBC = jnp.transpose(jax.nn.silu(conv + conv_b[None, :, None]), (0, 2, 1))
            x = xBC[..., :D_SSM].reshape(Bb, Ll, H, P)
            Bm = xBC[..., D_SSM:D_SSM + G * S].reshape(Bb, Ll, G, S)
            Cm = xBC[..., D_SSM + G * S:].reshape(Bb, Ll, G, S)
            rep = H // G
            Bh = jnp.repeat(Bm, rep, axis=2)
            Ch = jnp.repeat(Cm, rep, axis=2)
            dt = jax.nn.softplus(dt + dt_bias)
            a = jnp.exp(dt * -jnp.exp(A_log))
            db = dt[..., None, None] * x[..., None] * Bh[:, :, :, None, :]

            def combine(e1, e2):
                a1, s1 = e1
                a2, s2 = e2
                return (a1 * a2, a2[..., None, None] * s1 + s2)
            states = lax.associative_scan(combine, (a, db), axis=1)[1]
            y = jnp.einsum('blhps,blhs->blhp', states, Ch) + D_param[None, None, :, None] * x
            y = y.reshape(Bb, Ll, D_SSM) * jax.nn.silu(z)
            yg = y.reshape(Bb, Ll, G, D_SSM // G)
            var = jnp.mean(yg * yg, axis=-1, keepdims=True)
            y = (yg * lax.rsqrt(var + EPS)).reshape(Bb, Ll, D_SSM) * norm_w
            return y @ W_out + b_out
        key = jax.random.key(seed)
        ks = jax.random.split(key, 12)
        mults = np.array([0.9, 1.1, 0.8, 1.2, 1.0], dtype=np.float32)
        mv = np.ones(PROJ_DIM, dtype=np.float32)
        mv[:D_SSM] *= mults[0]
        mv[D_SSM:2 * D_SSM] *= mults[1]
        mv[2 * D_SSM:2 * D_SSM + G * S] *= mults[2]
        mv[2 * D_SSM + G * S:2 * D_SSM + 2 * G * S] *= mults[3]
        mv[2 * D_SSM + 2 * G * S:] *= mults[4]
        return {'hidden_states': jax.random.normal(ks[0], (B, L, D_MODEL), jnp.float32), 'W_in': jax.random.normal(ks[1], (D_MODEL, PROJ_DIM), jnp.float32) * 0.02, 'b_in': jax.random.normal(ks[2], (PROJ_DIM,), jnp.float32) * 0.01, 'conv_w': jax.random.normal(ks[3], (CONV_DIM, K), jnp.float32) * 0.2, 'conv_b': jax.random.normal(ks[4], (CONV_DIM,), jnp.float32) * 0.01, 'A_log': jnp.log(jax.random.uniform(ks[5], (H,), jnp.float32, 1.0, 16.0)), 'D_param': jax.random.normal(ks[6], (H,), jnp.float32) * 0.5 + 1.0, 'dt_bias': jax.random.normal(ks[7], (H,), jnp.float32) * 0.5, 'norm_w': jnp.ones((D_SSM,), jnp.float32) + 0.01 * jax.random.normal(ks[8], (D_SSM,), jnp.float32), 'W_out': jax.random.normal(ks[9], (D_SSM, D_MODEL), jnp.float32) * 0.02, 'b_out': jnp.zeros((D_MODEL,), jnp.float32), 'mup_vector': jnp.asarray(mv)}
    _L0_attn_all = _L0_attn_setup()
    _L0_attn_in = {k: v for k, v in _L0_attn_all.items() if k in ('W_in', 'b_in', 'conv_w', 'conv_b', 'A_log', 'D_param', 'dt_bias', 'norm_w', 'W_out', 'b_out', 'mup_vector')}
    del _L0_attn_all

    def _L0_ffn_setup():
        import jax, jax.numpy as jnp
        import numpy as np
        HIDDEN = 512
        INTER = 2048
        SCALE = 64.0

        def fwht(x):
            orig_shape = x.shape
            n = orig_shape[-1]
            x = x.reshape(-1, n)
            h = 1
            while h < n:
                x = x.reshape(-1, n // (2 * h), 2, h)
                a, b = (x[:, :, 0, :], x[:, :, 1, :])
                x = jnp.stack([a + b, a - b], axis=2).reshape(-1, n)
                h *= 2
            return (x / jnp.sqrt(jnp.asarray(n, x.dtype))).reshape(orig_shape)
        key = jax.random.key(seed)
        ks = jax.random.split(key, 8)
        inp = jax.random.normal(ks[0], (4, 512, HIDDEN), dtype=jnp.float32)
        SU_ug = jnp.where(jax.random.bernoulli(ks[1], 0.5, (HIDDEN,)), 1.0, -1.0).astype(jnp.float32)
        SU_dp = jnp.where(jax.random.bernoulli(ks[2], 0.5, (INTER,)), 1.0, -1.0).astype(jnp.float32)
        Wscale_ug = jax.random.uniform(ks[3], (2 * INTER,), jnp.float32, 0.5, 1.5)
        Wscale_dp = jax.random.uniform(ks[4], (HIDDEN,), jnp.float32, 0.5, 1.5)
        W_up = jax.random.normal(ks[5], (INTER, HIDDEN), dtype=jnp.float32) * 0.02
        W_gate = jax.random.normal(ks[6], (INTER, HIDDEN), dtype=jnp.float32) * 0.02
        W_down = jax.random.normal(ks[7], (HIDDEN, INTER), dtype=jnp.float32) * 0.02
        return {'input': inp, 'SU_ug': SU_ug, 'SU_dp': SU_dp, 'Wscale_ug': Wscale_ug, 'Wscale_dp': Wscale_dp, 'W_up': W_up, 'W_gate': W_gate, 'W_down': W_down}
    _L0_ffn_all = _L0_ffn_setup()
    _L0_ffn_in = {k: v for k, v in _L0_ffn_all.items() if k in ('SU_ug', 'SU_dp', 'Wscale_ug', 'Wscale_dp', 'W_up', 'W_gate', 'W_down')}
    del _L0_ffn_all
    return {'x': x, 'cls_tok': cls_tok, 'L0_tok_log_dt': _L0_tok_in['log_dt'], 'L0_tok_B_ri': _L0_tok_in['B_ri'], 'L0_tok_inv_A_real': _L0_tok_in['inv_A_real'], 'L0_tok_A_imag': _L0_tok_in['A_imag'], 'L0_attn_W_in': _L0_attn_in['W_in'], 'L0_attn_b_in': _L0_attn_in['b_in'], 'L0_attn_conv_w': _L0_attn_in['conv_w'], 'L0_attn_conv_b': _L0_attn_in['conv_b'], 'L0_attn_A_log': _L0_attn_in['A_log'], 'L0_attn_D_param': _L0_attn_in['D_param'], 'L0_attn_dt_bias': _L0_attn_in['dt_bias'], 'L0_attn_norm_w': _L0_attn_in['norm_w'], 'L0_attn_W_out': _L0_attn_in['W_out'], 'L0_attn_b_out': _L0_attn_in['b_out'], 'L0_attn_mup_vector': _L0_attn_in['mup_vector'], 'L0_ffn_SU_ug': _L0_ffn_in['SU_ug'], 'L0_ffn_SU_dp': _L0_ffn_in['SU_dp'], 'L0_ffn_Wscale_ug': _L0_ffn_in['Wscale_ug'], 'L0_ffn_Wscale_dp': _L0_ffn_in['Wscale_dp'], 'L0_ffn_W_up': _L0_ffn_in['W_up'], 'L0_ffn_W_gate': _L0_ffn_in['W_gate'], 'L0_ffn_W_down': _L0_ffn_in['W_down']}

def reference(x, cls_tok, L0_tok_log_dt, L0_tok_B_ri, L0_tok_inv_A_real, L0_tok_A_imag, L0_attn_W_in, L0_attn_b_in, L0_attn_conv_w, L0_attn_conv_b, L0_attn_A_log, L0_attn_D_param, L0_attn_dt_bias, L0_attn_norm_w, L0_attn_W_out, L0_attn_b_out, L0_attn_mup_vector, L0_ffn_SU_ug, L0_ffn_SU_dp, L0_ffn_Wscale_ug, L0_ffn_Wscale_dp, L0_ffn_W_up, L0_ffn_W_gate, L0_ffn_W_down):
    import jax
    import jax.numpy as jnp

    def _L0_tok_ref(C_ri, log_dt, B_ri, inv_A_real, A_imag, L):
        import jax, jax.numpy as jnp
        import numpy as np
        CH, H, N, N_SSM, SEQ_L = (1, 256, 64, 256, 512)

        def _kernel(C_ri, log_dt, B_ri, inv_A_real, A_imag, L):
            C = C_ri[..., 0] + 1j * C_ri[..., 1]
            B = B_ri[..., 0] + 1j * B_ri[..., 1]
            A = -jnp.exp(inv_A_real) + 1j * A_imag
            rep = log_dt.shape[0] // inv_A_real.shape[0]
            B = jnp.tile(B, (rep, 1))
            A = jnp.tile(A, (rep, 1))
            dt = jnp.exp(log_dt)
            dtA = A * dt[:, None]
            Ct = B[None] * C / (1.0 - dtA / 2) * dt[:, None]
            dA = (1.0 + dtA / 2) / (1.0 - dtA / 2)
            dA_log = jnp.log(dA)
            l = jnp.arange(L, dtype=jnp.float32)
            V = jnp.exp(dA_log[:, :, None] * l)
            K = 2.0 * jnp.einsum('chn,hnl->chl', Ct, V).real
            return K
        return _kernel(C_ri, log_dt, B_ri, inv_A_real, A_imag, L)

    def _L0_attn_ref(hidden_states, W_in, b_in, conv_w, conv_b, A_log, D_param, dt_bias, norm_w, W_out, b_out, mup_vector):
        import jax, jax.numpy as jnp
        from jax import lax
        import numpy as np
        B, L, D_MODEL = (1, 256, 512)
        H, P, G, S = (32, 64, 8, 32)
        D_SSM = H * P
        CONV_DIM = D_SSM + 2 * G * S
        PROJ_DIM = 2 * D_SSM + 2 * G * S + H
        K = 4
        EPS = 1e-05

        def _forward(hidden_states, W_in, b_in, conv_w, conv_b, A_log, D_param, dt_bias, norm_w, W_out, b_out, mup_vector):
            Bb, Ll, _ = hidden_states.shape
            zxbcdt = (hidden_states @ W_in + b_in) * mup_vector
            z = zxbcdt[..., :D_SSM]
            xBC = zxbcdt[..., D_SSM:D_SSM + CONV_DIM]
            dt = zxbcdt[..., D_SSM + CONV_DIM:]
            xBC_t = jnp.transpose(xBC, (0, 2, 1))
            conv = lax.conv_general_dilated(xBC_t, conv_w[:, None, :], (1,), [(K - 1, 0)], dimension_numbers=('NCH', 'OIH', 'NCH'), feature_group_count=CONV_DIM)
            xBC = jnp.transpose(jax.nn.silu(conv + conv_b[None, :, None]), (0, 2, 1))
            x = xBC[..., :D_SSM].reshape(Bb, Ll, H, P)
            Bm = xBC[..., D_SSM:D_SSM + G * S].reshape(Bb, Ll, G, S)
            Cm = xBC[..., D_SSM + G * S:].reshape(Bb, Ll, G, S)
            rep = H // G
            Bh = jnp.repeat(Bm, rep, axis=2)
            Ch = jnp.repeat(Cm, rep, axis=2)
            dt = jax.nn.softplus(dt + dt_bias)
            a = jnp.exp(dt * -jnp.exp(A_log))
            db = dt[..., None, None] * x[..., None] * Bh[:, :, :, None, :]

            def combine(e1, e2):
                a1, s1 = e1
                a2, s2 = e2
                return (a1 * a2, a2[..., None, None] * s1 + s2)
            states = lax.associative_scan(combine, (a, db), axis=1)[1]
            y = jnp.einsum('blhps,blhs->blhp', states, Ch) + D_param[None, None, :, None] * x
            y = y.reshape(Bb, Ll, D_SSM) * jax.nn.silu(z)
            yg = y.reshape(Bb, Ll, G, D_SSM // G)
            var = jnp.mean(yg * yg, axis=-1, keepdims=True)
            y = (yg * lax.rsqrt(var + EPS)).reshape(Bb, Ll, D_SSM) * norm_w
            return y @ W_out + b_out
        return _forward(hidden_states, W_in, b_in, conv_w, conv_b, A_log, D_param, dt_bias, norm_w, W_out, b_out, mup_vector)

    def _L0_ffn_ref(input, SU_ug, SU_dp, Wscale_ug, Wscale_dp, W_up, W_gate, W_down):
        import jax, jax.numpy as jnp
        import numpy as np
        HIDDEN = 512
        INTER = 2048
        SCALE = 64.0

        def fwht(x):
            orig_shape = x.shape
            n = orig_shape[-1]
            x = x.reshape(-1, n)
            h = 1
            while h < n:
                x = x.reshape(-1, n // (2 * h), 2, h)
                a, b = (x[:, :, 0, :], x[:, :, 1, :])
                x = jnp.stack([a + b, a - b], axis=2).reshape(-1, n)
                h *= 2
            return (x / jnp.sqrt(jnp.asarray(n, x.dtype))).reshape(orig_shape)
        n = SU_ug.shape[0]
        x = input.reshape(-1, n)
        x = fwht(x * SU_ug) / SCALE
        x_up = x @ W_up.T * (Wscale_ug[:INTER] * SCALE)
        x_gate = x @ W_gate.T * (Wscale_ug[INTER:] * SCALE)
        x = jax.nn.silu(x_gate) * x_up
        x = fwht(x * SU_dp) / SCALE
        x = x @ W_down.T * (Wscale_dp * SCALE)
        return x.reshape(input.shape)
    h = _L0_tok_ref(x, L0_tok_log_dt, L0_tok_B_ri, L0_tok_inv_A_real, L0_tok_A_imag, 512)
    h = jnp.concatenate([jnp.broadcast_to(cls_tok, (h.shape[0], 1, h.shape[2])), h], axis=1)
    h = h + _L0_attn_ref(_layernorm(h, axis=-1), L0_attn_W_in, L0_attn_b_in, L0_attn_conv_w, L0_attn_conv_b, L0_attn_A_log, L0_attn_D_param, L0_attn_dt_bias, L0_attn_norm_w, L0_attn_W_out, L0_attn_b_out, L0_attn_mup_vector)
    h = h + _L0_ffn_ref(_layernorm(h, axis=-1), L0_ffn_SU_ug, L0_ffn_SU_dp, L0_ffn_Wscale_ug, L0_ffn_Wscale_dp, L0_ffn_W_up, L0_ffn_W_gate, L0_ffn_W_down)
    return h

_drawn_inputs = setup_inputs


def setup_inputs(seed=0):
    import zlib

    import numpy as np

    out = dict(_drawn_inputs(seed))
    spreads = {'L0_attn_b_out': (0.0, 0.613)}
    factors = {'L0_attn_b_in': 3.032,
     'L0_attn_A_log': 64.0,
     'L0_attn_dt_bias': 8.0,
     'L0_attn_norm_w': 46.453,
     'L0_ffn_Wscale_dp': 13.504,
     'L0_ffn_Wscale_ug': 3.309}
    for name, (base, spread) in spreads.items():
        noise = np.random.default_rng([zlib.crc32(name.encode()), seed]).standard_normal(out[name].shape)
        drawn = base * np.exp(spread * noise) if base else spread * noise
        out[name] = jnp.asarray(drawn.astype(out[name].dtype))
    for name, factor in factors.items():
        out[name] = (out[name] * factor).astype(out[name].dtype)
    return out
```

```python
from contextlib import ExitStack

import numpy as np

import concourse.bass as bass
from concourse import mybir

F32 = mybir.dt.float32
F16 = mybir.dt.float16
ALU = mybir.AluOpType
ACT = mybir.ActivationFunctionType

P = 128
NB = 16
NH = 256
NS = 64
D = 512
L = NH + 1
KT = D // P
HEADS = 32
HD = 64
GROUPS = 8
GH = HEADS // GROUPS
SD = 32
DS = HEADS * HD
ZT = DS // P
CT = (DS + 2 * GROUPS * SD) // P
PT = ZT + CT
PROJ = 2 * DS + 2 * GROUPS * SD + HEADS
INTER = 2048
IT = INTER // P
EPS = 1e-5
UNITS = NB * GROUPS

X_SCALE = 16.0
W_SCALE = 256.0
O_SCALE = 16.0

HC = 8
CHUNKS = NH // HC


class Link:

    def __init__(self, eng, sem):
        self.eng, self.sem, self.n = eng, sem, 0

    def __call__(self, ins):
        ins.then_inc(self.sem, 1)
        self.n += 1
        self.eng.wait_ge(self.sem, self.n)


def bcast(ap, axis, n):
    u = ap.unsqueeze(axis)
    shape = list(u.shape)
    shape[axis] = n
    return u.broadcast_to(shape)


def static(v):
    return isinstance(v, int)


def peeled(eng, first, stop, body):
    body(first)
    with eng.Fori(first + 1, stop) as i:
        body(i)


def s4_phase(nc, t, scratch):
    with ExitStack() as ctx:
        def sb(name, shape, dt=F32):
            return ctx.enter_context(nc.sbuf_tensor(name, shape, dt))

        def sem(name):
            return ctx.enter_context(nc.semaphore(name))

        inv, aim, bre, bim, ldt = (sb(n, [P, NH]) for n in ("s4_inv", "s4_aim", "s4_bre", "s4_bim", "s4_ldt"))
        cp = sb("s4_cp", [P, NH, NB])
        cq = sb("s4_cq", [P, NH, NB])
        tmp = [sb(f"s4_tmp{i}", [P, NH]) for i in range(6)]
        er, ei = sb("s4_er", [P, 9, NH]), sb("s4_ei", [P, 9, NH])
        xj, yj = sb("s4_xj", [P, 16, NH]), sb("s4_yj", [P, 16, NH])
        cr, ci = sb("s4_cr", [P, 8, NH]), sb("s4_ci", [P, 8, NH])
        gr, gi = sb("s4_gr", [P, 4, NH]), sb("s4_gi", [P, 4, NH])
        sgn = sb("s4_sgn", [P, 3])
        v = sb("s4_v", [P, 2, HC, P])
        big = v[:, :, :, :].rearrange("p s h l -> p (s h l)")
        vt = sb("s4_vt", [P, 2, HC, P])
        uu = sb("s4_u", [P, 2, HC, 64])
        ut = sb("s4_ut", [P, 2, HC, 64])
        cls = sb("s4_cls", [P, KT])
        ht = sb("s4_ht", [P, KT, NB, L])
        ps = [ctx.enter_context(nc.psum_tensor(f"s4_ps{i}", [P, 8, 4, NB], F32)) for i in range(2)]

        loaded, cls_in, stored = sem("s4_loaded"), sem("s4_cls_in"), sem("s4_stored")
        exps, chain, params = sem("s4_exps"), sem("s4_chain"), sem("s4_params")
        pool_part, v_step, uv_ready = sem("s4_pool_part"), sem("s4_v_step"), sem("s4_uv_ready")
        mm_done, evac, cls_done = sem("s4_mm_done"), sem("s4_evac"), sem("s4_cls_done")

        block = ctx.enter_context(nc.Block())

        @block.sync
        def _(sp):
            for dst, src in ((inv, t["inv_A_real"]), (aim, t["A_imag"]), (bre, t["B_re"]), (bim, t["B_im"])):
                for h in range(2):
                    sp.dma_start(dst[NS * h:NS * h + NS, :], src).then_inc(loaded, 16)
            sp.dma_start(ldt[:, :], t["log_dt"].partition_broadcast(P)).then_inc(loaded, 16)
            sp.dma_start(cp[:, :, :], t["C"]).then_inc(loaded, 16)
            for h in range(2):
                sp.dma_start(cq[NS * h:NS * h + NS, :, :],
                             t["C"][NS * (1 - h):NS * (1 - h) + NS]).then_inc(loaded, 16)
            sp.dma_start(cls[:, :], t["cls"]).then_inc(cls_in, 16)
            sp.wait_ge(evac, CHUNKS)
            sp.wait_ge(cls_done, 1)
            for b in range(NB):
                sp.dma_start(scratch["h"][b], ht[:, :, b, :]).then_inc(stored, 16)
            sp.wait_ge(stored, 16 * NB)

        @block.scalar
        def _(act):
            act.wait_ge(cls_in, 16)
            act.activation(ht[:, :, :, 0], bcast(cls[:, :], 2, NB), ACT.Identity).then_inc(cls_done, 1)
            act.wait_ge(loaded, 16 * 12)
            act.activation(inv[:, :], inv[:, :], ACT.Exp).then_inc(exps, 1)
            act.activation(ldt[:, :], ldt[:, :], ACT.Exp).then_inc(exps, 1)

            def evacuate(i):
                for s in range(2):
                    act.wait_ge(mm_done, 2 * i + s + 1)
                    act.activation(ht[:, :, :, bass.ds(2 * HC * i + (1 + HC * s), HC)],
                                   ps[s][:, :, :, :].rearrange("p h a c -> p a c h"),
                                   ACT.Identity).then_inc(evac, 1)

            peeled(act, 0, CHUNKS // 2, evacuate)

        @block.vector
        def _(dve):
            link = Link(dve, chain)
            TT, TS, STT = nc.vector.tensor_tensor, nc.vector.tensor_scalar, nc.vector.scalar_tensor_tensor
            link(nc.vector.memset(sgn[:, :], 0.0))
            for half, vals in ((0, (1.0, 0.0, 2.0)), (1, (0.0, 1.0, -2.0))):
                for c, val in enumerate(vals):
                    link(nc.vector.memset(sgn[NS * half:NS * half + NS, c:c + 1], val))
            dve.wait_ge(exps, 2)
            t0, t1, t2, t3, t4, t5 = (x[:, :] for x in tmp)
            dt, a = ldt[:, :], inv[:, :]
            link(TS(t5, dt, 0.5, None, ALU.mult))
            link(STT(out=t0, in0=a, scalar=-1.0, in1=t5, op0=ALU.mult, op1=ALU.mult))
            link(TT(t1, aim[:, :], t5, ALU.mult))
            link(TS(t2, t0, -1.0, 1.0, ALU.mult, ALU.add))
            link(TT(t3, t2, t2, ALU.mult))
            link(TT(t4, t1, t1, ALU.mult))
            link(TT(t3, t3, t4, ALU.add))
            link(nc.vector.reciprocal(t3, t3))
            link(TT(t5, t0, t0, ALU.mult))
            link(TT(t5, t5, t4, ALU.add))
            link(TS(t5, t5, -1.0, 1.0, ALU.mult, ALU.add))
            link(TT(er[:, 0, :], t5, t3, ALU.mult))
            link(STT(out=ei[:, 0, :], in0=t1, scalar=2.0, in1=t3, op0=ALU.mult, op1=ALU.mult))
            link(TT(t3, t3, dt, ALU.mult))
            link(TT(t2, t2, t3, ALU.mult))
            link(TT(t1, t1, t3, ALU.mult))
            link(TT(gr[:, 0, :], bre[:, :], t2, ALU.mult))
            link(TT(t0, bim[:, :], t1, ALU.mult))
            link(TT(gr[:, 0, :], gr[:, 0, :], t0, ALU.subtract))
            link(TT(gi[:, 0, :], bre[:, :], t1, ALU.mult))
            link(TT(t0, bim[:, :], t2, ALU.mult))
            link(TT(gi[:, 0, :], gi[:, 0, :], t0, ALU.add))
            for k in range(8):
                r, i = er[:, k, :], ei[:, k, :]
                link(TT(t0, i, i, ALU.mult))
                link(TT(t1, r, r, ALU.mult))
                link(TT(er[:, k + 1, :], t1, t0, ALU.subtract))
                link(STT(out=ei[:, k + 1, :], in0=r, scalar=2.0, in1=i, op0=ALU.mult, op1=ALU.mult))

            def double(re, im, k, e, conj):
                tb = big[:, 0:k * NH].rearrange("p (k h) -> p k h", k=k)
                c, s = bcast(er[:, e, :], 1, k), bcast(ei[:, e, :], 1, k)
                r0, i0, r1, i1 = re[:, 0:k, :], im[:, 0:k, :], re[:, k:2 * k, :], im[:, k:2 * k, :]
                link(TT(tb, i0, s, ALU.mult))
                link(TT(r1, r0, c, ALU.mult))
                link(TT(r1, r1, tb, ALU.add if conj else ALU.subtract))
                link(TT(tb, r0, s, ALU.mult))
                link(TT(i1, i0, c, ALU.mult))
                link(TT(i1, i1, tb, ALU.subtract if conj else ALU.add))

            link(nc.vector.memset(xj[:, 0, :], 0.0))
            link(nc.vector.memset(yj[:, 0, :], 0.0))
            link(TS(xj[:, 0, :], xj[:, 0, :], sgn[:, 0:1], None, ALU.add))
            link(TS(yj[:, 0, :], yj[:, 0, :], sgn[:, 1:2], None, ALU.add))
            for e in range(4):
                double(xj, yj, 1 << e, e, True)
            link(nc.vector.memset(cr[:, 0, :], 1.0))
            link(nc.vector.memset(ci[:, 0, :], 0.0))
            for e in range(3):
                double(cr, ci, 1 << e, 4 + e, False)
            for e in range(2):
                double(gr, gi, 1 << e, 7 + e, False)
            link(TS(gr[:, :, :], gr[:, :, :], sgn[:, 2:3], None, ALU.mult))
            link(TS(gi[:, :, :], gi[:, :, :], -2.0, None, ALU.mult))
            nc.vector.memset(sgn[:, 0:1], 1.0).then_inc(params, 1)

            def form(i):
                for s in range(2):
                    hs = bass.ds(2 * HC * i + HC * s, HC)
                    n = 2 * i + s
                    c3 = bcast(cr[:, :, hs].rearrange("p i h -> p h i"), 3, 16)
                    x3 = bcast(xj[:, :, hs].rearrange("p j h -> p h j"), 2, 8)
                    if not static(i):
                        dve.wait_ge(mm_done, n - 1)
                    TT(v[:, s, :, :].rearrange("p h (i j) -> p h i j", i=8), c3, x3, ALU.mult).then_inc(v_step, 1)
                    g3 = bcast(gr[:, :, hs].rearrange("p a h -> p h a"), 3, NB)
                    p3 = bcast(cp[:, hs, :], 2, 4)
                    TT(uu[:, s, :, :].rearrange("p h (a c) -> p h a c", a=4), g3, p3, ALU.mult).then_inc(v_step, 1)
                    dve.wait_ge(v_step, 2 * n + 2)
                    dve.wait_ge(pool_part, 2 * n + 2)
                    TT(v[:, s, :, :], v[:, s, :, :], vt[:, s, :, :], ALU.add).then_inc(uv_ready, 1)
                    TT(uu[:, s, :, :], uu[:, s, :, :], ut[:, s, :, :], ALU.add).then_inc(uv_ready, 1)

            peeled(dve, 0, CHUNKS // 2, form)

        @block.gpsimd
        def _(pool):
            pool.wait_ge(params, 1)

            def partners(i):
                for s in range(2):
                    hs = bass.ds(2 * HC * i + HC * s, HC)
                    n = 2 * i + s
                    s3 = bcast(ci[:, :, hs].rearrange("p i h -> p h i"), 3, 16)
                    y3 = bcast(yj[:, :, hs].rearrange("p j h -> p h j"), 2, 8)
                    if not static(i):
                        pool.wait_ge(uv_ready, 2 * n - 2)
                    nc.gpsimd.tensor_tensor(vt[:, s, :, :].rearrange("p h (i j) -> p h i j", i=8), s3, y3,
                                            ALU.mult).then_inc(pool_part, 1)
                    g3 = bcast(gi[:, :, hs].rearrange("p a h -> p h a"), 3, NB)
                    q3 = bcast(cq[:, hs, :], 2, 4)
                    nc.gpsimd.tensor_tensor(ut[:, s, :, :].rearrange("p h (a c) -> p h a c", a=4), g3, q3,
                                            ALU.mult).then_inc(pool_part, 1)

            peeled(pool, 0, CHUNKS // 2, partners)

        @block.tensor
        def _(pe):
            def multiply(i):
                for s in range(2):
                    n = 2 * i + s
                    pe.wait_ge(uv_ready, 2 * n + 2)
                    if not static(i):
                        pe.wait_ge(evac, n - 1)
                    for h in range(HC):
                        last = nc.tensor.matmul(ps[s][:, h, :, :], v[:, s, h, :], uu[:, s, h, :],
                                                start=True, stop=True)
                    last.then_inc(mm_done, 1)

            peeled(pe, 0, CHUNKS // 2, multiply)


def prep_phase(nc, t, scratch, keep):
    with ExitStack() as ctx:
        def sb(name, shape, dt=F32):
            return ctx.enter_context(nc.sbuf_tensor(name, shape, dt))

        def sem(name):
            return ctx.enter_context(nc.semaphore(name))

        WC = P * PT // 4
        hb, xc, sq = sb("p_hb", [P, 2, KT, L]), sb("p_xc", [P, 2, KT, L]), sb("p_sq", [P, 2, KT, L])
        sd, rs = sb("p_sd", [P, 2, L]), sb("p_rs", [P, 2, L])
        xsp = sb("p_xsp", [P, 2, 2, KT, L], F16)
        wst = sb("p_wst", [P, 2, WC])
        ost = sb("p_ost", [P, 2, D])
        wdt = sb("p_wdt", [P, KT, HEADS])
        wdt_hi, wdt_lo = sb("p_wdt_hi", [P, KT, HEADS], F16), sb("p_wdt_lo", [P, KT, HEADS], F16)
        dtv = sb("p_dtv", [P, 4])
        nw = sb("p_nw", [P, ZT])
        eps = sb("p_eps", [P, 1])
        vec = sb("p_vec", [P, 3])
        dtr = sb("p_dtr", [P, 4, L])
        mean_ps = [ctx.enter_context(nc.psum_tensor(f"p_mean{i}", [P, 512], F32)) for i in range(2)]
        var_ps = [ctx.enter_context(nc.psum_tensor(f"p_var{i}", [P, 512], F32)) for i in range(2)]
        dt_ps = [ctx.enter_context(nc.psum_tensor(f"p_dt{i}", [P, 512], F32)) for i in range(2)]
        tr_ps = [ctx.enter_context(nc.psum_tensor(f"p_tr{i}", [P, P], F32)) for i in range(2)]

        small_in = sem("p_small_in")
        h_in = [sem(f"p_h_in{i}") for i in range(2)]
        w_in = [sem(f"p_w_in{i}") for i in range(2)]
        o_in = [sem(f"p_o_in{i}") for i in range(2)]
        setup, setup_act, consts = sem("p_setup"), sem("p_setup_act"), sem("p_consts")
        mean_done, centered, squared, var_done = sem("p_mean_done"), sem("p_centered"), sem("p_squared"), sem("p_var_done")
        sd_done, rs_done, normed, hi_done, lo_done = sem("p_sd_done"), sem("p_rs_done"), sem("p_normed"), sem("p_hi_done"), sem("p_lo_done")
        w_hi_done, w_lo_done, o_hi_done, o_lo_done = sem("p_w_hi_done"), sem("p_w_lo_done"), sem("p_o_hi_done"), sem("p_o_lo_done")
        dt_mm, dt_out = sem("p_dt_mm"), sem("p_dt_out")
        x_out = [sem(f"p_x_out{i}") for i in range(2)]
        chain, soft_act, dt_ready, tr_done, a_ready = sem("p_chain"), sem("p_soft_act"), sem("p_dt_ready"), sem("p_tr_done"), sem("p_a_ready")
        tr_out, stored, tail_in = sem("p_tr_out"), sem("p_stored"), sem("p_tail_in")

        block = ctx.enter_context(nc.Block())

        @block.sync
        def _(sp):
            sp.dma_start(wdt[:, :, :], t["W_in"][:, P * PT:].rearrange("(k p) n -> p k n", p=P)).then_inc(small_in, 16)
            sp.dma_start(dtv[:, :], t["dt_vec"]).then_inc(small_in, 16)
            sp.dma_start(nw[:, :], t["norm_w"]).then_inc(small_in, 16)
            sp.dma_start(keep["ident"][:, :], t["ident"]).then_inc(small_in, 16)

            def four(i):
                first = isinstance(i, int)
                for g in range(4):
                    n, s = 4 * i + g, g % 2
                    if not (first and g < 2):
                        sp.wait_ge(centered, n - 1)
                        sp.wait_ge(w_lo_done, n - 1)
                        sp.wait_ge(o_lo_done, n - 1)
                    sp.dma_start(hb[:, s, :, :], scratch["h"][n]).then_inc(h_in[s], 16)
                    sp.dma_start(wst[:, s, :], t["W_in"][bass.ds(i * P, P), g * WC:g * WC + WC]).then_inc(w_in[s], 16)
                    sp.dma_start(ost[:, s, :], t["W_out"][bass.ds(n * P, P), :]).then_inc(o_in[s], 16)
                    if not (first and g == 0):
                        sp.wait_ge(hi_done, n)
                        sp.wait_ge(lo_done, n)
                        q = (g - 1) % 2
                        sp.dma_start(scratch["xn"][n - 1], xsp[:, q, :, :, :]).then_inc(x_out[q], 16)

            peeled(sp, 0, 4, four)
            sp.wait_ge(hi_done, NB)
            sp.wait_ge(lo_done, NB)
            sp.dma_start(scratch["xn"][NB - 1], xsp[:, 1, :, :, :]).then_inc(x_out[1], 16)
            sp.wait_ge(a_ready, 1)
            for g in range(4):
                rows = slice(HEADS * g, HEADS * g + HEADS)
                sp.dma_start(scratch["a"].rearrange("(i g) h l -> g h i l", g=4)[g], keep["a"][rows, :, :]).then_inc(stored, 16)
                sp.dma_start(scratch["dt_tail"].rearrange("(i g) h o -> g h i o", g=4)[g],
                             dtr[rows, :, L - 1:L], allow_slow_non_contiguous=True).then_inc(stored, 16)
            sp.wait_ge(stored, 16 * 8)
            sp.dma_start(keep["dt_tail"][:, :, :], scratch["dt_tail"].rearrange("b h o -> (b h o)").partition_broadcast(P)
                         .rearrange("p (b h) -> p b h", b=NB)).then_inc(tail_in, 16)
            sp.wait_ge(tail_in, 16)
            for q in range(2):
                sp.wait_ge(x_out[q], 16 * 8)

        @block.tensor
        def _(pe):
            ones = keep["ones_d"]

            def mean(n, s):
                pe.wait_ge(h_in[s], n * 8 + 8 * (2 - s))
                if s is not None and not (isinstance(n, int) and n < 2):
                    pe.wait_ge(centered, n - 1)
                for k in range(KT):
                    last = nc.tensor.matmul(mean_ps[s][:, 0:L], ones[:, :], hb[:, s, k, :], start=k == 0, stop=k == KT - 1)
                last.then_inc(mean_done, 1)

            def var(n, s):
                pe.wait_ge(squared, n + 1)
                if not (isinstance(n, int) and n < 2):
                    pe.wait_ge(sd_done, n - 1)
                for k in range(KT):
                    last = nc.tensor.matmul(var_ps[s][:, 0:L], ones[:, :], sq[:, s, k, :], start=k == 0, stop=k == KT - 1)
                last.then_inc(var_done, 1)

            def dts(n, s, g):
                pe.wait_ge(lo_done, n + 1)
                pe.wait_ge(hi_done, n + 1)
                if not (isinstance(n, int) and n < 2):
                    pe.wait_ge(dt_out, n - 1)
                rows = slice(HEADS * g, HEADS * g + HEADS)
                for k in range(KT):
                    for m, (w, x) in enumerate(((wdt_hi, 0), (wdt_hi, 1), (wdt_lo, 0))):
                        last = nc.tensor.matmul(dt_ps[s][rows, 0:L], w[:, k, :], xsp[:, s, x, k, :],
                                                start=k == 0 and m == 0, stop=k == KT - 1 and m == 2)
                last.then_inc(dt_mm, 1)

            pe.wait_ge(consts, 2)
            pe.wait_ge(setup, 5)
            mean(0, 0)

            def four(i):
                for g in range(4):
                    n = 4 * i + g
                    if not (g == 3 and isinstance(i, int) and i == 3):
                        mean(n + 1, (g + 1) % 2)
                    var(n, g % 2)
                    if not (g == 0 and isinstance(i, int) and i == 0):
                        dts(n - 1, (g - 1) % 2, (g - 1) % 4)

            four(0)
            with pe.Fori(1, 3) as i:
                four(i)
            four(3)
            dts(NB - 1, 1, 3)
            pe.wait_ge(dt_ready, 1)
            for m in range(2):
                for i in range(4):
                    n = 4 * m + i
                    if n >= 2:
                        pe.wait_ge(tr_out, n - 1)
                    nc.tensor.transpose(tr_ps[n % 2][:, :], dtr[:, i, P * m:P * m + P], keep["ident"][:, 0:P]).then_inc(tr_done, 1)

        @block.scalar
        def _(act):
            A = act.activation
            act.wait_ge(consts, 2)
            act.wait_ge(small_in, 64)
            A(wdt_hi[:, :, :], wdt[:, :, :], ACT.Identity, scale=W_SCALE).then_inc(setup_act, 1)
            act.wait_ge(setup, 1)
            A(vec[:, 2:3], vec[:, 2:3], ACT.Exp).then_inc(setup_act, 1)
            act.wait_ge(setup, 5)

            def square(n, s):
                act.wait_ge(centered, n + 1)
                if not (isinstance(n, int) and n < 2):
                    act.wait_ge(var_done, n - 1)
                A(sq[:, s, :, :], xc[:, s, :, :], ACT.Square).then_inc(squared, 1)

            square(0, 0)

            def four(i):
                for g in range(4):
                    n, s = 4 * i + g, g % 2
                    if not (g == 3 and isinstance(i, int) and i == 3):
                        square(n + 1, (g + 1) % 2)
                    act.wait_ge(w_in[s], 16 * (2 * i + g // 2 + 1))
                    A(keep["w_hi"][:, i, g * WC:g * WC + WC], wst[:, s, :], ACT.Identity, scale=W_SCALE).then_inc(w_hi_done, 1)
                    act.wait_ge(o_in[s], 16 * (2 * i + g // 2 + 1))
                    A(keep["o_hi"][:, n, :], ost[:, s, :], ACT.Identity, scale=nw[:, n:n + 1] if isinstance(n, int) else nw[:, bass.ds(n, 1)]).then_inc(o_hi_done, 1)
                    act.wait_ge(var_done, n + 1)
                    if not (isinstance(n, int) and n < 2):
                        act.wait_ge(rs_done, n - 1)
                    A(sd[:, s, :], var_ps[s][:, 0:L], ACT.Sqrt, bias=eps[:, 0:1]).then_inc(sd_done, 1)
                    if not (g == 0 and isinstance(i, int) and i == 0):
                        dt_evac(n - 1, (g - 1) % 2, (g - 1) % 4, i if g else i - 1)
                    act.wait_ge(normed, n + 1)
                    if not (isinstance(n, int) and n < 2):
                        act.wait_ge(x_out[s], 16 * (2 * i + g // 2))
                    A(xsp[:, s, 0, :, :], xc[:, s, :, :], ACT.Identity).then_inc(hi_done, 1)

            def dt_evac(n, s, g, i):
                act.wait_ge(dt_mm, n + 1)
                rows = slice(HEADS * g, HEADS * g + HEADS)
                A(dtr[rows, i, :], dt_ps[s][rows, 0:L], ACT.Identity, scale=vec[rows, 0:1],
                  bias=vec[rows, 1:2]).then_inc(dt_out, 1)

            four(0)
            with act.Fori(1, 3) as i:
                four(i)
            four(3)
            dt_evac(NB - 1, 1, 3, 3)
            act.wait_ge(dt_out, NB)
            A(sq[:, 0, :, :], dtr[:, :, :], ACT.Abs).then_inc(soft_act, 1)
            act.wait_ge(soft_act, 1)
            A(sq[:, 1, :, :], sq[:, 0, :, :], ACT.Exp, scale=-1.0).then_inc(soft_act, 1)
            act.wait_ge(dt_ready, 2)
            A(keep["a"][:, :, :], sq[:, 0, :, :], ACT.Exp).then_inc(soft_act, 1)

        @block.vector
        def _(dve):
            TT, TS, STT = nc.vector.tensor_tensor, nc.vector.tensor_scalar, nc.vector.scalar_tensor_tensor
            dve.wait_ge(small_in, 64)
            TS(vec[:, 2:3], dtv[:, 3:4], 88.0, None, ALU.min).then_inc(setup, 1)
            TS(vec[:, 0:1], dtv[:, 1:2], 1.0 / (X_SCALE * W_SCALE), None, ALU.mult).then_inc(setup, 1)
            STT(out=vec[:, 1:2], in0=dtv[:, 0:1], scalar=dtv[:, 1:2], in1=dtv[:, 2:3], op0=ALU.mult, op1=ALU.add).then_inc(setup, 1)
            TS(nw[:, :], nw[:, :], O_SCALE, None, ALU.mult).then_inc(setup, 1)
            dve.wait_ge(setup_act, 1)
            STT(out=wdt_lo[:, :, :], in0=wdt[:, :, :], scalar=W_SCALE, in1=wdt_hi[:, :, :],
                op0=ALU.mult, op1=ALU.subtract).then_inc(setup, 1)
            dve.wait_ge(setup_act, 2)
            dve.wait_ge(setup, 5)
            TS(vec[:, 2:3], vec[:, 2:3], -1.0, None, ALU.mult).then_inc(setup, 1)

            def center(n, s):
                dve.wait_ge(mean_done, n + 1)
                if not (isinstance(n, int) and n < 2):
                    dve.wait_ge(hi_done, n - 1)
                    dve.wait_ge(lo_done, n - 1)
                TT(xc[:, s, :, :], hb[:, s, :, :], bcast(mean_ps[s][:, 0:L], 1, KT), ALU.subtract).then_inc(centered, 1)

            center(0, 0)

            def four(i):
                for g in range(4):
                    n, s = 4 * i + g, g % 2
                    if not (g == 3 and isinstance(i, int) and i == 3):
                        center(n + 1, (g + 1) % 2)
                    dve.wait_ge(w_hi_done, n + 1)
                    cols = slice(g * WC, g * WC + WC)
                    STT(out=keep["w_lo"][:, i, cols], in0=wst[:, s, :], scalar=W_SCALE, in1=keep["w_hi"][:, i, cols],
                        op0=ALU.mult, op1=ALU.subtract).then_inc(w_lo_done, 1)
                    dve.wait_ge(o_hi_done, n + 1)
                    STT(out=keep["o_lo"][:, n, :], in0=ost[:, s, :], scalar=nw[:, n:n + 1] if isinstance(n, int) else nw[:, bass.ds(n, 1)],
                        in1=keep["o_hi"][:, n, :], op0=ALU.mult, op1=ALU.subtract).then_inc(o_lo_done, 1)
                    dve.wait_ge(sd_done, n + 1)
                    if not (isinstance(n, int) and n < 2):
                        dve.wait_ge(normed, n - 1)
                    nc.vector.reciprocal(rs[:, s, :], sd[:, s, :]).then_inc(rs_done, 1)
                    dve.wait_ge(rs_done, n + 1)
                    STT(out=xc[:, s, :, :], in0=xc[:, s, :, :], scalar=X_SCALE, in1=bcast(rs[:, s, :], 1, KT),
                        op0=ALU.mult, op1=ALU.mult).then_inc(normed, 1)

            four(0)
            with dve.Fori(1, 3) as i:
                four(i)
            four(3)
            link = Link(dve, chain)
            dve.wait_ge(soft_act, 2)
            u, q, q2, w = sq[:, 1, :, :], sq[:, 0, :, :], xc[:, 0, :, :], xc[:, 1, :, :]
            link(TS(q, u, 2.0, None, ALU.add))
            link(nc.vector.reciprocal(q, q))
            link(TT(q, q, u, ALU.mult))
            link(TT(q2, q, q, ALU.mult))
            link(TS(w, q2, 1.0 / 17, None, ALU.mult))
            for k in range(7, 0, -1):
                link(STT(out=w, in0=w, scalar=1.0 / (2 * k + 1), in1=q2, op0=ALU.add, op1=ALU.mult))
            link(STT(out=w, in0=w, scalar=1.0, in1=q, op0=ALU.add, op1=ALU.mult))
            link(TS(w, w, 2.0, None, ALU.mult))
            STT(out=dtr[:, :, :], in0=dtr[:, :, :], scalar=0.0, in1=w, op0=ALU.max, op1=ALU.add).then_inc(dt_ready, 1)
            dve.wait_ge(dt_ready, 1)
            TS(sq[:, 0, :, :], dtr[:, :, :], vec[:, 2:3], -200.0, ALU.mult, ALU.max).then_inc(dt_ready, 1)
            dve.wait_ge(soft_act, 3)
            nc.vector.memset(keep["a"][:, :, 0:1], 0.0).then_inc(a_ready, 1)
            for m in range(2):
                for i in range(4):
                    n = 4 * m + i
                    dve.wait_ge(tr_done, n + 1)
                    nc.vector.tensor_copy(keep["dt_tok"][:, m, 4 * i:4 * i + 4, :].rearrange("p b h -> p (b h)"),
                                          tr_ps[n % 2][:, :]).then_inc(tr_out, 1)

        @block.gpsimd
        def _(pool):
            nc.gpsimd.memset(keep["ones_d"][:, :], 1.0 / D).then_inc(consts, 1)
            nc.gpsimd.memset(eps[:, :], EPS).then_inc(consts, 1)

            def four(i):
                for g in range(4):
                    n, s = 4 * i + g, g % 2
                    pool.wait_ge(hi_done, n + 1)
                    if not (isinstance(n, int) and n < 2):
                        pool.wait_ge(x_out[s], 16 * (2 * i + g // 2))
                    nc.gpsimd.tensor_tensor(xsp[:, s, 1, :, :], xc[:, s, :, :], xsp[:, s, 0, :, :], ALU.subtract).then_inc(lo_done, 1)

            peeled(pool, 0, 4, four)


class Mamba:

    STEP = 5 * GROUPS + 8

    @staticmethod
    def base(b, g):
        if isinstance(b, int) and b == 0 and g < 3:
            return 8 + 4 * g
        return 2 + Mamba.STEP * b + 5 * g + (4 if g > 2 else 0)

    @staticmethod
    def project(b, g):
        return Mamba.base(b, g) + (5 if g == GROUPS - 1 else 0)

    @staticmethod
    def norm(b, g):
        if g == GROUPS - 1:
            return Mamba.base(b, g)
        return Mamba.base(b, g) + (4 if g != 2 or (isinstance(b, int) and b == 0) else 8)

    @staticmethod
    def pair(b, g):
        return 2 + 10 * b + g


def mamba_phase(nc, t, scratch, keep):
    with ExitStack() as ctx:
        def sb(name, shape, dt=F32):
            return ctx.enter_context(nc.sbuf_tensor(name, shape, dt))

        def sem(name):
            return ctx.enter_context(nc.semaphore("m_" + name))

        L1 = L - P
        xn = sb("m_xn", [P, 2, KT, L], F16)
        hb, h1 = sb("m_hb", [P, KT, L]), sb("m_h1", [P, KT, L])
        vb, vm = sb("m_vb", [P, PT]), sb("m_vm", [P, PT])
        cw, cb = sb("m_cw", [P, CT, 4]), sb("m_cb", [P, CT])
        sc3, bi3 = sb("m_sc3", [P, CT]), sb("m_bi3", [P, CT])
        dp, bo = sb("m_dp", [P, ZT]), sb("m_bo", [P, KT])
        xb, acc = sb("m_xb", [P, 2, 2, L + 3]), sb("m_acc", [P, 2, 2, L])
        xs, zs = sb("m_xs", [P, 4, 2, L]), sb("m_zs", [P, 4, 2, L])
        bz = sb("m_bz", [P, 2, 4, L])
        cs = sb("m_cs", [P, 2, L])
        xt = sb("m_xt", [P, 2, 2, 2 * P])
        dec = sb("m_dec", [P, 2, GH, L])
        dec1 = sb("m_dec1", [P, 2, GH, L1])
        yg = sb("m_yg", [P, 2, 2, L])
        sq = sb("m_sq", [P, 2, L])
        sd, rs = sb("m_sd", [P, L]), sb("m_rs", [P, L])
        yn_hi, yn_lo = sb("m_yn_hi", [P, ZT, L], F16), sb("m_yn_lo", [P, ZT, L], F16)
        tailp, tailw = sb("m_tailp", [P, 2, 4]), sb("m_tailw", [P, GROUPS, 2])
        ones_g, ones = sb("m_ones_g", [P, P]), sb("m_ones", [P, P])
        eps = sb("m_eps", [P, 1])
        ident = keep["ident"]
        pi = [ctx.enter_context(nc.psum_tensor(f"m_pi{i}", [P, 512], F32)) for i in range(4)]
        pt = ctx.enter_context(nc.psum_tensor("m_pt", [P, 2, 2 * P], F32))
        pg = ctx.enter_context(nc.psum_tensor("m_pg", [P, 512], F32))
        py = [ctx.enter_context(nc.psum_tensor(f"m_py{i}", [P, 512], F32)) for i in range(2)]

        small_in, consts, setup = sem("small_in"), sem("consts"), sem("setup")
        xn_in, h_in, h1_out = sem("xn_in"), sem("h_in"), sem("h1_out")
        dec_in = [sem(f"dec_in{i}") for i in range(2)]
        tile_full, tile_free = sem("tile_full"), sem("tile_free")
        transposed, cb_done, heads_done = sem("transposed"), sem("cb_done"), sem("heads_done")
        convolved, activated = sem("convolved"), sem("activated")
        squared, hi_done, lo_done, h1_done = sem("squared"), sem("hi_done"), sem("lo_done"), sem("h1_done")
        xt_done, scanned, weighted = sem("xt_done"), sem("scanned"), sem("weighted")
        tailp_done, tailw_done = sem("tailp_done"), sem("tailw_done")
        y_step, gated, rs_done, normed = sem("y_step"), sem("gated"), sem("rs_done"), sem("normed")

        block = ctx.enter_context(nc.Block())

        def batches(eng, body):
            body(0)
            with eng.Fori(1, NB - 1) as b:
                body(b)
            body(NB - 1)

        def last(b):
            return static(b) and b == NB - 1

        @block.sync
        def _(sp):
            for dst, src in ((vb, "b_in"), (vm, "mup"), (cb, "conv_b"), (dp, "D"), (bo, "b_out")):
                sp.dma_start(dst[:, :], t[src]).then_inc(small_in, 16)
            sp.dma_start(cw[:, :, :], t["conv_w"]).then_inc(small_in, 16)

            def decays(n, b, g, s):
                sp.dma_start(dec[:, s, :, :].rearrange("p h l -> p (h l)"),
                             scratch["a"].rearrange("b (g h) l -> b g (h l)", h=GH)[b, g].partition_broadcast(P)
                             ).then_inc(dec_in[s], 16)

            sp.dma_start(xn[:, :, :, :], scratch["xn"][0]).then_inc(xn_in, 16)
            decays(0, 0, 0, 0)

            def batch(b):
                for g in range(GROUPS):
                    u = 8 * b + g
                    if g == 0:
                        if not (static(b) and b == 0):
                            sp.wait_ge(h1_done, b - 1) if static(b) and b > 1 else None
                            if not static(b):
                                sp.wait_ge(h1_done, b - 1)
                            sp.dma_start(hb[:, :, :], scratch["h"][b - 1]).then_inc(h_in, 16)
                    if g == 3 and not (static(b) and b == 0):
                        sp.wait_ge(h1_done, b)
                        sp.dma_start(scratch["h1"][b - 1], h1[:, :, :]).then_inc(h1_out, 16)
                    if g == GROUPS - 1 and not last(b):
                        sp.wait_ge(tile_full, Mamba.project(b, GROUPS - 2) + 4)
                        sp.dma_start(xn[:, :, :, :], scratch["xn"][b + 1]).then_inc(xn_in, 16)
                    if not (last(b) and g == GROUPS - 1):
                        if not (static(b) and b == 0 and g == 0):
                            sp.wait_ge(heads_done, u)
                        if g < GROUPS - 1:
                            decays(u + 1, b, g + 1, (g + 1) % 2)
                        else:
                            decays(u + 1, b + 1, 0, 0)

            batches(sp, batch)
            sp.wait_ge(h1_done, NB - 1)
            sp.dma_start(hb[:, :, :], scratch["h"][NB - 1]).then_inc(h_in, 16)
            sp.wait_ge(h1_done, NB)
            sp.dma_start(scratch["h1"][NB - 1], h1[:, :, :]).then_inc(h1_out, 16)
            sp.wait_ge(h1_out, 16 * NB)

        @block.tensor
        def _(pe):
            def split_mm(dst, k_tiles, w_hi, w_lo, x_hi, x_lo):
                for k in range(k_tiles):
                    for m, (w, x) in enumerate(((w_hi, x_hi), (w_hi, x_lo), (w_lo, x_hi))):
                        ins = nc.tensor.matmul(dst, w(k), x(k), start=k == 0 and m == 0,
                                               stop=k == k_tiles - 1 and m == 2)
                ins.then_inc(tile_full, 1)

            def project(tile, q, cols):
                if not static(tile) or tile >= 4:
                    pe.wait_ge(tile_free, tile - 3)
                cols = slice(cols * P, cols * P + P)
                split_mm(pi[q][:, 0:L], KT, lambda k: keep["w_hi"][:, k, cols], lambda k: keep["w_lo"][:, k, cols],
                         lambda k: xn[:, 0, k, :], lambda k: xn[:, 1, k, :])

            def project_bc(tile, q):
                for j in range(4):
                    project(tile + j, (q + j) % 4, 2 * ZT + j)

            def project_unit(tile, q, g):
                for j in range(2):
                    project(tile + j, (q + j) % 4, ZT + 2 * g + j)
                for j in range(2):
                    project(tile + 2 + j, (q + 2 + j) % 4, 2 * g + j)

            def heads(n, s):
                pe.wait_ge(weighted, 2 * n + 2)
                pe.wait_ge(xt_done, n + 1)
                if not (static(n) and n == 0):
                    pe.wait_ge(y_step, 4 * n)
                for q in range(2):
                    for hh in range(2):
                        h = 2 * q + hh
                        rows, cols = slice(HD * hh, HD * hh + HD), slice(HD * h, HD * h + HD)
                        nc.tensor.matmul(py[q][rows, 0:L], xt[:, s, 0, cols], dec[:, s, h, :], start=True, stop=False)
                        ins = nc.tensor.matmul(py[q][rows, P:L], xt[:, s, 1, cols], dec1[:, s, h, :], start=False, stop=True)
                ins.then_inc(heads_done, 1)

            def norm(tile, q, n):
                pe.wait_ge(squared, n + 1)
                pe.wait_ge(tile_free, tile - 3)
                for j in range(2):
                    ins = nc.tensor.matmul(pi[q][:, 0:L], ones_g[:, :], sq[:, j, :], start=j == 0, stop=j == 1)
                ins.then_inc(tile_full, 1)

            def out_project(tile, q, b):
                pe.wait_ge(lo_done, 8 * b + 8)
                pe.wait_ge(hi_done, 8 * b + 8)
                for j in range(KT):
                    pe.wait_ge(tile_free, tile + j - 3)
                    cols = slice(j * P, j * P + P)
                    split_mm(pi[(q + j) % 4][:, 0:L], ZT, lambda k: keep["o_hi"][:, k, cols],
                             lambda k: keep["o_lo"][:, k, cols], lambda k: yn_hi[:, k, :], lambda k: yn_lo[:, k, :])

            pe.wait_ge(consts, 8)
            pe.wait_ge(xn_in, 16)
            project_bc(0, 0)
            project_unit(4, 0, 0)

            def batch(b):
                for g in range(GROUPS):
                    u = 8 * b + g
                    q = (2 + 5 * g + (4 if g > 2 else 0)) % 4
                    if static(b) and b == 0 and g < 3:
                        q = 0
                    pe.wait_ge(activated, Mamba.pair(b, g) + 1)
                    if not (static(b) and b == 0 and g == 0):
                        pe.wait_ge(xt_done, u)
                    for m in range(2):
                        for j in range(2):
                            ins = nc.tensor.transpose(pt[:, m, j * P:j * P + P], xs[:, g % 4, j, m * P:m * P + P], ident[:, 0:P])
                    ins.then_inc(transposed, 1)
                    if not (static(b) and b == 0 and g == 0):
                        pe.wait_ge(weighted, 2 * u)
                    if g == 0:
                        pe.wait_ge(tailp_done, b + 1)
                        nc.tensor.matmul(pg[:, 400:408], ones[:, :], tailp[:, :, :].rearrange("p t r -> p (t r)"),
                                         start=True, stop=True)
                    if g == 1:
                        pe.wait_ge(tailw_done, 2 * b + 2)
                    nc.tensor.matmul(pg[:, 0:L], bz[:, g // 4, g % 4, 0:P], cs[:, g // 4, :], start=True, stop=True)
                    nc.tensor.matmul(pg[:, L:L + L1], bz[:, g // 4, g % 4, P:2 * P], cs[:, g // 4, P:L],
                                     start=True, stop=True).then_inc(cb_done, 1)

                    def previous():
                        if not (static(b) and b == 0 and g == 0):
                            heads(u - 1, (g - 1) % 2)
                        if not (static(b) and b == 0 and g < 2):
                            norm(Mamba.norm(b, g), (q + (0 if g == 7 else 8 if g == 2 and not (static(b) and b == 0) else 4)) % 4, u - 2)

                    if g == GROUPS - 1:
                        previous()
                        if not last(b):
                            pe.wait_ge(xn_in, 16 * (b + 2))
                            project_bc(Mamba.base(b, g) + 1, q + 1)
                            project_unit(Mamba.project(b, g), q + 5, 0)
                    else:
                        project_unit(Mamba.base(b, g), q, g + 1)
                        if g == 2 and not (static(b) and b == 0):
                            out_project(Mamba.base(b, g) + 4, q + 4, b - 1)
                        previous()

            batches(pe, batch)
            end = Mamba.base(NB - 1, 7) + 1
            heads(UNITS - 1, 1)
            norm(end, end % 4, UNITS - 2)
            norm(end + 1, (end + 1) % 4, UNITS - 1)
            out_project(end + 2, (end + 2) % 4, NB - 1)

        @block.scalar
        def _(act):
            A = act.activation

            def pair(tile, q, p, c, g_slot):
                s = p
                for j in range(2):
                    act.wait_ge(tile_full, tile + j + 1)
                    ps = pi[(q + j) % 4][:, 0:L]
                    A(xb[:, g_slot, j, 3:L + 3], ps, ACT.Identity, scale=vm[:, ZT + c + j:ZT + c + j + 1],
                      bias=vb[:, ZT + c + j:ZT + c + j + 1])
                    A(acc[:, g_slot, j, :], ps, ACT.Identity, scale=sc3[:, c + j:c + j + 1],
                      bias=bi3[:, c + j:c + j + 1]).then_inc(tile_free, 1)

            def project_pair(tile, q, p, c, slot):
                if not (static(p) and p < 2):
                    act.wait_ge(activated, p - 1)
                pair(tile, q, p, c, slot)

            def silu_x(p, slot, b, g):
                act.wait_ge(convolved, 6 * p + 6)
                u = 8 * b + g
                if not (static(b) and b == 0 and g < 4):
                    act.wait_ge(y_step, 4 * (u - 3))
                A(xs[:, g % 4, :, :], acc[:, slot, :, :], ACT.Silu).then_inc(activated, 1)

            def silu_bc(b, p):
                act.wait_ge(convolved, 6 * p + 6)
                if not (static(b) and b == 0):
                    act.wait_ge(cb_done, 8 * b)
                for r in range(4):
                    rows = slice(SD * r, SD * r + SD)
                    ins = A(bz[rows, :, r, :], acc[rows, 0, :, :], ACT.Silu)
                ins.then_inc(activated, 1)
                act.wait_ge(convolved, 6 * p + 12)
                A(cs[:, :, :], acc[:, 1, :, :], ACT.Silu).then_inc(activated, 1)

            def gates(tile, q, b, g):
                u = 8 * b + g
                if not (static(b) and b == 0 and g < 4):
                    act.wait_ge(gated, u - 3)
                for j in range(2):
                    act.wait_ge(tile_full, tile + j + 1)
                    c = 2 * g + j
                    A(zs[:, g % 4, j, :], pi[(q + j) % 4][:, 0:L], ACT.Silu, scale=vm[:, c:c + 1],
                      bias=vb[:, c:c + 1]).then_inc(tile_free, 1)

            def unit(tile, q, b, g):
                p = Mamba.pair(b, g)
                project_pair(tile, q, p, 2 * g, g % 2)
                gates(tile + 2, q + 2, b, g)
                silu_x(p, g % 2, b, g)

            def bc(tile, q, b):
                p = 10 * b
                project_pair(tile, q, p, ZT, 0)
                project_pair(tile + 2, q + 2, p + 1, ZT + 2, 1)
                silu_bc(b, p)

            def deviation(tile, q, n):
                act.wait_ge(tile_full, tile + 1)
                if not (static(n) and n == 0):
                    act.wait_ge(rs_done, n)
                A(sd[:, :], pi[q % 4][:, 0:L], ACT.Sqrt, bias=eps[:, 0:1]).then_inc(tile_free, 1)

            def square(n, s, norm_tile):
                act.wait_ge(gated, n + 1)
                if norm_tile is not None:
                    act.wait_ge(tile_full, norm_tile + 1)
                A(sq[:, :, :], yg[:, s, :, :], ACT.Square).then_inc(squared, 1)

            def high(n, s, g):
                act.wait_ge(normed, n + 1)
                A(yn_hi[:, 2 * g:2 * g + 2, :], yg[:, s, :, :], ACT.Identity).then_inc(hi_done, 1)

            def residual(tile, q, b):
                if not (static(b) and b == 0):
                    act.wait_ge(h1_out, 16 * b)
                for j in range(KT):
                    act.wait_ge(tile_full, tile + j + 1)
                    A(h1[:, j, :], pi[(q + j) % 4][:, 0:L], ACT.Identity, scale=1.0 / (X_SCALE * O_SCALE),
                      bias=bo[:, j:j + 1]).then_inc(tile_free, 1)

            act.wait_ge(consts, 8)
            act.wait_ge(setup, 3 + 2)
            bc(0, 0, 0)
            unit(4, 0, 0, 0)

            def batch(b):
                for g in range(GROUPS):
                    u = 8 * b + g
                    q = (2 + 5 * g + (4 if g > 2 else 0)) % 4
                    if static(b) and b == 0 and g < 3:
                        q = 0

                    def previous():
                        if not (static(b) and b == 0 and g < 2):
                            nt = Mamba.norm(b, g)
                            deviation(nt, q + (0 if g == 7 else 8 if g == 2 and not (static(b) and b == 0) else 4), u - 2)
                        else:
                            nt = None
                        if not (static(b) and b == 0 and g == 0):
                            square(u - 1, (g - 1) % 2, nt)
                        if not (static(b) and b == 0 and g < 2):
                            high(u - 2, g % 2, (g - 2) % 8)

                    if g == GROUPS - 1:
                        previous()
                        if not last(b):
                            bc(Mamba.base(b, g) + 1, q + 1, b + 1)
                            unit(Mamba.project(b, g), q + 5, b + 1, 0)
                    else:
                        unit(Mamba.base(b, g), q, b, g + 1)
                        if g == 2 and not (static(b) and b == 0):
                            residual(Mamba.base(b, g) + 4, q + 4, b - 1)
                        previous()

            batches(act, batch)
            end = Mamba.base(NB - 1, 7) + 1
            deviation(end, end, UNITS - 2)
            square(UNITS - 1, 1, end)
            high(UNITS - 2, 0, 6)
            deviation(end + 1, end + 1, UNITS - 1)
            high(UNITS - 1, 1, 7)
            residual(end + 2, end + 2, NB - 1)

        @block.vector
        def _(dve):
            TT, TS, STT = nc.vector.tensor_tensor, nc.vector.tensor_scalar, nc.vector.scalar_tensor_tensor
            nc.vector.memset(xb[:, :, :, 0:3], 0.0).then_inc(consts, 1)
            nc.vector.memset(ones[:, :], 1.0).then_inc(consts, 1)
            nc.vector.memset(ones_g[:, :], float(GROUPS) / DS).then_inc(consts, 1)
            nc.vector.memset(eps[:, :], EPS).then_inc(consts, 1)
            for r in range(4):
                nc.vector.memset(bz[:, :, r, :], 0.0).then_inc(consts, 1)
            dve.wait_ge(small_in, 16 * 6)
            TT(vb[:, :], vb[:, :], vm[:, :], ALU.mult).then_inc(setup, 1)
            dve.wait_ge(setup, 1)
            TS(vm[:, :], vm[:, :], 1.0 / (X_SCALE * W_SCALE), None, ALU.mult).then_inc(setup, 1)
            dve.wait_ge(setup, 2)
            TT(sc3[:, :], vm[:, ZT:], cw[:, :, 3], ALU.mult).then_inc(setup, 1)
            TT(bi3[:, :], vb[:, ZT:], cw[:, :, 3], ALU.mult).then_inc(setup, 1)
            dve.wait_ge(setup, 4)
            TT(bi3[:, :], bi3[:, :], cb[:, :], ALU.add).then_inc(setup, 1)

            def convolve(p, slot, c, tile):
                dve.wait_ge(tile_free, tile + 2)
                for k in (2, 1, 0):
                    for j in range(2):
                        if k < 2:
                            dve.wait_ge(convolved, 6 * p + 2 * (1 - k) + j + 1)
                        STT(out=acc[:, slot, j, :], in0=xb[:, slot, j, k:k + L], scalar=cw[:, c + j, k:k + 1],
                            in1=acc[:, slot, j, :], op0=ALU.mult, op1=ALU.add).then_inc(convolved, 1)

            def tokens(n, s, b, g):
                dve.wait_ge(transposed, n + 1)
                if not (static(n) and n < 2):
                    dve.wait_ge(heads_done, n - 1)
                dt = keep["dt_tok"][:, :, b, GH * g:GH * g + GH]
                TT(xt[:, s, :, :].rearrange("p m (h f) -> p m h f", h=GH),
                   pt[:, :, :].rearrange("p m (h f) -> p m h f", h=GH), bcast(dt, 3, HD), ALU.mult).then_inc(xt_done, 1)

            def scan(n, s, count):
                dve.wait_ge(dec_in[s], count)
                if not (static(n) and n < 2):
                    dve.wait_ge(heads_done, n - 1)
                for h in range(GH):
                    nc.vector.tensor_tensor_scan(dec1[:, s, h, :], dec[:, s, h, P:L], ident[:, 0:L1], 0.0,
                                                 ALU.mult, ALU.add).then_inc(scanned, 1)
                dve.wait_ge(scanned, 8 * n + 4)
                for h in range(GH):
                    nc.vector.tensor_tensor_scan(dec[:, s, h, :], dec[:, s, h, :], ident[:, :], 0.0,
                                                 ALU.mult, ALU.add).then_inc(scanned, 1)

            def weigh(n, s):
                dve.wait_ge(cb_done, n + 1)
                dve.wait_ge(scanned, 8 * n + 8)
                TT(dec1[:, s, :, :], dec1[:, s, :, :], bcast(pg[:, L:L + L1], 1, GH), ALU.mult).then_inc(weighted, 1)
                TT(dec[:, s, :, :], dec[:, s, :, :], bcast(pg[:, 0:L], 1, GH), ALU.mult).then_inc(weighted, 1)

            def tail_products(b):
                dve.wait_ge(activated, 10 * b + 2)
                if not (static(b) and b == 0):
                    dve.wait_ge(cb_done, 8 * b)
                TT(tailp[:, :, :], bz[:, :, :, L - 1], bcast(cs[:, :, L - 1], 2, 4), ALU.mult).then_inc(tailp_done, 1)

            def tail_weights(b):
                if not (static(b) and b == 0):
                    dve.wait_ge(y_step, 32 * b)
                for hh in range(2):
                    rows = slice(HD * hh, HD * hh + HD)
                    dt = keep["dt_tail"][rows, b, :].rearrange("p (g q e) -> p g q e", q=2, e=2)[:, :, :, hh]
                    TT(tailw[rows, :, :], dt, bcast(pg[rows, 400:408], 2, 2), ALU.mult).then_inc(tailw_done, 1)

            def output(n, s, g, b1):
                dve.wait_ge(heads_done, n + 1)
                dve.wait_ge(tailw_done, 2 * b1)
                if not (static(n) and n < 2):
                    dve.wait_ge(lo_done, n - 1)
                    dve.wait_ge(hi_done, n - 1)
                for j in range(2):
                    c = 2 * g + j
                    STT(out=yg[:, s, j, :], in0=xs[:, g % 4, j, :], scalar=dp[:, c:c + 1], in1=py[j][:, 0:L],
                        op0=ALU.mult, op1=ALU.add).then_inc(y_step, 1)
                for j in range(2):
                    dve.wait_ge(y_step, 4 * n + j + 1)
                    col = yg[:, s, j, L - 1:L]
                    STT(out=col, in0=xs[:, g % 4, j, L - 1:L], scalar=tailw[:, g, j:j + 1], in1=col,
                        op0=ALU.mult, op1=ALU.add).then_inc(y_step, 1)
                dve.wait_ge(y_step, 4 * n + 4)
                TT(yg[:, s, :, :], yg[:, s, :, :], zs[:, g % 4, :, :], ALU.mult).then_inc(gated, 1)

            def normalise(n, s, tile):
                dve.wait_ge(tile_free, tile + 1)
                dve.wait_ge(squared, n + 1)
                if not (static(n) and n == 0):
                    dve.wait_ge(normed, n)
                nc.vector.reciprocal(rs[:, :], sd[:, :]).then_inc(rs_done, 1)
                dve.wait_ge(rs_done, n + 1)
                STT(out=yg[:, s, :, :], in0=yg[:, s, :, :], scalar=X_SCALE, in1=bcast(rs[:, :], 1, 2),
                    op0=ALU.mult, op1=ALU.mult).then_inc(normed, 1)

            dve.wait_ge(consts, 8)
            convolve(0, 0, ZT, 0)
            convolve(1, 1, ZT + 2, 2)
            convolve(2, 0, 0, 4)

            def batch(b):
                for g in range(GROUPS):
                    u = 8 * b + g
                    if g == 0:
                        tail_products(b)
                    tokens(u, g % 2, b, g)

                    def previous():
                        if not (static(b) and b == 0 and g == 0):
                            output(u - 1, (g - 1) % 2, (g - 1) % 8, b if g == 0 else b + 1)
                        if not (static(b) and b == 0 and g < 2):
                            normalise(u - 2, g % 2, Mamba.norm(b, g))
                        if g == 0:
                            tail_weights(b)

                    def now():
                        scan(u, g % 2, 16 * (4 * b + g // 2 + 1))
                        weigh(u, g % 2)

                    if g == GROUPS - 1:
                        now()
                        previous()
                        if not last(b):
                            tile, p = Mamba.base(b, g) + 1, 10 * b + 10
                            convolve(p, 0, ZT, tile)
                            convolve(p + 1, 1, ZT + 2, tile + 2)
                            convolve(p + 2, 0, 0, tile + 4)
                    else:
                        convolve(Mamba.pair(b, g + 1), (g + 1) % 2, 2 * (g + 1), Mamba.base(b, g))
                        now()
                        previous()

            batches(dve, batch)
            end = Mamba.base(NB - 1, 7) + 1
            output(UNITS - 1, 1, 7, NB)
            normalise(UNITS - 2, 0, end)
            normalise(UNITS - 1, 1, end + 1)

        @block.gpsimd
        def _(pool):
            def low(n, s, g):
                pool.wait_ge(hi_done, n + 1)
                nc.gpsimd.tensor_tensor(yn_lo[:, 2 * g:2 * g + 2, :], yg[:, s, :, :], yn_hi[:, 2 * g:2 * g + 2, :],
                                        ALU.subtract).then_inc(lo_done, 1)

            def add_residual(b, tile):
                pool.wait_ge(tile_free, tile + KT)
                pool.wait_ge(h_in, 16 * (b + 1))
                nc.gpsimd.tensor_tensor(h1[:, :, :], h1[:, :, :], hb[:, :, :], ALU.add).then_inc(h1_done, 1)

            def batch(b):
                for g in range(GROUPS):
                    if g == 2 and not (static(b) and b == 0):
                        add_residual(b - 1, Mamba.base(b, g) + 4)
                    if not (static(b) and b == 0 and g < 2):
                        low(8 * b + g - 2, g % 2, (g - 2) % 8)

            batches(pool, batch)
            end = Mamba.base(NB - 1, 7) + 1
            low(UNITS - 2, 0, 6)
            low(UNITS - 1, 1, 7)
            add_residual(NB - 1, end + 2)


def rotate_phase(nc, t, ffn):
    with ExitStack() as ctx:
        def sb(name, shape, dt=F32):
            return ctx.enter_context(nc.sbuf_tensor(name, shape, dt))

        def sem(name):
            return ctx.enter_context(nc.semaphore("r_" + name))

        UC, DC = D, P
        NU, ND = 2 * INTER // UC, D // DC
        PIECE = KT * UC
        assert IT * DC == PIECE
        had = sb("r_had", [P, P])
        wst = sb("r_wst", [P, 2, PIECE])
        mid = sb("r_mid", [P, 2, PIECE])
        su, sd = sb("r_su", [P, KT]), sb("r_sd", [P, IT])
        ps = [ctx.enter_context(nc.psum_tensor(f"r_ps{i}", [P, 512], F32)) for i in range(4)]
        small_in, scales = sem("small_in"), sem("scales")
        w_in = [sem(f"w_in{i}") for i in range(2)]
        step, summed, rotated, hi_done, lo_done = sem("step"), sem("summed"), sem("rotated"), sem("hi_done"), sem("lo_done")
        block = ctx.enter_context(nc.Block())
        pieces = [("ug", c) for c in range(NU)] + [("down", c) for c in range(ND)]

        @block.sync
        def _(sp):
            for dst, src in ((had, "hadamard"), (su, "SU_ug"), (sd, "SU_dp"),
                             (ffn["ws_ug"], "Wscale_ug"), (ffn["ws_dp"], "Wscale_dp")):
                sp.dma_start(dst[:, :], t[src]).then_inc(small_in, 16)
            for n, (kind, c) in enumerate(pieces):
                if n >= 2:
                    sp.wait_ge(summed, n - 1)
                if kind == "ug":
                    src, cols, k = t["W_ug"], slice(c * UC, c * UC + UC), KT
                else:
                    src, cols, k = t["W_down"], slice(c * DC, c * DC + DC), IT
                sp.dma_start(wst[:, n % 2, :].rearrange("p (k n) -> p k n", k=k),
                             src[:, cols].rearrange("(k p) n -> p k n", p=P)).then_inc(w_in[n % 2], 16)

        def target(n, q, which):
            kind, c = pieces[n]
            if kind == "ug":
                return ffn["ug_" + which][:, q, c * UC:c * UC + UC], [(slice(0, UC), su[:, q:q + 1])]
            return ffn["d_" + which][:, 4 * q:4 * q + 4, c * DC:c * DC + DC], [
                (slice(DC * j, DC * j + DC), sd[:, 4 * q + j:4 * q + j + 1]) for j in range(4)]

        def lows(dve, n):
            for q in range(4):
                dve.wait_ge(hi_done, 4 * n + q + 1)
                hi, parts = target(n, q, "hi")
                lo, _ = target(n, q, "lo")
                for j, (cols, scale) in enumerate(parts):
                    h, l = (hi, lo) if len(parts) == 1 else (hi[:, j, :], lo[:, j, :])
                    ins = nc.vector.scalar_tensor_tensor(out=l, in0=ps[q][:, cols], scalar=scale, in1=h,
                                                         op0=ALU.mult, op1=ALU.subtract)
                ins.then_inc(lo_done, 1)

        @block.vector
        def _(dve):
            TT, TS = nc.vector.tensor_tensor, nc.vector.tensor_scalar
            dve.wait_ge(small_in, 16 * 5)
            TS(su[:, :], su[:, :], W_SCALE / float(np.sqrt(D)), None, ALU.mult).then_inc(scales, 1)
            TS(sd[:, :], sd[:, :], W_SCALE / float(np.sqrt(INTER)), None, ALU.mult).then_inc(scales, 1)
            TS(ffn["ws_ug"][:, :], ffn["ws_ug"][:, :], 1.0 / (X_SCALE * W_SCALE), None, ALU.mult).then_inc(scales, 1)
            TS(ffn["ws_dp"][:, :], ffn["ws_dp"][:, :], 1.0 / W_SCALE, None, ALU.mult).then_inc(scales, 1)
            steps = 0
            for n, (kind, c) in enumerate(pieces):
                s = n % 2
                dve.wait_ge(w_in[s], 16 * (n // 2 + 1))
                if n >= 2:
                    dve.wait_ge(rotated, 4 * (n - 1))
                tiles = KT if kind == "ug" else IT
                levels = tiles.bit_length() - 1
                src, dst = wst, mid
                for level in range(levels):
                    d = 1 << level
                    v = lambda x: x[:, s, :].rearrange("p (a two b) -> p a two b", two=2, b=d * PIECE // tiles)
                    TT(v(dst)[:, :, 0, :], v(src)[:, :, 0, :], v(src)[:, :, 1, :], ALU.add).then_inc(step, 1)
                    TT(v(dst)[:, :, 1, :], v(src)[:, :, 0, :], v(src)[:, :, 1, :], ALU.subtract).then_inc(step, 1)
                    steps += 2
                    dve.wait_ge(step, steps)
                    src, dst = dst, src
                nc.vector.tensor_copy(mid[:, s, :], wst[:, s, :]).then_inc(summed, 1)
                if n:
                    lows(dve, n - 1)
            lows(dve, len(pieces) - 1)

        @block.scalar
        def _(act):
            act.wait_ge(scales, 4)
            for n in range(len(pieces)):
                for q in range(4):
                    act.wait_ge(rotated, 4 * n + q + 1)
                    hi, parts = target(n, q, "hi")
                    for j, (cols, scale) in enumerate(parts):
                        h = hi if len(parts) == 1 else hi[:, j, :]
                        ins = act.activation(h, ps[q][:, cols], ACT.Identity, scale=scale)
                    ins.then_inc(hi_done, 1)

        @block.tensor
        def _(pe):
            pe.wait_ge(small_in, 16 * 5)
            for n in range(len(pieces)):
                pe.wait_ge(summed, n + 1)
                for q in range(4):
                    if n:
                        pe.wait_ge(lo_done, 4 * (n - 1) + q + 1)
                    nc.tensor.matmul(ps[q][:, :], had[:, :], mid[:, n % 2, 512 * q:512 * q + 512],
                                     start=True, stop=True).then_inc(rotated, 1)


def ffn_phase(nc, t, scratch, keep, ffn, out):
    with ExitStack() as ctx:
        def sb(name, shape, dt=F32):
            return ctx.enter_context(nc.sbuf_tensor(name, shape, dt))

        def sem(name):
            return ctx.enter_context(nc.semaphore("f_" + name))

        h1 = sb("f_h1", [P, 2, KT, L])
        xc, sq = sb("f_xc", [P, KT, L]), sb("f_sq", [P, KT, L])
        sd, rs = sb("f_sd", [P, L]), sb("f_rs", [P, L])
        x2 = sb("f_x2", [P, 2, KT, L], F16)
        sg = sb("f_sg", [P, 2, L])
        mid = sb("f_mid", [P, 2, L])
        m_hi, m_lo = sb("f_m_hi", [P, IT, L], F16), sb("f_m_lo", [P, IT, L], F16)
        o = sb("f_o", [P, KT, L])
        eps = sb("f_eps", [P, 1])
        ws_ug, ws_dp = ffn["ws_ug"], ffn["ws_dp"]
        pu = [ctx.enter_context(nc.psum_tensor(f"f_pu{i}", [P, 512], F32)) for i in range(2)]
        pgt = [ctx.enter_context(nc.psum_tensor(f"f_pg{i}", [P, 512], F32)) for i in range(2)]
        pd = [ctx.enter_context(nc.psum_tensor(f"f_pd{i}", [P, 512], F32)) for i in range(2)]
        pm = ctx.enter_context(nc.psum_tensor("f_pm", [P, 512], F32))
        pv = ctx.enter_context(nc.psum_tensor("f_pv", [P, 512], F32))
        consts = sem("consts")
        h1_in = [sem(f"h1_in{i}") for i in range(2)]
        mean_done, centered, squared, var_done, sd_done, rs_done, normed = (sem(x) for x in (
            "mean_done", "centered", "squared", "var_done", "sd_done", "rs_done", "normed"))
        x_hi, x_lo = sem("x_hi"), sem("x_lo")
        gate_mm, up_mm, gate_act, product, mid_hi, mid_lo = (sem(x) for x in (
            "gate_mm", "up_mm", "gate_act", "product", "mid_hi", "mid_lo"))
        down_mm, summed, stored = sem("down_mm"), sem("summed"), sem("stored")
        block = ctx.enter_context(nc.Block())
        AT_MEAN, AT_VAR = 3, 7

        def pairs(eng, body):
            body(0, 0)
            body(1, 1)
            with eng.Fori(1, NB // 2 - 1) as i:
                body(2 * i, 0)
                body(2 * i + 1, 1)
            body(NB - 2, 0)
            body(NB - 1, 1)

        def more(b):
            return not (static(b) and b == NB - 1)

        @block.sync
        def _(sp):
            sp.dma_start(h1[:, 0, :, :], scratch["h1"][0]).then_inc(h1_in[0], 16)

            def batch(b, s):
                if more(b):
                    if not (static(b) and b == 0):
                        sp.wait_ge(summed, 4 * b)
                    sp.dma_start(h1[:, 1 - s, :, :], scratch["h1"][b + 1]).then_inc(h1_in[1 - s], 16)
                sp.wait_ge(summed, 4 * b + 4)
                sp.dma_start(out[b], o[:, :, :]).then_inc(stored, 16)

            pairs(sp, batch)
            sp.wait_ge(stored, 16 * NB)

        @block.tensor
        def _(pe):
            ones = keep["ones_d"]

            def moments(dst, src, ins_sem):
                for k in range(KT):
                    ins = nc.tensor.matmul(dst[:, 0:L], ones[:, :], src[:, k, :], start=k == 0, stop=k == KT - 1)
                ins.then_inc(ins_sem, 1)

            def mean(n, s):
                pe.wait_ge(h1_in[s], (n - s) * 8 + 16)
                if not (static(n) and n == 0):
                    pe.wait_ge(centered, n)
                moments(pm, h1[:, s, :, :], mean_done)

            def var(n):
                pe.wait_ge(squared, n + 1)
                if not (static(n) and n == 0):
                    pe.wait_ge(sd_done, n)
                moments(pv, sq, var_done)

            def split_mm(dst, k_tiles, w_hi, w_lo, x_hi, x_lo, done):
                for k in range(k_tiles):
                    for m, (w, x) in enumerate(((w_hi, x_hi), (w_hi, x_lo), (w_lo, x_hi))):
                        ins = nc.tensor.matmul(dst, w(k), x(k), start=k == 0 and m == 0,
                                               stop=k == k_tiles - 1 and m == 2)
                ins.then_inc(done, 1)

            def wide(dst, col, done):
                cols = slice(col, col + P)
                split_mm(dst[:, 0:L], KT, lambda k: ffn["ug_hi"][:, k, cols], lambda k: ffn["ug_lo"][:, k, cols],
                         lambda k: x2[:, 0, k, :], lambda k: x2[:, 1, k, :], done)

            pe.wait_ge(consts, 1)
            mean(0, 0)
            var(0)

            def batch(b, s):
                pe.wait_ge(x_lo, b + 1)
                pe.wait_ge(x_hi, b + 1)
                for j in range(IT):
                    n = 16 * b + j
                    if not (static(b) and b == 0 and j < 2):
                        pe.wait_ge(gate_act, n - 1)
                    wide(pgt[j % 2], INTER + j * P, gate_mm)
                    if not (static(b) and b == 0 and j < 2):
                        pe.wait_ge(product, n - 1)
                    wide(pu[j % 2], j * P, up_mm)
                    if more(b) and j == AT_MEAN:
                        mean(b + 1, 1 - s)
                    if more(b) and j == AT_VAR:
                        var(b + 1)
                for j in range(KT):
                    if not (static(b) and b == 0 and j < 2):
                        pe.wait_ge(summed, 4 * b + j - 1)
                    cols = slice(j * P, j * P + P)
                    if j == 0:
                        pe.wait_ge(mid_lo, 16 * b + 14)
                        pe.wait_ge(mid_hi, 16 * b + 14)
                    for k in range(IT):
                        if j == 0 and k >= 14:
                            pe.wait_ge(mid_lo, 16 * b + k + 1)
                            pe.wait_ge(mid_hi, 16 * b + k + 1)
                        for m, (w, x) in enumerate((("d_hi", m_hi), ("d_hi", m_lo), ("d_lo", m_hi))):
                            ins = nc.tensor.matmul(pd[j % 2][:, 0:L], ffn[w][:, k, cols], x[:, k, :],
                                                   start=k == 0 and m == 0, stop=k == IT - 1 and m == 2)
                    ins.then_inc(down_mm, 1)

            pairs(pe, batch)

        @block.scalar
        def _(act):
            A = act.activation

            def square(n):
                act.wait_ge(centered, n + 1)
                if not (static(n) and n == 0):
                    act.wait_ge(var_done, n)
                A(sq[:, :, :], xc[:, :, :], ACT.Square).then_inc(squared, 1)

            def deviation(n):
                act.wait_ge(var_done, n + 1)
                if not (static(n) and n == 0):
                    act.wait_ge(rs_done, n)
                A(sd[:, :], pv[:, 0:L], ACT.Sqrt, bias=eps[:, 0:1]).then_inc(sd_done, 1)

            def high(n, mm):
                act.wait_ge(normed, n + 1)
                if mm is not None:
                    act.wait_ge(up_mm, mm)
                A(x2[:, 0, :, :], xc[:, :, :], ACT.Identity).then_inc(x_hi, 1)

            act.wait_ge(consts, 1)
            square(0)
            deviation(0)
            high(0, None)

            def mid_high(n, j):
                act.wait_ge(product, n + 1)
                A(m_hi[:, j, :], mid[:, j % 2, :], ACT.Identity).then_inc(mid_hi, 1)

            def batch(b, s):
                for j in range(IT):
                    n = 16 * b + j
                    act.wait_ge(gate_mm, n + 1)
                    if not (static(b) and b == 0 and j < 2):
                        act.wait_ge(product, n - 1)
                    A(sg[:, j % 2, :], pgt[j % 2][:, 0:L], ACT.Silu, scale=ws_ug[:, IT + j:IT + j + 1]).then_inc(gate_act, 1)
                    if j == 0 and not (static(b) and b == 0):
                        act.wait_ge(down_mm, 4 * b)
                    if j:
                        mid_high(n - 1, j - 1)
                    if more(b) and j == AT_MEAN + 1:
                        square(b + 1)
                    if more(b) and j == AT_VAR + 1:
                        deviation(b + 1)
                mid_high(16 * b + IT - 1, IT - 1)
                if more(b):
                    high(b + 1, 16 * b + 16)

            pairs(act, batch)

        @block.vector
        def _(dve):
            TT, STT = nc.vector.tensor_tensor, nc.vector.scalar_tensor_tensor
            nc.vector.memset(eps[:, :], EPS).then_inc(consts, 1)

            def center(n, s):
                dve.wait_ge(mean_done, n + 1)
                if not (static(n) and n == 0):
                    dve.wait_ge(x_lo, n)
                    dve.wait_ge(x_hi, n)
                TT(xc[:, :, :], h1[:, s, :, :], bcast(pm[:, 0:L], 1, KT), ALU.subtract).then_inc(centered, 1)

            def normalise(n):
                dve.wait_ge(sd_done, n + 1)
                if not (static(n) and n == 0):
                    dve.wait_ge(normed, n)
                nc.vector.reciprocal(rs[:, :], sd[:, :]).then_inc(rs_done, 1)
                dve.wait_ge(rs_done, n + 1)
                dve.wait_ge(squared, n + 1)
                STT(out=xc[:, :, :], in0=xc[:, :, :], scalar=X_SCALE, in1=bcast(rs[:, :], 1, KT),
                    op0=ALU.mult, op1=ALU.mult).then_inc(normed, 1)

            dve.wait_ge(consts, 1)
            center(0, 0)
            normalise(0)

            def mid_low(n, j):
                dve.wait_ge(mid_hi, n + 1)
                TT(m_lo[:, j, :], mid[:, j % 2, :], m_hi[:, j, :], ALU.subtract).then_inc(mid_lo, 1)

            def batch(b, s):
                for j in range(IT):
                    n = 16 * b + j
                    dve.wait_ge(up_mm, n + 1)
                    dve.wait_ge(gate_act, n + 1)
                    if not (static(b) and b == 0 and j < 2):
                        dve.wait_ge(mid_lo, n - 1)
                    STT(out=mid[:, j % 2, :], in0=pu[j % 2][:, 0:L], scalar=ws_ug[:, j:j + 1], in1=sg[:, j % 2, :],
                        op0=ALU.mult, op1=ALU.mult).then_inc(product, 1)
                    if j:
                        mid_low(n - 1, j - 1)
                    if more(b) and j == AT_MEAN:
                        center(b + 1, 1 - s)
                    if more(b) and j == AT_VAR + 1:
                        normalise(b + 1)
                mid_low(16 * b + IT - 1, IT - 1)
                for j in range(KT):
                    dve.wait_ge(down_mm, 4 * b + j + 1)
                    if j == 0 and not (static(b) and b == 0):
                        dve.wait_ge(stored, 16 * b)
                    STT(out=o[:, j, :], in0=pd[j % 2][:, 0:L], scalar=ws_dp[:, j:j + 1], in1=h1[:, s, j, :],
                        op0=ALU.mult, op1=ALU.add).then_inc(summed, 1)

            pairs(dve, batch)

        @block.gpsimd
        def _(pool):
            def low(n):
                pool.wait_ge(x_hi, n + 1)
                nc.gpsimd.tensor_tensor(x2[:, 1, :, :], xc[:, :, :], x2[:, 0, :, :], ALU.subtract).then_inc(x_lo, 1)

            low(0)
            with pool.Fori(1, NB) as n:
                low(n)


def build(nc, t, out):
    def scr(name, shape, dt=F32):
        return nc.dram_tensor(f"scratch_{name}", shape, dt, kind="Internal").ap()

    scratch = {"h": scr("h", (NB, P, KT, L)), "xn": scr("xn", (NB, P, 2, KT, L), F16),
               "a": scr("a", (NB, HEADS, L)), "dt_tail": scr("dt_tail", (NB, HEADS, 1)),
               "h1": scr("h1", (NB, P, KT, L))}
    s4_phase(nc, t, scratch)
    with ExitStack() as ctx:
        def sb(name, shape, dt=F32):
            return ctx.enter_context(nc.sbuf_tensor(name, shape, dt))

        keep = {"ident": sb("ident", [P, L]), "ones_d": sb("ones_d", [P, P])}
        with ExitStack() as inner:
            def sbi(name, shape, dt=F32):
                return inner.enter_context(nc.sbuf_tensor(name, shape, dt))

            keep |= {"dt_tok": sbi("dt_tok", [P, 2, NB, HEADS]), "dt_tail": sbi("dt_tail", [P, NB, HEADS]),
                     "w_hi": sbi("w_hi", [P, KT, P * PT], F16), "w_lo": sbi("w_lo", [P, KT, P * PT], F16),
                     "o_hi": sbi("o_hi", [P, ZT, D], F16), "o_lo": sbi("o_lo", [P, ZT, D], F16)}
            with nc.sbuf_tensor("a_keep", [P, 4, L], F32) as a_keep:
                keep["a"] = a_keep
                prep_phase(nc, t, scratch, keep)
            mamba_phase(nc, t, scratch, keep)
        with ExitStack() as inner:
            def sbi(name, shape, dt=F32):
                return inner.enter_context(nc.sbuf_tensor(name, shape, dt))

            ffn = {"ug_hi": sbi("ug_hi", [P, KT, 2 * INTER], F16), "ug_lo": sbi("ug_lo", [P, KT, 2 * INTER], F16),
                   "d_hi": sbi("d_hi", [P, IT, D], F16), "d_lo": sbi("d_lo", [P, IT, D], F16),
                   "ws_ug": sbi("ws_ug", [P, 2 * IT]), "ws_dp": sbi("ws_dp", [P, KT])}
            rotate_phase(nc, t, ffn)
            ffn_phase(nc, t, scratch, keep, ffn, out)


def _hadamard(n):
    h = np.ones((1, 1), np.float32)
    while h.shape[0] < n:
        h = np.block([[h, h], [h, -h]])
    return h.astype(np.float32)


def _tiles(v):
    return np.ascontiguousarray(v.reshape(-1, P).T)


def layout(i):
    w_in, mup = i["L0_attn_W_in"], i["L0_attn_mup_vector"]
    b_in, n = i["L0_attn_b_in"], P * PT
    return {
        "C": np.ascontiguousarray(i["x"].transpose(3, 2, 1, 0)).reshape(P, NH, NB),
        "cls": _tiles(i["cls_tok"].reshape(-1)),
        "log_dt": i["L0_tok_log_dt"],
        "B_re": np.ascontiguousarray(i["L0_tok_B_ri"][..., 0].T),
        "B_im": np.ascontiguousarray(i["L0_tok_B_ri"][..., 1].T),
        "inv_A_real": np.ascontiguousarray(i["L0_tok_inv_A_real"].T),
        "A_imag": np.ascontiguousarray(i["L0_tok_A_imag"].T),
        "W_in": w_in,
        "b_in": _tiles(b_in[:n]),
        "mup": _tiles(mup[:n]),
        "dt_vec": np.ascontiguousarray(np.stack(
            [np.tile(v, P // HEADS) for v in (b_in[n:], mup[n:], i["L0_attn_dt_bias"], i["L0_attn_A_log"])], 1)),
        "conv_w": np.ascontiguousarray(i["L0_attn_conv_w"].reshape(CT, P, 4).transpose(1, 0, 2)),
        "conv_b": _tiles(i["L0_attn_conv_b"]),
        "D": _tiles(np.repeat(i["L0_attn_D_param"], HD)),
        "norm_w": _tiles(i["L0_attn_norm_w"]),
        "W_out": i["L0_attn_W_out"],
        "b_out": _tiles(i["L0_attn_b_out"]),
        "SU_ug": _tiles(i["L0_ffn_SU_ug"]),
        "SU_dp": _tiles(i["L0_ffn_SU_dp"]),
        "Wscale_ug": _tiles(i["L0_ffn_Wscale_ug"]),
        "Wscale_dp": _tiles(i["L0_ffn_Wscale_dp"]),
        "W_ug": np.ascontiguousarray(np.concatenate([i["L0_ffn_W_up"], i["L0_ffn_W_gate"]]).T),
        "W_down": np.ascontiguousarray(i["L0_ffn_W_down"].T),
        "hadamard": _hadamard(P),
        "ident": np.eye(P, L, dtype=np.float32),
    }


def kernel(**inputs):
    import concourse.bacc as bacc
    from concourse.bass_utils import run_bass_kernel_spmd

    arrays = {f"in_{k}": np.ascontiguousarray(v)
              for k, v in layout({k: np.asarray(v) for k, v in inputs.items()}).items()}
    nc = bacc.Bacc("TRN2", target_bir_lowering=False, num_devices=1)
    t = {k[3:]: nc.dram_tensor(k, a.shape, F32, kind="ExternalInput").ap() for k, a in arrays.items()}
    out = nc.dram_tensor("out", (NB, P, KT, L), F32, kind="ExternalOutput").ap()
    build(nc, t, out)
    r = run_bass_kernel_spmd(nc, [arrays], core_ids=[0])
    got = r.results[0]["out"]
    return np.ascontiguousarray(got.transpose(0, 3, 2, 1)).reshape(NB, L, D)
```

```python
from contextlib import ExitStack

import numpy as np

import concourse.bass as bass
from concourse import mybir

F32 = mybir.dt.float32
F16 = mybir.dt.float16
ALU = mybir.AluOpType
ACT = mybir.ActivationFunctionType

P = 128
NB = 16
NH = 256
NS = 64
D = 512
L = NH + 1
KT = D // P
HEADS = 32
HD = 64
GROUPS = 8
GH = HEADS // GROUPS
SD = 32
DS = HEADS * HD
ZT = DS // P
CT = (DS + 2 * GROUPS * SD) // P
PT = ZT + CT
PROJ = 2 * DS + 2 * GROUPS * SD + HEADS
INTER = 2048
IT = INTER // P
EPS = 1e-5
UNITS = NB * GROUPS

X_SCALE = 16.0
W_SCALE = 256.0
O_SCALE = 16.0

UCOLS = 2 * INTER // (2 * NB)
DCOLS = D // NB
PIECE = KT * UCOLS
assert PIECE == IT * DCOLS

HC = 8
CHUNKS = NH // HC


class Link:

    def __init__(self, eng, sem):
        self.eng, self.sem, self.n = eng, sem, 0

    def __call__(self, ins):
        ins.then_inc(self.sem, 1)
        self.n += 1
        self.eng.wait_ge(self.sem, self.n)


def bcast(ap, axis, n):
    u = ap.unsqueeze(axis)
    shape = list(u.shape)
    shape[axis] = n
    return u.broadcast_to(shape)


def static(v):
    return isinstance(v, int)


def peeled(eng, first, stop, body):
    body(first)
    with eng.Fori(first + 1, stop) as i:
        body(i)


def s4_phase(nc, t, scratch):
    with ExitStack() as ctx:
        def sb(name, shape, dt=F32):
            return ctx.enter_context(nc.sbuf_tensor(name, shape, dt))

        def sem(name):
            return ctx.enter_context(nc.semaphore(name))

        inv, aim, bre, bim, ldt = (sb(n, [P, NH]) for n in ("s4_inv", "s4_aim", "s4_bre", "s4_bim", "s4_ldt"))
        cp = sb("s4_cp", [P, NH, NB])
        cq = sb("s4_cq", [P, NH, NB])
        tmp = [sb(f"s4_tmp{i}", [P, NH]) for i in range(6)]
        er, ei = sb("s4_er", [P, 9, NH]), sb("s4_ei", [P, 9, NH])
        xj, yj = sb("s4_xj", [P, 16, NH]), sb("s4_yj", [P, 16, NH])
        cr, ci = sb("s4_cr", [P, 8, NH]), sb("s4_ci", [P, 8, NH])
        gr, gi = sb("s4_gr", [P, 4, NH]), sb("s4_gi", [P, 4, NH])
        sgn = sb("s4_sgn", [P, 3])
        v = sb("s4_v", [P, 2, HC, P])
        big = v[:, :, :, :].rearrange("p s h l -> p (s h l)")
        vt = sb("s4_vt", [P, 2, HC, P])
        uu = sb("s4_u", [P, 2, HC, 64])
        ut = sb("s4_ut", [P, 2, HC, 64])
        cls = sb("s4_cls", [P, KT])
        ht = sb("s4_ht", [P, KT, NB, L])
        ps = [ctx.enter_context(nc.psum_tensor(f"s4_ps{i}", [P, 8, 4, NB], F32)) for i in range(2)]

        loaded, cls_in, stored = sem("s4_loaded"), sem("s4_cls_in"), sem("s4_stored")
        exps, chain, params = sem("s4_exps"), sem("s4_chain"), sem("s4_params")
        pool_part, v_step, uv_ready = sem("s4_pool_part"), sem("s4_v_step"), sem("s4_uv_ready")
        mm_done, evac, cls_done = sem("s4_mm_done"), sem("s4_evac"), sem("s4_cls_done")

        block = ctx.enter_context(nc.Block())

        @block.sync
        def _(sp):
            for dst, src in ((inv, t["inv_A_real"]), (aim, t["A_imag"]), (bre, t["B_re"]), (bim, t["B_im"])):
                for h in range(2):
                    sp.dma_start(dst[NS * h:NS * h + NS, :], src).then_inc(loaded, 16)
            sp.dma_start(ldt[:, :], t["log_dt"].partition_broadcast(P)).then_inc(loaded, 16)
            sp.dma_start(cp[:, :, :], t["C"]).then_inc(loaded, 16)
            for h in range(2):
                sp.dma_start(cq[NS * h:NS * h + NS, :, :],
                             t["C"][NS * (1 - h):NS * (1 - h) + NS]).then_inc(loaded, 16)
            sp.dma_start(cls[:, :], t["cls"]).then_inc(cls_in, 16)
            sp.wait_ge(evac, CHUNKS)
            sp.wait_ge(cls_done, 1)
            for b in range(NB):
                sp.dma_start(scratch["h"][b], ht[:, :, b, :]).then_inc(stored, 16)
            sp.wait_ge(stored, 16 * NB)

        @block.scalar
        def _(act):
            act.wait_ge(cls_in, 16)
            act.activation(ht[:, :, :, 0], bcast(cls[:, :], 2, NB), ACT.Identity).then_inc(cls_done, 1)
            act.wait_ge(loaded, 16 * 12)
            act.activation(inv[:, :], inv[:, :], ACT.Exp).then_inc(exps, 1)
            act.activation(ldt[:, :], ldt[:, :], ACT.Exp).then_inc(exps, 1)

            def evacuate(i):
                for s in range(2):
                    act.wait_ge(mm_done, 2 * i + s + 1)
                    act.activation(ht[:, :, :, bass.ds(2 * HC * i + (1 + HC * s), HC)],
                                   ps[s][:, :, :, :].rearrange("p h a c -> p a c h"),
                                   ACT.Identity).then_inc(evac, 1)

            peeled(act, 0, CHUNKS // 2, evacuate)

        @block.vector
        def _(dve):
            link = Link(dve, chain)
            TT, TS, STT = nc.vector.tensor_tensor, nc.vector.tensor_scalar, nc.vector.scalar_tensor_tensor
            link(nc.vector.memset(sgn[:, :], 0.0))
            for half, vals in ((0, (1.0, 0.0, 2.0)), (1, (0.0, 1.0, -2.0))):
                for c, val in enumerate(vals):
                    link(nc.vector.memset(sgn[NS * half:NS * half + NS, c:c + 1], val))
            dve.wait_ge(exps, 2)
            t0, t1, t2, t3, t4, t5 = (x[:, :] for x in tmp)
            dt, a = ldt[:, :], inv[:, :]
            link(TS(t5, dt, 0.5, None, ALU.mult))
            link(STT(out=t0, in0=a, scalar=-1.0, in1=t5, op0=ALU.mult, op1=ALU.mult))
            link(TT(t1, aim[:, :], t5, ALU.mult))
            link(TS(t2, t0, -1.0, 1.0, ALU.mult, ALU.add))
            link(TT(t3, t2, t2, ALU.mult))
            link(TT(t4, t1, t1, ALU.mult))
            link(TT(t3, t3, t4, ALU.add))
            link(nc.vector.reciprocal(t3, t3))
            link(TT(t5, t0, t0, ALU.mult))
            link(TT(t5, t5, t4, ALU.add))
            link(TS(t5, t5, -1.0, 1.0, ALU.mult, ALU.add))
            link(TT(er[:, 0, :], t5, t3, ALU.mult))
            link(STT(out=ei[:, 0, :], in0=t1, scalar=2.0, in1=t3, op0=ALU.mult, op1=ALU.mult))
            link(TT(t3, t3, dt, ALU.mult))
            link(TT(t2, t2, t3, ALU.mult))
            link(TT(t1, t1, t3, ALU.mult))
            link(TT(gr[:, 0, :], bre[:, :], t2, ALU.mult))
            link(TT(t0, bim[:, :], t1, ALU.mult))
            link(TT(gr[:, 0, :], gr[:, 0, :], t0, ALU.subtract))
            link(TT(gi[:, 0, :], bre[:, :], t1, ALU.mult))
            link(TT(t0, bim[:, :], t2, ALU.mult))
            link(TT(gi[:, 0, :], gi[:, 0, :], t0, ALU.add))
            for k in range(8):
                r, i = er[:, k, :], ei[:, k, :]
                link(TT(t0, i, i, ALU.mult))
                link(TT(t1, r, r, ALU.mult))
                link(TT(er[:, k + 1, :], t1, t0, ALU.subtract))
                link(STT(out=ei[:, k + 1, :], in0=r, scalar=2.0, in1=i, op0=ALU.mult, op1=ALU.mult))

            def double(re, im, k, e, conj):
                tb = big[:, 0:k * NH].rearrange("p (k h) -> p k h", k=k)
                c, s = bcast(er[:, e, :], 1, k), bcast(ei[:, e, :], 1, k)
                r0, i0, r1, i1 = re[:, 0:k, :], im[:, 0:k, :], re[:, k:2 * k, :], im[:, k:2 * k, :]
                link(TT(tb, i0, s, ALU.mult))
                link(TT(r1, r0, c, ALU.mult))
                link(TT(r1, r1, tb, ALU.add if conj else ALU.subtract))
                link(TT(tb, r0, s, ALU.mult))
                link(TT(i1, i0, c, ALU.mult))
                link(TT(i1, i1, tb, ALU.subtract if conj else ALU.add))

            link(nc.vector.memset(xj[:, 0, :], 0.0))
            link(nc.vector.memset(yj[:, 0, :], 0.0))
            link(TS(xj[:, 0, :], xj[:, 0, :], sgn[:, 0:1], None, ALU.add))
            link(TS(yj[:, 0, :], yj[:, 0, :], sgn[:, 1:2], None, ALU.add))
            for e in range(4):
                double(xj, yj, 1 << e, e, True)
            link(nc.vector.memset(cr[:, 0, :], 1.0))
            link(nc.vector.memset(ci[:, 0, :], 0.0))
            for e in range(3):
                double(cr, ci, 1 << e, 4 + e, False)
            for e in range(2):
                double(gr, gi, 1 << e, 7 + e, False)
            link(TS(gr[:, :, :], gr[:, :, :], sgn[:, 2:3], None, ALU.mult))
            link(TS(gi[:, :, :], gi[:, :, :], -2.0, None, ALU.mult))
            nc.vector.memset(sgn[:, 0:1], 1.0).then_inc(params, 1)

            def form(i):
                for s in range(2):
                    hs = bass.ds(2 * HC * i + HC * s, HC)
                    n = 2 * i + s
                    c3 = bcast(cr[:, :, hs].rearrange("p i h -> p h i"), 3, 16)
                    x3 = bcast(xj[:, :, hs].rearrange("p j h -> p h j"), 2, 8)
                    if not static(i):
                        dve.wait_ge(mm_done, n - 1)
                    TT(v[:, s, :, :].rearrange("p h (i j) -> p h i j", i=8), c3, x3, ALU.mult).then_inc(v_step, 1)
                    g3 = bcast(gr[:, :, hs].rearrange("p a h -> p h a"), 3, NB)
                    p3 = bcast(cp[:, hs, :], 2, 4)
                    TT(uu[:, s, :, :].rearrange("p h (a c) -> p h a c", a=4), g3, p3, ALU.mult).then_inc(v_step, 1)
                    dve.wait_ge(v_step, 2 * n + 2)
                    dve.wait_ge(pool_part, 2 * n + 2)
                    TT(v[:, s, :, :], v[:, s, :, :], vt[:, s, :, :], ALU.add).then_inc(uv_ready, 1)
                    TT(uu[:, s, :, :], uu[:, s, :, :], ut[:, s, :, :], ALU.add).then_inc(uv_ready, 1)

            peeled(dve, 0, CHUNKS // 2, form)

        @block.gpsimd
        def _(pool):
            pool.wait_ge(params, 1)

            def partners(i):
                for s in range(2):
                    hs = bass.ds(2 * HC * i + HC * s, HC)
                    n = 2 * i + s
                    s3 = bcast(ci[:, :, hs].rearrange("p i h -> p h i"), 3, 16)
                    y3 = bcast(yj[:, :, hs].rearrange("p j h -> p h j"), 2, 8)
                    if not static(i):
                        pool.wait_ge(uv_ready, 2 * n - 2)
                    nc.gpsimd.tensor_tensor(vt[:, s, :, :].rearrange("p h (i j) -> p h i j", i=8), s3, y3,
                                            ALU.mult).then_inc(pool_part, 1)
                    g3 = bcast(gi[:, :, hs].rearrange("p a h -> p h a"), 3, NB)
                    q3 = bcast(cq[:, hs, :], 2, 4)
                    nc.gpsimd.tensor_tensor(ut[:, s, :, :].rearrange("p h (a c) -> p h a c", a=4), g3, q3,
                                            ALU.mult).then_inc(pool_part, 1)

            peeled(pool, 0, CHUNKS // 2, partners)

        @block.tensor
        def _(pe):
            def multiply(i):
                for s in range(2):
                    n = 2 * i + s
                    pe.wait_ge(uv_ready, 2 * n + 2)
                    if not static(i):
                        pe.wait_ge(evac, n - 1)
                    for h in range(HC):
                        last = nc.tensor.matmul(ps[s][:, h, :, :], v[:, s, h, :], uu[:, s, h, :],
                                                start=True, stop=True)
                    last.then_inc(mm_done, 1)

            peeled(pe, 0, CHUNKS // 2, multiply)


def prep_phase(nc, t, scratch, keep):
    with ExitStack() as ctx:
        def sb(name, shape, dt=F32):
            return ctx.enter_context(nc.sbuf_tensor(name, shape, dt))

        def sem(name):
            return ctx.enter_context(nc.semaphore(name))

        WC = P * PT // 4
        hb, xc, sq = sb("p_hb", [P, 4, KT, L]), sb("p_xc", [P, 2, KT, L]), sb("p_sq", [P, 2, KT, L])
        sd, rs = sb("p_sd", [P, 2, L]), sb("p_rs", [P, 2, L])
        xsp = sb("p_xsp", [P, 2, 2, KT, L], F16)
        wst = sb("p_wst", [P, 2, WC])
        ost = sb("p_ost", [P, 2, D])
        wdt = sb("p_wdt", [P, KT, HEADS])
        wdt_hi, wdt_lo = sb("p_wdt_hi", [P, KT, HEADS], F16), sb("p_wdt_lo", [P, KT, HEADS], F16)
        dtv = sb("p_dtv", [P, 4])
        nw = sb("p_nw", [P, ZT])
        eps = sb("p_eps", [P, 1])
        vec = sb("p_vec", [P, 3])
        dtr = sb("p_dtr", [P, 4, L])
        mean_ps = [ctx.enter_context(nc.psum_tensor(f"p_mean{i}", [P, 512], F32)) for i in range(2)]
        var_ps = [ctx.enter_context(nc.psum_tensor(f"p_var{i}", [P, 512], F32)) for i in range(2)]
        dt_ps = [ctx.enter_context(nc.psum_tensor(f"p_dt{i}", [P, 512], F32)) for i in range(2)]
        tr_ps = [ctx.enter_context(nc.psum_tensor(f"p_tr{i}", [P, P], F32)) for i in range(2)]

        small_in = sem("p_small_in")
        h_in = [sem(f"p_h_in{i}") for i in range(4)]
        w_in = [sem(f"p_w_in{i}") for i in range(2)]
        o_in = [sem(f"p_o_in{i}") for i in range(2)]
        setup, setup_act, consts = sem("p_setup"), sem("p_setup_act"), sem("p_consts")
        mean_done, centered, squared, var_done = sem("p_mean_done"), sem("p_centered"), sem("p_squared"), sem("p_var_done")
        sd_done, rs_done, normed, hi_done, lo_done = sem("p_sd_done"), sem("p_rs_done"), sem("p_normed"), sem("p_hi_done"), sem("p_lo_done")
        w_hi_done, w_lo_done, o_hi_done, o_lo_done = sem("p_w_hi_done"), sem("p_w_lo_done"), sem("p_o_hi_done"), sem("p_o_lo_done")
        dt_mm, dt_out = sem("p_dt_mm"), sem("p_dt_out")
        x_out = [sem(f"p_x_out{i}") for i in range(2)]
        chain, soft_act, dt_ready, tr_done, a_ready = sem("p_chain"), sem("p_soft_act"), sem("p_dt_ready"), sem("p_tr_done"), sem("p_a_ready")
        tr_out, stored, tail_in = sem("p_tr_out"), sem("p_stored"), sem("p_tail_in")

        block = ctx.enter_context(nc.Block())

        @block.sync
        def _(sp):
            sp.dma_start(wdt[:, :, :], t["W_in"][:, P * PT:].rearrange("(k p) n -> p k n", p=P)).then_inc(small_in, 16)
            sp.dma_start(dtv[:, :], t["dt_vec"]).then_inc(small_in, 16)
            sp.dma_start(nw[:, :], t["norm_w"]).then_inc(small_in, 16)
            sp.dma_start(keep["ident"][:, :], t["ident"]).then_inc(small_in, 16)

            def load_h(i, g):
                if not (static(i) and i == 0):
                    sp.wait_ge(centered, 4 * i + g - 3)
                sp.dma_start(hb[:, g, :, :], scratch["h"][4 * i + g]).then_inc(h_in[g], 16)

            def load_weights(i, g):
                n, s = 4 * i + g, g % 2
                if not (static(i) and i == 0 and g < 2):
                    sp.wait_ge(w_lo_done, n - 1)
                    sp.wait_ge(o_lo_done, n - 1)
                sp.dma_start(wst[:, s, :], t["W_in"][bass.ds(i * P, P), g * WC:g * WC + WC]).then_inc(w_in[s], 16)
                sp.dma_start(ost[:, s, :], t["W_out"][bass.ds(n * P, P), :]).then_inc(o_in[s], 16)

            for g in range(2):
                load_h(0, g)

            def four(i):
                for g in range(4):
                    if g < 2:
                        load_h(i, g + 2)
                    elif not (static(i) and i == 3):
                        load_h(i + 1, g - 2)
                    load_weights(i, g)

            four(0)
            with sp.Fori(1, 3) as i:
                four(i)
            four(3)
            sp.wait_ge(a_ready, 1)
            for g in range(4):
                rows = slice(HEADS * g, HEADS * g + HEADS)
                sp.dma_start(scratch["a"].rearrange("(i g) h l -> g h i l", g=4)[g], keep["a"][rows, :, :]).then_inc(stored, 16)
                sp.dma_start(scratch["dt_tail"].rearrange("(i g) h o -> g h i o", g=4)[g],
                             dtr[rows, :, L - 1:L], allow_slow_non_contiguous=True).then_inc(stored, 16)
            sp.wait_ge(stored, 16 * 8)
            sp.dma_start(keep["dt_tail"][:, :, :], scratch["dt_tail"].rearrange("b h o -> (b h o)").partition_broadcast(P)
                         .rearrange("p (b h) -> p b h", b=NB)).then_inc(tail_in, 16)
            sp.wait_ge(tail_in, 16)
            for q in range(2):
                sp.wait_ge(x_out[q], 16 * 8)

        @block.tensor
        def _(pe):
            ones = keep["ones_d"]

            def mean(i, g):
                n, s = 4 * i + g, g % 2
                pe.wait_ge(h_in[g], 16 * i + 16)
                if not (static(i) and i == 0 and g < 2):
                    pe.wait_ge(centered, n - 1)
                for k in range(KT):
                    last = nc.tensor.matmul(mean_ps[s][:, 0:L], ones[:, :], hb[:, g, k, :], start=k == 0, stop=k == KT - 1)
                last.then_inc(mean_done, 1)

            def var(n, s):
                pe.wait_ge(squared, n + 1)
                if not (static(n) and n < 2):
                    pe.wait_ge(sd_done, n - 1)
                for k in range(KT):
                    last = nc.tensor.matmul(var_ps[s][:, 0:L], ones[:, :], sq[:, s, k, :], start=k == 0, stop=k == KT - 1)
                last.then_inc(var_done, 1)

            def dts(n, s, g):
                pe.wait_ge(lo_done, n + 1)
                pe.wait_ge(hi_done, n + 1)
                if not (static(n) and n < 2):
                    pe.wait_ge(dt_out, n - 1)
                rows = slice(HEADS * g, HEADS * g + HEADS)
                for k in range(KT):
                    for m, (w, x) in enumerate(((wdt_hi, 0), (wdt_hi, 1), (wdt_lo, 0))):
                        last = nc.tensor.matmul(dt_ps[s][rows, 0:L], w[:, k, :], xsp[:, s, x, k, :],
                                                start=k == 0 and m == 0, stop=k == KT - 1 and m == 2)
                last.then_inc(dt_mm, 1)

            pe.wait_ge(consts, 2)
            pe.wait_ge(setup, 5)
            mean(0, 0)

            def four(i):
                for g in range(4):
                    n = 4 * i + g
                    var(n, g % 2)
                    if g < 3:
                        mean(i, g + 1)
                    elif not (static(i) and i == 3):
                        mean(i + 1, 0)
                    if not (g == 0 and static(i) and i == 0):
                        dts(n - 1, (g - 1) % 2, (g - 1) % 4)

            four(0)
            with pe.Fori(1, 3) as i:
                four(i)
            four(3)
            dts(NB - 1, 1, 3)
            pe.wait_ge(dt_ready, 1)
            for m in range(2):
                for i in range(4):
                    n = 4 * m + i
                    if n >= 2:
                        pe.wait_ge(tr_out, n - 1)
                    nc.tensor.transpose(tr_ps[n % 2][:, :], dtr[:, i, P * m:P * m + P], keep["ident"][:, 0:P]).then_inc(tr_done, 1)

        @block.scalar
        def _(act):
            A = act.activation
            act.wait_ge(consts, 2)
            act.wait_ge(small_in, 64)
            A(wdt_hi[:, :, :], wdt[:, :, :], ACT.Identity, scale=W_SCALE).then_inc(setup_act, 1)
            act.wait_ge(setup, 1)
            A(vec[:, 2:3], vec[:, 2:3], ACT.Exp).then_inc(setup_act, 1)
            act.wait_ge(setup, 5)

            def square(n, s):
                act.wait_ge(centered, n + 1)
                if not (static(n) and n < 2):
                    act.wait_ge(var_done, n - 1)
                A(sq[:, s, :, :], xc[:, s, :, :], ACT.Square).then_inc(squared, 1)

            square(0, 0)

            def four(i):
                for g in range(4):
                    n, s = 4 * i + g, g % 2
                    nws = nw[:, n:n + 1] if static(n) else nw[:, bass.ds(n, 1)]
                    act.wait_ge(var_done, n + 1)
                    if not (static(n) and n < 2):
                        act.wait_ge(rs_done, n - 1)
                    A(sd[:, s, :], var_ps[s][:, 0:L], ACT.Sqrt, bias=eps[:, 0:1]).then_inc(sd_done, 1)
                    if not (static(n) and n == 0):
                        act.wait_ge(lo_done, n)
                        act.dma_start(scratch["xn"][n - 1], xsp[:, 1 - s, :, :, :]).then_inc(x_out[1 - s], 16)
                    act.wait_ge(w_in[s], 16 * (2 * i + g // 2 + 1))
                    A(keep["w_hi"][:, i, g * WC:g * WC + WC], wst[:, s, :], ACT.Identity, scale=W_SCALE).then_inc(w_hi_done, 1)
                    act.wait_ge(o_in[s], 16 * (2 * i + g // 2 + 1))
                    A(keep["o_hi"][:, n, :], ost[:, s, :], ACT.Identity, scale=nws).then_inc(o_hi_done, 1)
                    act.wait_ge(normed, n + 1)
                    if not (static(n) and n < 2):
                        act.wait_ge(x_out[s], 16 * (2 * i + g // 2))
                    A(xsp[:, s, 0, :, :], xc[:, s, :, :], ACT.Identity).then_inc(hi_done, 1)
                    if not (g == 3 and static(i) and i == 3):
                        square(n + 1, (g + 1) % 2)
                    if not (g == 0 and static(i) and i == 0):
                        dt_evac(n - 1, (g - 1) % 2, (g - 1) % 4, i if g else i - 1)

            def dt_evac(n, s, g, i):
                act.wait_ge(dt_mm, n + 1)
                rows = slice(HEADS * g, HEADS * g + HEADS)
                A(dtr[rows, i, :], dt_ps[s][rows, 0:L], ACT.Identity, scale=vec[rows, 0:1],
                  bias=vec[rows, 1:2]).then_inc(dt_out, 1)

            four(0)
            with act.Fori(1, 3) as i:
                four(i)
            four(3)
            act.wait_ge(lo_done, NB)
            act.dma_start(scratch["xn"][NB - 1], xsp[:, 1, :, :, :]).then_inc(x_out[1], 16)
            dt_evac(NB - 1, 1, 3, 3)
            act.wait_ge(dt_out, NB)
            A(sq[:, 0, :, :], dtr[:, :, :], ACT.Abs).then_inc(soft_act, 1)
            act.wait_ge(soft_act, 1)
            A(sq[:, 1, :, :], sq[:, 0, :, :], ACT.Exp, scale=-1.0).then_inc(soft_act, 1)
            act.wait_ge(dt_ready, 2)
            A(keep["a"][:, :, :], sq[:, 0, :, :], ACT.Exp).then_inc(soft_act, 1)

        @block.vector
        def _(dve):
            TT, TS, STT = nc.vector.tensor_tensor, nc.vector.tensor_scalar, nc.vector.scalar_tensor_tensor
            dve.wait_ge(small_in, 64)
            TS(vec[:, 2:3], dtv[:, 3:4], 88.0, None, ALU.min).then_inc(setup, 1)
            TS(vec[:, 0:1], dtv[:, 1:2], 1.0 / (X_SCALE * W_SCALE), None, ALU.mult).then_inc(setup, 1)
            STT(out=vec[:, 1:2], in0=dtv[:, 0:1], scalar=dtv[:, 1:2], in1=dtv[:, 2:3], op0=ALU.mult, op1=ALU.add).then_inc(setup, 1)
            TS(nw[:, :], nw[:, :], O_SCALE, None, ALU.mult).then_inc(setup, 1)
            dve.wait_ge(setup_act, 1)
            STT(out=wdt_lo[:, :, :], in0=wdt[:, :, :], scalar=W_SCALE, in1=wdt_hi[:, :, :],
                op0=ALU.mult, op1=ALU.subtract).then_inc(setup, 1)
            dve.wait_ge(setup_act, 2)
            dve.wait_ge(setup, 5)
            TS(vec[:, 2:3], vec[:, 2:3], -1.0, None, ALU.mult).then_inc(setup, 1)

            def center(n, s, g):
                dve.wait_ge(mean_done, n + 1)
                if not (static(n) and n < 2):
                    dve.wait_ge(lo_done, n - 1)
                TT(xc[:, s, :, :], hb[:, g, :, :], bcast(mean_ps[s][:, 0:L], 1, KT), ALU.subtract).then_inc(centered, 1)

            center(0, 0, 0)

            def four(i):
                for g in range(4):
                    n, s = 4 * i + g, g % 2
                    nws = nw[:, n:n + 1] if static(n) else nw[:, bass.ds(n, 1)]
                    dve.wait_ge(sd_done, n + 1)
                    if not (static(n) and n < 2):
                        dve.wait_ge(normed, n - 1)
                    nc.vector.reciprocal(rs[:, s, :], sd[:, s, :]).then_inc(rs_done, 1)
                    dve.wait_ge(rs_done, n + 1)
                    STT(out=xc[:, s, :, :], in0=xc[:, s, :, :], scalar=X_SCALE, in1=bcast(rs[:, s, :], 1, KT),
                        op0=ALU.mult, op1=ALU.mult).then_inc(normed, 1)
                    if not (g == 3 and static(i) and i == 3):
                        center(n + 1, (g + 1) % 2, (g + 1) % 4)
                    dve.wait_ge(w_hi_done, n + 1)
                    cols = slice(g * WC, g * WC + WC)
                    STT(out=keep["w_lo"][:, i, cols], in0=wst[:, s, :], scalar=W_SCALE, in1=keep["w_hi"][:, i, cols],
                        op0=ALU.mult, op1=ALU.subtract).then_inc(w_lo_done, 1)
                    dve.wait_ge(o_hi_done, n + 1)
                    STT(out=keep["o_lo"][:, n, :], in0=ost[:, s, :], scalar=nws,
                        in1=keep["o_hi"][:, n, :], op0=ALU.mult, op1=ALU.subtract).then_inc(o_lo_done, 1)

            four(0)
            with dve.Fori(1, 3) as i:
                four(i)
            four(3)
            link = Link(dve, chain)
            dve.wait_ge(soft_act, 2)
            u, q, q2, w = sq[:, 1, :, :], sq[:, 0, :, :], xc[:, 0, :, :], xc[:, 1, :, :]
            link(TS(q, u, 2.0, None, ALU.add))
            link(nc.vector.reciprocal(q, q))
            link(TT(q, q, u, ALU.mult))
            link(TT(q2, q, q, ALU.mult))
            link(TS(w, q2, 1.0 / 17, None, ALU.mult))
            for k in range(7, 0, -1):
                link(STT(out=w, in0=w, scalar=1.0 / (2 * k + 1), in1=q2, op0=ALU.add, op1=ALU.mult))
            link(STT(out=w, in0=w, scalar=1.0, in1=q, op0=ALU.add, op1=ALU.mult))
            link(TS(w, w, 2.0, None, ALU.mult))
            STT(out=dtr[:, :, :], in0=dtr[:, :, :], scalar=0.0, in1=w, op0=ALU.max, op1=ALU.add).then_inc(dt_ready, 1)
            dve.wait_ge(dt_ready, 1)
            TS(sq[:, 0, :, :], dtr[:, :, :], vec[:, 2:3], -200.0, ALU.mult, ALU.max).then_inc(dt_ready, 1)
            dve.wait_ge(soft_act, 3)
            nc.vector.memset(keep["a"][:, :, 0:1], 0.0).then_inc(a_ready, 1)
            for m in range(2):
                for i in range(4):
                    n = 4 * m + i
                    dve.wait_ge(tr_done, n + 1)
                    nc.vector.tensor_copy(keep["dt_tok"][:, m, 4 * i:4 * i + 4, :].rearrange("p b h -> p (b h)"),
                                          tr_ps[n % 2][:, :]).then_inc(tr_out, 1)

        @block.gpsimd
        def _(pool):
            nc.gpsimd.memset(keep["ones_d"][:, :], 1.0 / D).then_inc(consts, 1)
            nc.gpsimd.memset(eps[:, :], EPS).then_inc(consts, 1)

            def four(i):
                for g in range(4):
                    n, s = 4 * i + g, g % 2
                    pool.wait_ge(hi_done, n + 1)
                    if not (static(n) and n < 2):
                        pool.wait_ge(x_out[s], 16 * (2 * i + g // 2))
                    nc.gpsimd.tensor_tensor(xsp[:, s, 1, :, :], xc[:, s, :, :], xsp[:, s, 0, :, :], ALU.subtract).then_inc(lo_done, 1)

            peeled(pool, 0, 4, four)


class Mamba:

    STEP = 5 * GROUPS + 8

    @staticmethod
    def starts(b, g):
        return static(b) and b == 0 and g < 2

    @staticmethod
    def base(b, g):
        if static(b) and b == 0 and g < 3:
            return 8 + 4 * g
        return 2 + Mamba.STEP * b + 5 * g + (4 if g > 2 else 0)

    @staticmethod
    def bank(b, g):
        return Mamba.base(0 if static(b) and b == 0 else 1, g) % 4

    @staticmethod
    def x(b, g):
        return 5 if g == GROUPS - 1 else 0

    @staticmethod
    def z(b, g):
        return 7 if g == GROUPS - 1 else 2 if Mamba.starts(b, g) else 3

    @staticmethod
    def norm(b, g):
        return 0 if g == GROUPS - 1 else 2

    OUT = 5

    @staticmethod
    def pair(b, g):
        return 2 + 10 * b + g


def mamba_phase(nc, t, scratch, keep):
    with ExitStack() as ctx:
        def sb(name, shape, dt=F32):
            return ctx.enter_context(nc.sbuf_tensor(name, shape, dt))

        def sem(name):
            return ctx.enter_context(nc.semaphore("m_" + name))

        L1 = L - P
        xn = sb("m_xn", [P, 2, KT, L], F16)
        hb, h1 = sb("m_hb", [P, KT, L]), sb("m_h1", [P, KT, L])
        vb, vm = sb("m_vb", [P, PT]), sb("m_vm", [P, PT])
        cw, cb = sb("m_cw", [P, CT, 4]), sb("m_cb", [P, CT])
        sc3, bi3 = sb("m_sc3", [P, CT]), sb("m_bi3", [P, CT])
        dp, bo = sb("m_dp", [P, ZT]), sb("m_bo", [P, KT])
        xb, acc = sb("m_xb", [P, 2, 2, L + 3]), sb("m_acc", [P, 2, 2, L])
        xs, zs = sb("m_xs", [P, 4, 2, L]), sb("m_zs", [P, 4, 2, L])
        bz = sb("m_bz", [P, 2, 4, L])
        cs = sb("m_cs", [P, 2, L])
        xt = sb("m_xt", [P, 2, 2, 2 * P])
        dec = sb("m_dec", [P, 2, GH, L])
        dec1 = sb("m_dec1", [P, 2, GH, L1])
        yg = sb("m_yg", [P, 2, 2, L])
        sq = sb("m_sq", [P, 2, L])
        sd, rs = sb("m_sd", [P, L]), sb("m_rs", [P, L])
        yn_hi, yn_lo = sb("m_yn_hi", [P, ZT, L], F16), sb("m_yn_lo", [P, ZT, L], F16)
        tailp, tailw = sb("m_tailp", [P, 2, 4]), sb("m_tailw", [P, GROUPS, 2])
        ones_g, ones = sb("m_ones_g", [P, P]), sb("m_ones", [P, P])
        eps = sb("m_eps", [P, 1])
        rot_in, rot_mid = sb("m_rot_in", [P, 2, PIECE]), sb("m_rot_mid", [P, PIECE])
        ident = keep["ident"]
        pi = [ctx.enter_context(nc.psum_tensor(f"m_pi{i}", [P, 512], F32)) for i in range(4)]
        pt = ctx.enter_context(nc.psum_tensor("m_pt", [P, 2, 2 * P], F32))
        pg = ctx.enter_context(nc.psum_tensor("m_pg", [P, 512], F32))
        py = [ctx.enter_context(nc.psum_tensor(f"m_py{i}", [P, 512], F32)) for i in range(2)]

        small_in, consts, setup = sem("small_in"), sem("consts"), sem("setup")
        xn_in, h_in, h1_out = sem("xn_in"), sem("h_in"), sem("h1_out")
        dec_in = [sem(f"dec_in{i}") for i in range(2)]
        piece_in, piece_out = ([sem(f"piece_{x}{j}") for j in range(3)] for x in ("in", "out"))
        piece_step = sem("piece_step")
        load_at, store_at = {0: 0, 1: 1, 4: 2}, {3: (0, 1), 6: (2,)}
        tile_full, tile_free = sem("tile_full"), sem("tile_free")
        transposed, cb_done, heads_done = sem("transposed"), sem("cb_done"), sem("heads_done")
        convolved, activated = sem("convolved"), sem("activated")
        squared, hi_done, lo_done, h1_done = sem("squared"), sem("hi_done"), sem("lo_done"), sem("h1_done")
        xt_done, scanned, weighted = sem("xt_done"), sem("scanned"), sem("weighted")
        tailp_done, tailw_done = sem("tailp_done"), sem("tailw_done")
        y_step, gated, rs_done, normed = sem("y_step"), sem("gated"), sem("rs_done"), sem("normed")

        block = ctx.enter_context(nc.Block())

        def batches(eng, body):
            body(0)
            body(1)
            with eng.Fori(2, NB - 1) as b:
                body(b)
            body(NB - 1)

        def last(b):
            return static(b) and b == NB - 1

        @block.sync
        def _(sp):
            for dst, src in ((vb, "b_in"), (vm, "mup"), (cb, "conv_b"), (dp, "D"), (bo, "b_out")):
                sp.dma_start(dst[:, :], t[src]).then_inc(small_in, 16)
            sp.dma_start(cw[:, :, :], t["conv_w"]).then_inc(small_in, 16)

            def decays(n, b, g, s):
                sp.dma_start(dec[:, s, :, :].rearrange("p h l -> p (h l)"),
                             scratch["a"].rearrange("b (g h) l -> b g (h l)", h=GH)[b, g].partition_broadcast(P)
                             ).then_inc(dec_in[s], 16)

            sp.dma_start(xn[:, :, :, :], scratch["xn"][0]).then_inc(xn_in, 16)
            decays(0, 0, 0, 0)

            def load_h(b):
                if not (static(b) and b == 1):
                    sp.wait_ge(h1_done, b - 1)
                sp.dma_start(hb[:, :, :], scratch["h"][b - 1]).then_inc(h_in, 16)

            def piece(b, j):
                if j:
                    return t["W_ug"][2 * b + j - 1], scratch["ug_sum"][2 * b + j - 1]
                return t["W_down"][b], scratch["down_sum"][b]

            def load_piece(b, j):
                if j == 2:
                    sp.wait_ge(piece_out[0], 16 * b + 16)
                elif not (static(b) and b == 0):
                    sp.wait_ge(piece_out[(2, 1)[j]], 16 * b)
                sp.dma_start(rot_in[:, j % 2, :], piece(b, j)[0]).then_inc(piece_in[j], 16)

            def store_piece(b, j):
                sp.wait_ge(piece_step, 16 * b + (8, 12, 16)[j])
                sp.dma_start(piece(b, j)[1], rot_in[:, j % 2, :]).then_inc(piece_out[j], 16)

            def batch(b):
                for g in range(GROUPS):
                    u = 8 * b + g
                    if g == 0:
                        if not (static(b) and b == 0):
                            load_h(b)
                    if g == 3 and not (static(b) and b == 0):
                        sp.wait_ge(h1_done, b)
                        sp.dma_start(scratch["h1"][b - 1], h1[:, :, :]).then_inc(h1_out, 16)
                    if g == GROUPS - 1 and not last(b):
                        sp.wait_ge(tile_full, Mamba.base(b, g - 1) + Mamba.z(b, g - 1) + 2)
                        sp.dma_start(xn[:, :, :, :], scratch["xn"][b + 1]).then_inc(xn_in, 16)
                    if not (last(b) and g == GROUPS - 1):
                        if not (static(b) and b == 0 and g == 0):
                            sp.wait_ge(heads_done, u)
                        if g < GROUPS - 1:
                            decays(u + 1, b, g + 1, (g + 1) % 2)
                        else:
                            decays(u + 1, b + 1, 0, 0)
                    if g in store_at:
                        for j in store_at[g]:
                            store_piece(b, j)
                    if g in load_at:
                        load_piece(b, load_at[g])

            batches(sp, batch)
            sp.wait_ge(h1_done, NB - 1)
            sp.dma_start(hb[:, :, :], scratch["h"][NB - 1]).then_inc(h_in, 16)
            sp.wait_ge(h1_done, NB)
            sp.dma_start(scratch["h1"][NB - 1], h1[:, :, :]).then_inc(h1_out, 16)
            sp.wait_ge(h1_out, 16 * NB)
            for j in range(3):
                sp.wait_ge(piece_out[j], 16 * NB)

        @block.tensor
        def _(pe):
            def split_mm(dst, k_tiles, w_hi, w_lo, x_hi, x_lo):
                for k in range(k_tiles):
                    for m, (w, x) in enumerate(((w_hi, x_hi), (w_hi, x_lo), (w_lo, x_hi))):
                        ins = nc.tensor.matmul(dst, w(k), x(k), start=k == 0 and m == 0,
                                               stop=k == k_tiles - 1 and m == 2)
                ins.then_inc(tile_full, 1)

            def project(tile, q, cols):
                if not static(tile) or tile >= 4:
                    pe.wait_ge(tile_free, tile - 3)
                cols = slice(cols * P, cols * P + P)
                split_mm(pi[q][:, 0:L], KT, lambda k: keep["w_hi"][:, k, cols], lambda k: keep["w_lo"][:, k, cols],
                         lambda k: xn[:, 0, k, :], lambda k: xn[:, 1, k, :])

            def project_bc(tile, q):
                for j in range(4):
                    project(tile + j, (q + j) % 4, 2 * ZT + j)

            def project_x(tile, q, g):
                for j in range(2):
                    project(tile + j, (q + j) % 4, ZT + 2 * g + j)

            def project_z(tile, q, g):
                for j in range(2):
                    project(tile + j, (q + j) % 4, 2 * g + j)

            def heads(n, s):
                pe.wait_ge(weighted, 2 * n + 2)
                pe.wait_ge(xt_done, n + 1)
                if not (static(n) and n == 0):
                    pe.wait_ge(y_step, 4 * n)
                for q in range(2):
                    for hh in range(2):
                        h = 2 * q + hh
                        rows, cols = slice(HD * hh, HD * hh + HD), slice(HD * h, HD * h + HD)
                        nc.tensor.matmul(py[q][rows, 0:L], xt[:, s, 0, cols], dec[:, s, h, :], start=True, stop=False)
                        ins = nc.tensor.matmul(py[q][rows, P:L], xt[:, s, 1, cols], dec1[:, s, h, :], start=False, stop=True)
                ins.then_inc(heads_done, 1)

            def norm(tile, q, n):
                pe.wait_ge(squared, n + 1)
                pe.wait_ge(tile_free, tile - 3)
                for j in range(2):
                    ins = nc.tensor.matmul(pi[q][:, 0:L], ones_g[:, :], sq[:, j, :], start=j == 0, stop=j == 1)
                ins.then_inc(tile_full, 1)

            def out_project(tile, q, b):
                pe.wait_ge(lo_done, 8 * b + 8)
                pe.wait_ge(hi_done, 8 * b + 8)
                for j in range(KT):
                    pe.wait_ge(tile_free, tile + j - 3)
                    cols = slice(j * P, j * P + P)
                    split_mm(pi[(q + j) % 4][:, 0:L], ZT, lambda k: keep["o_hi"][:, k, cols],
                             lambda k: keep["o_lo"][:, k, cols], lambda k: yn_hi[:, k, :], lambda k: yn_lo[:, k, :])

            pe.wait_ge(consts, 8)
            pe.wait_ge(xn_in, 16)
            project_bc(0, 0)
            project_x(4, 0, 0)
            project_z(6, 2, 0)

            def batch(b):
                for g in range(GROUPS):
                    u = 8 * b + g
                    tile, q = Mamba.base(b, g), Mamba.bank(b, g)
                    x, z, nt = Mamba.x(b, g), Mamba.z(b, g), Mamba.norm(b, g)
                    pe.wait_ge(activated, Mamba.pair(b, g) + 1)
                    if not (static(b) and b == 0 and g == 0):
                        pe.wait_ge(xt_done, u)
                    for m in range(2):
                        for j in range(2):
                            ins = nc.tensor.transpose(pt[:, m, j * P:j * P + P], xs[:, g % 4, j, m * P:m * P + P], ident[:, 0:P])
                    ins.then_inc(transposed, 1)
                    if not (static(b) and b == 0 and g == 0):
                        pe.wait_ge(weighted, 2 * u)
                    if g == 0:
                        pe.wait_ge(tailp_done, b + 1)
                        nc.tensor.matmul(pg[:, 400:408], ones[:, :], tailp[:, :, :].rearrange("p t r -> p (t r)"),
                                         start=True, stop=True)
                    if g == 1:
                        pe.wait_ge(tailw_done, 2 * b + 2)
                    nc.tensor.matmul(pg[:, 0:L], bz[:, g // 4, g % 4, 0:P], cs[:, g // 4, :], start=True, stop=True)
                    nc.tensor.matmul(pg[:, L:L + L1], bz[:, g // 4, g % 4, P:2 * P], cs[:, g // 4, P:L],
                                     start=True, stop=True).then_inc(cb_done, 1)

                    def sums():
                        if not Mamba.starts(b, g):
                            norm(tile + nt, (q + nt) % 4, u - 2)

                    def previous():
                        if not (static(b) and b == 0 and g == 0):
                            heads(u - 1, (g - 1) % 2)

                    if g == GROUPS - 1:
                        sums()
                        previous()
                        if not last(b):
                            pe.wait_ge(xn_in, 16 * (b + 2))
                            project_bc(tile + 1, q + 1)
                            project_x(tile + x, q + x, 0)
                            project_z(tile + z, q + z, 0)
                    else:
                        project_x(tile + x, q + x, g + 1)
                        sums()
                        previous()
                        project_z(tile + z, q + z, g + 1)
                        if g == 2 and not (static(b) and b == 0):
                            out_project(tile + Mamba.OUT, q + Mamba.OUT, b - 1)

            batches(pe, batch)
            end = Mamba.base(NB - 1, 7) + 1
            heads(UNITS - 1, 1)
            norm(end, end % 4, UNITS - 2)
            norm(end + 1, (end + 1) % 4, UNITS - 1)
            out_project(end + 2, (end + 2) % 4, NB - 1)

        @block.scalar
        def _(act):
            A = act.activation

            def pair(tile, q, p, c, g_slot):
                for j in range(2):
                    act.wait_ge(tile_full, tile + j + 1)
                    ps = pi[(q + j) % 4][:, 0:L]
                    A(xb[:, g_slot, j, 3:L + 3], ps, ACT.Identity, scale=vm[:, ZT + c + j:ZT + c + j + 1],
                      bias=vb[:, ZT + c + j:ZT + c + j + 1])
                    A(acc[:, g_slot, j, :], ps, ACT.Identity, scale=sc3[:, c + j:c + j + 1],
                      bias=bi3[:, c + j:c + j + 1]).then_inc(tile_free, 1)

            def project_pair(tile, q, p, c, slot):
                if not (static(p) and p < 2):
                    act.wait_ge(activated, p - 1)
                pair(tile, q, p, c, slot)

            def silu_x(p, slot, b, g):
                act.wait_ge(convolved, 6 * p + 6)
                u = 8 * b + g
                if not (static(b) and b == 0 and g < 4):
                    act.wait_ge(y_step, 4 * (u - 3))
                A(xs[:, g % 4, :, :], acc[:, slot, :, :], ACT.Silu).then_inc(activated, 1)

            def silu_b(b, p):
                act.wait_ge(convolved, 6 * p + 6)
                if not (static(b) and b == 0):
                    act.wait_ge(cb_done, 8 * b)
                for r in range(4):
                    rows = slice(SD * r, SD * r + SD)
                    ins = A(bz[rows, :, r, :], acc[rows, 0, :, :], ACT.Silu)
                ins.then_inc(activated, 1)

            def silu_c(p):
                act.wait_ge(convolved, 6 * p + 12)
                A(cs[:, :, :], acc[:, 1, :, :], ACT.Silu).then_inc(activated, 1)

            def gates(tile, q, b, g):
                u = 8 * b + g
                if not (static(b) and b == 0 and g < 4):
                    act.wait_ge(gated, u - 3)
                for j in range(2):
                    act.wait_ge(tile_full, tile + j + 1)
                    c = 2 * g + j
                    A(zs[:, g % 4, j, :], pi[(q + j) % 4][:, 0:L], ACT.Silu, scale=vm[:, c:c + 1],
                      bias=vb[:, c:c + 1]).then_inc(tile_free, 1)

            def pair_x(tile, q, b, g):
                project_pair(tile, q, Mamba.pair(b, g), 2 * g, g % 2)

            def pair_bc(tile, q, b, j):
                project_pair(tile + 2 * j, q + 2 * j, 10 * b + j, ZT + 2 * j, j)

            def deviation(tile, q, n):
                act.wait_ge(tile_full, tile + 1)
                if not (static(n) and n == 0):
                    act.wait_ge(rs_done, n)
                A(sd[:, :], pi[q % 4][:, 0:L], ACT.Sqrt, bias=eps[:, 0:1]).then_inc(tile_free, 1)

            def square(n, s, norm_tile):
                act.wait_ge(gated, n + 1)
                if norm_tile is not None:
                    act.wait_ge(tile_full, norm_tile + 1)
                A(sq[:, :, :], yg[:, s, :, :], ACT.Square).then_inc(squared, 1)

            def high(n, s, g):
                act.wait_ge(normed, n + 1)
                A(yn_hi[:, 2 * g:2 * g + 2, :], yg[:, s, :, :], ACT.Identity).then_inc(hi_done, 1)

            def residual(tile, q, b):
                if not (static(b) and b == 0):
                    act.wait_ge(h1_out, 16 * b)
                for j in range(KT):
                    act.wait_ge(tile_full, tile + j + 1)
                    A(h1[:, j, :], pi[(q + j) % 4][:, 0:L], ACT.Identity, scale=1.0 / (X_SCALE * O_SCALE),
                      bias=bo[:, j:j + 1]).then_inc(tile_free, 1)

            act.wait_ge(consts, 8)
            act.wait_ge(setup, 3 + 2)
            pair_bc(0, 0, 0, 0)
            pair_bc(0, 0, 0, 1)
            silu_b(0, 0)
            silu_c(0)
            pair_x(4, 0, 0, 0)
            silu_x(2, 0, 0, 0)
            gates(6, 2, 0, 0)

            def batch(b):
                for g in range(GROUPS):
                    u = 8 * b + g
                    tile, q = Mamba.base(b, g), Mamba.bank(b, g)
                    x, z, nt = Mamba.x(b, g), Mamba.z(b, g), Mamba.norm(b, g)
                    starts, first = Mamba.starts(b, g), static(b) and b == 0 and g == 0
                    out = g == 2 and not (static(b) and b == 0)

                    if g == GROUPS - 1:
                        deviation(tile + nt, q + nt, u - 2)
                        square(u - 1, (g - 1) % 2, tile + nt)
                        if not last(b):
                            pair_bc(tile + 1, q + 1, b + 1, 0)
                        high(u - 2, g % 2, (g - 2) % 8)
                        if not last(b):
                            pair_bc(tile + 1, q + 1, b + 1, 1)
                            silu_b(b + 1, 10 * b + 10)
                            pair_x(tile + x, q + x, b + 1, 0)
                            silu_c(10 * b + 10)
                            silu_x(Mamba.pair(b + 1, 0), 0, b + 1, 0)
                            gates(tile + z, q + z, b + 1, 0)
                    else:
                        pair_x(tile + x, q + x, b, g + 1)
                        if not starts:
                            deviation(tile + nt, q + nt, u - 2)
                        silu_x(Mamba.pair(b, g + 1), (g + 1) % 2, b, g + 1)
                        gates(tile + z, q + z, b, g + 1)
                        if not first:
                            square(u - 1, (g - 1) % 2, None if starts else tile + nt)
                        if not (starts or out):
                            high(u - 2, g % 2, (g - 2) % 8)
                        if out:
                            residual(tile + Mamba.OUT, q + Mamba.OUT, b - 1)
                            high(u - 2, g % 2, (g - 2) % 8)

            batches(act, batch)
            end = Mamba.base(NB - 1, 7) + 1
            deviation(end, end, UNITS - 2)
            square(UNITS - 1, 1, end)
            high(UNITS - 2, 0, 6)
            deviation(end + 1, end + 1, UNITS - 1)
            high(UNITS - 1, 1, 7)
            residual(end + 2, end + 2, NB - 1)

        @block.vector
        def _(dve):
            TT, TS, STT = nc.vector.tensor_tensor, nc.vector.tensor_scalar, nc.vector.scalar_tensor_tensor
            nc.vector.memset(xb[:, :, :, 0:3], 0.0).then_inc(consts, 1)
            nc.vector.memset(ones[:, :], 1.0).then_inc(consts, 1)
            nc.vector.memset(ones_g[:, :], float(GROUPS) / DS / X_SCALE ** 2).then_inc(consts, 1)
            nc.vector.memset(eps[:, :], EPS / X_SCALE ** 2).then_inc(consts, 1)
            for r in range(4):
                nc.vector.memset(bz[:, :, r, :], 0.0).then_inc(consts, 1)
            dve.wait_ge(small_in, 16 * 6)
            TT(vb[:, :], vb[:, :], vm[:, :], ALU.mult).then_inc(setup, 1)
            dve.wait_ge(setup, 1)
            TS(vm[:, :], vm[:, :], 1.0 / (X_SCALE * W_SCALE), None, ALU.mult).then_inc(setup, 1)
            dve.wait_ge(setup, 2)
            TT(sc3[:, :], vm[:, ZT:], cw[:, :, 3], ALU.mult).then_inc(setup, 1)
            TT(bi3[:, :], vb[:, ZT:], cw[:, :, 3], ALU.mult).then_inc(setup, 1)
            dve.wait_ge(setup, 4)
            TT(bi3[:, :], bi3[:, :], cb[:, :], ALU.add).then_inc(setup, 1)

            def convolve(p, slot, c, tile):
                dve.wait_ge(tile_free, tile + 2)
                for k in (2, 1, 0):
                    for j in range(2):
                        if k < 2:
                            dve.wait_ge(convolved, 6 * p + 2 * (1 - k) + j + 1)
                        STT(out=acc[:, slot, j, :], in0=xb[:, slot, j, k:k + L], scalar=cw[:, c + j, k:k + 1],
                            in1=acc[:, slot, j, :], op0=ALU.mult, op1=ALU.add).then_inc(convolved, 1)

            def tokens(n, s, b, g):
                dve.wait_ge(transposed, n + 1)
                if not (static(n) and n < 2):
                    dve.wait_ge(heads_done, n - 1)
                dt = keep["dt_tok"][:, :, b, GH * g:GH * g + GH]
                TT(xt[:, s, :, :].rearrange("p m (h f) -> p m h f", h=GH),
                   pt[:, :, :].rearrange("p m (h f) -> p m h f", h=GH), bcast(dt, 3, HD), ALU.mult).then_inc(xt_done, 1)

            def scan(n, s, count):
                dve.wait_ge(dec_in[s], count)
                if not (static(n) and n < 2):
                    dve.wait_ge(heads_done, n - 1)
                for h in range(GH):
                    nc.vector.tensor_tensor_scan(dec1[:, s, h, :], dec[:, s, h, P:L], ident[:, 0:L1], 0.0,
                                                 ALU.mult, ALU.add).then_inc(scanned, 1)
                dve.wait_ge(scanned, 8 * n + 4)
                for h in range(GH):
                    nc.vector.tensor_tensor_scan(dec[:, s, h, :], dec[:, s, h, :], ident[:, :], 0.0,
                                                 ALU.mult, ALU.add).then_inc(scanned, 1)

            def weigh(n, s):
                dve.wait_ge(cb_done, n + 1)
                dve.wait_ge(scanned, 8 * n + 8)
                TT(dec1[:, s, :, :], dec1[:, s, :, :], bcast(pg[:, L:L + L1], 1, GH), ALU.mult).then_inc(weighted, 1)
                TT(dec[:, s, :, :], dec[:, s, :, :], bcast(pg[:, 0:L], 1, GH), ALU.mult).then_inc(weighted, 1)

            def tail_products(b):
                dve.wait_ge(activated, 10 * b + 2)
                if not (static(b) and b == 0):
                    dve.wait_ge(cb_done, 8 * b)
                TT(tailp[:, :, :], bz[:, :, :, L - 1], bcast(cs[:, :, L - 1], 2, 4), ALU.mult).then_inc(tailp_done, 1)

            def tail_weights(b):
                if not (static(b) and b == 0):
                    dve.wait_ge(y_step, 32 * b)
                for hh in range(2):
                    rows = slice(HD * hh, HD * hh + HD)
                    dt = keep["dt_tail"][rows, b, :].rearrange("p (g q e) -> p g q e", q=2, e=2)[:, :, :, hh]
                    TT(tailw[rows, :, :], dt, bcast(pg[rows, 400:408], 2, 2), ALU.mult).then_inc(tailw_done, 1)

            def output(n, s, g, b1):
                dve.wait_ge(heads_done, n + 1)
                dve.wait_ge(tailw_done, 2 * b1)
                if not (static(n) and n < 2):
                    dve.wait_ge(lo_done, n - 1)
                    dve.wait_ge(hi_done, n - 1)
                for j in range(2):
                    c = 2 * g + j
                    STT(out=yg[:, s, j, :], in0=xs[:, g % 4, j, :], scalar=dp[:, c:c + 1], in1=py[j][:, 0:L],
                        op0=ALU.mult, op1=ALU.add).then_inc(y_step, 1)
                for j in range(2):
                    dve.wait_ge(y_step, 4 * n + j + 1)
                    col = yg[:, s, j, L - 1:L]
                    STT(out=col, in0=xs[:, g % 4, j, L - 1:L], scalar=tailw[:, g, j:j + 1], in1=col,
                        op0=ALU.mult, op1=ALU.add).then_inc(y_step, 1)

            def invert(n, tile):
                dve.wait_ge(tile_free, tile + 1)
                if not (static(n) and n == 0):
                    dve.wait_ge(normed, n)
                nc.vector.reciprocal(rs[:, :], sd[:, :]).then_inc(rs_done, 1)

            dve.wait_ge(consts, 8)
            convolve(0, 0, ZT, 0)
            convolve(1, 1, ZT + 2, 2)
            convolve(2, 0, 0, 4)
            scan(0, 0, 16)

            def batch(b):
                for g in range(GROUPS):
                    u = 8 * b + g
                    if g == 0:
                        tail_products(b)
                    tokens(u, g % 2, b, g)
                    weigh(u, g % 2)
                    tile, nt = Mamba.base(b, g), Mamba.norm(b, g)
                    if g < GROUPS - 1:
                        convolve(Mamba.pair(b, g + 1), (g + 1) % 2, 2 * (g + 1), tile)
                    if not (static(b) and b == 0 and g == 0):
                        output(u - 1, (g - 1) % 2, (g - 1) % 8, b if g == 0 else b + 1)
                    if not Mamba.starts(b, g):
                        invert(u - 2, tile + nt)
                    if g == 0:
                        tail_weights(b)
                    if g == GROUPS - 1 and not last(b):
                        p = 10 * b + 10
                        convolve(p, 0, ZT, tile + 1)
                        convolve(p + 1, 1, ZT + 2, tile + 3)
                        convolve(p + 2, 0, 0, tile + Mamba.x(b, g))
                    if not (last(b) and g == GROUPS - 1):
                        scan(u + 1, (g + 1) % 2, 16 * (4 * b + (g + 1) // 2 + 1))

            batches(dve, batch)
            end = Mamba.base(NB - 1, 7) + 1
            output(UNITS - 1, 1, 7, NB)
            invert(UNITS - 2, end)
            invert(UNITS - 1, end + 1)

        @block.gpsimd
        def _(pool):
            TT = nc.gpsimd.tensor_tensor

            def gate(n, s, g):
                pool.wait_ge(y_step, 4 * n + 4)
                TT(yg[:, s, :, :], yg[:, s, :, :], zs[:, g % 4, :, :], ALU.mult).then_inc(gated, 1)

            def normalise(n, s):
                pool.wait_ge(rs_done, n + 1)
                pool.wait_ge(squared, n + 1)
                TT(yg[:, s, :, :], yg[:, s, :, :], bcast(rs[:, :], 1, 2), ALU.mult).then_inc(normed, 1)

            def low(n, s, g):
                pool.wait_ge(hi_done, n + 1)
                TT(yn_lo[:, 2 * g:2 * g + 2, :], yg[:, s, :, :], yn_hi[:, 2 * g:2 * g + 2, :],
                   ALU.subtract).then_inc(lo_done, 1)

            def add_residual(b, tile):
                pool.wait_ge(tile_free, tile + KT)
                pool.wait_ge(h_in, 16 * (b + 1))
                TT(h1[:, :, :], h1[:, :, :], hb[:, :, :], ALU.add).then_inc(h1_done, 1)

            def sum_tiles(b, j, tiles, before):
                pool.wait_ge(piece_in[j], 16 * b + 16)
                if not (static(b) and b == 0 and before == 0):
                    pool.wait_ge(piece_step, 16 * b + before)
                bufs = [rot_in[:, j % 2, :], rot_mid[:, :]]
                for level in range(tiles.bit_length() - 1):
                    src, dst = (x.rearrange("p (a two b) -> p a two b", two=2, b=(1 << level) * PIECE // tiles)
                                for x in (bufs[level % 2], bufs[1 - level % 2]))
                    TT(dst[:, :, 0, :], src[:, :, 0, :], src[:, :, 1, :], ALU.add).then_inc(piece_step, 1)
                    TT(dst[:, :, 1, :], src[:, :, 0, :], src[:, :, 1, :], ALU.subtract).then_inc(piece_step, 1)
                    before += 2
                    pool.wait_ge(piece_step, 16 * b + before)

            def batch(b):
                for g in range(GROUPS):
                    u = 8 * b + g
                    if not (static(b) and b == 0 and g == 0):
                        gate(u - 1, (g - 1) % 2, (g - 1) % 8)
                    if not Mamba.starts(b, g):
                        normalise(u - 2, g % 2)
                    if g == 2:
                        sum_tiles(b, 0, IT, 0)
                        sum_tiles(b, 1, KT, 8)
                    if g == 2 and not (static(b) and b == 0):
                        add_residual(b - 1, Mamba.base(b, g) + Mamba.OUT)
                    if not Mamba.starts(b, g):
                        low(u - 2, g % 2, (g - 2) % 8)
                    if g == 5:
                        sum_tiles(b, 2, KT, 12)

            batches(pool, batch)
            end = Mamba.base(NB - 1, 7) + 1
            gate(UNITS - 1, 1, 7)
            normalise(UNITS - 2, 0)
            low(UNITS - 2, 0, 6)
            normalise(UNITS - 1, 1)
            low(UNITS - 1, 1, 7)
            add_residual(NB - 1, end + 2)


def rotate_phase(nc, t, scratch, ffn):
    with ExitStack() as ctx:
        def sb(name, shape, dt=F32):
            return ctx.enter_context(nc.sbuf_tensor(name, shape, dt))

        def sem(name):
            return ctx.enter_context(nc.semaphore("r_" + name))

        SLOTS = 4
        NU, ND = 2 * NB // 4, NB // 4
        had = sb("r_had", [P, P])
        wst = sb("r_wst", [P, SLOTS, 4, PIECE])
        su, sd = sb("r_su", [P, KT]), sb("r_sd", [P, IT])
        ps = [ctx.enter_context(nc.psum_tensor(f"r_ps{i}", [P, 512], F32)) for i in range(8)]
        small_in, scales = sem("small_in"), sem("scales")
        w_in = [sem(f"w_in{i}") for i in range(SLOTS)]
        rotated, hi_done, lo_done = sem("rotated"), sem("hi_done"), sem("lo_done")
        block = ctx.enter_context(nc.Block())
        turns = [("ug", c) for c in range(NU)] + [("down", c) for c in range(ND)]

        @block.sync
        def _(sp):
            for dst, src in ((had, "hadamard"), (su, "SU_ug"), (sd, "SU_dp"),
                             (ffn["ws_ug"], "Wscale_ug"), (ffn["ws_dp"], "Wscale_dp")):
                sp.dma_start(dst[:, :], t[src]).then_inc(small_in, 16)
            for n, (kind, c) in enumerate(turns):
                if n >= SLOTS:
                    sp.wait_ge(rotated, 4 * (n - SLOTS + 1))
                sp.dma_start(wst[:, n % SLOTS, :, :], scratch[kind + "_sum"][4 * c:4 * c + 4]
                             .rearrange("c p n -> p c n")).then_inc(w_in[n % SLOTS], 16)

        def target(n, q, which):
            kind, c = turns[n]
            bank = ps[4 * (n % 2) + q]
            if kind == "ug":
                return [(ffn["ug_" + which][:, q, 4 * c * UCOLS:4 * (c + 1) * UCOLS], bank[:, :], su[:, q:q + 1])]
            v = bank[:, :].rearrange("p (c k n) -> p c k n", c=4, k=4)
            return [(ffn["d_" + which][:, 4 * q + j, 4 * c * DCOLS:4 * (c + 1) * DCOLS].rearrange("p (c n) -> p c n", c=4),
                     v[:, :, j, :], sd[:, 4 * q + j:4 * q + j + 1]) for j in range(4)]

        @block.vector
        def _(dve):
            TS = nc.vector.tensor_scalar
            dve.wait_ge(small_in, 16 * 5)
            TS(su[:, :], su[:, :], W_SCALE / float(np.sqrt(D)), None, ALU.mult).then_inc(scales, 1)
            TS(sd[:, :], sd[:, :], W_SCALE / float(np.sqrt(INTER)), None, ALU.mult).then_inc(scales, 1)
            TS(ffn["ws_ug"][:, :], ffn["ws_ug"][:, :], 1.0 / (X_SCALE * W_SCALE), None, ALU.mult).then_inc(scales, 1)
            TS(ffn["ws_dp"][:, :], ffn["ws_dp"][:, :], 1.0 / W_SCALE, None, ALU.mult).then_inc(scales, 1)
            dve.wait_ge(scales, 4)
            for n in range(len(turns)):
                for q in range(4):
                    dve.wait_ge(hi_done, 4 * n + q + 1)
                    for (lo, src, scale), (hi, _, _) in zip(target(n, q, "lo"), target(n, q, "hi")):
                        ins = nc.vector.scalar_tensor_tensor(out=lo, in0=src, scalar=scale, in1=hi,
                                                             op0=ALU.mult, op1=ALU.subtract)
                    ins.then_inc(lo_done, 1)

        @block.scalar
        def _(act):
            act.wait_ge(scales, 4)
            for n in range(len(turns)):
                for q in range(4):
                    act.wait_ge(rotated, 4 * n + q + 1)
                    for hi, src, scale in target(n, q, "hi"):
                        ins = act.activation(hi, src, ACT.Identity, scale=scale)
                    ins.then_inc(hi_done, 1)

        @block.tensor
        def _(pe):
            pe.wait_ge(small_in, 16 * 5)
            for n, (kind, c) in enumerate(turns):
                s = n % SLOTS
                pe.wait_ge(w_in[s], 16 * (n // SLOTS + 1))
                for q in range(4):
                    if n >= 2:
                        pe.wait_ge(lo_done, 4 * (n - 2) + q + 1)
                    width = (UCOLS if kind == "ug" else 4 * DCOLS)
                    nc.tensor.matmul(ps[4 * (n % 2) + q][:, :], had[:, :], wst[:, s, :, width * q:width * (q + 1)],
                                     start=True, stop=True).then_inc(rotated, 1)


def ffn_phase(nc, t, scratch, keep, ffn, out):
    with ExitStack() as ctx:
        def sb(name, shape, dt=F32):
            return ctx.enter_context(nc.sbuf_tensor(name, shape, dt))

        def sem(name):
            return ctx.enter_context(nc.semaphore("f_" + name))

        h1 = sb("f_h1", [P, 2, KT, L])
        xc, sq = sb("f_xc", [P, KT, L]), sb("f_sq", [P, KT, L])
        sd, rs = sb("f_sd", [P, L]), sb("f_rs", [P, L])
        x2 = sb("f_x2", [P, 2, KT, L], F16)
        sg = sb("f_sg", [P, 2, L])
        mid = sb("f_mid", [P, 2, L])
        m_hi, m_lo = sb("f_m_hi", [P, IT, L], F16), sb("f_m_lo", [P, IT, L], F16)
        o = sb("f_o", [P, KT, L])
        eps = sb("f_eps", [P, 1])
        ws_ug, ws_dp = ffn["ws_ug"], ffn["ws_dp"]
        pu = [ctx.enter_context(nc.psum_tensor(f"f_pu{i}", [P, 512], F32)) for i in range(2)]
        pgt = [ctx.enter_context(nc.psum_tensor(f"f_pg{i}", [P, 512], F32)) for i in range(2)]
        pd = [ctx.enter_context(nc.psum_tensor(f"f_pd{i}", [P, 512], F32)) for i in range(2)]
        pm = ctx.enter_context(nc.psum_tensor("f_pm", [P, 512], F32))
        pv = ctx.enter_context(nc.psum_tensor("f_pv", [P, 512], F32))
        consts = sem("consts")
        h1_in = [sem(f"h1_in{i}") for i in range(2)]
        mean_done, centered, squared, var_done, sd_done, rs_done, normed = (sem(x) for x in (
            "mean_done", "centered", "squared", "var_done", "sd_done", "rs_done", "normed"))
        x_hi, x_lo = sem("x_hi"), sem("x_lo")
        gate_mm, up_mm, gate_act, product, mid_hi, mid_lo = (sem(x) for x in (
            "gate_mm", "up_mm", "gate_act", "product", "mid_hi", "mid_lo"))
        down_mm, summed, stored = sem("down_mm"), sem("summed"), sem("stored")
        block = ctx.enter_context(nc.Block())
        AT_MEAN, AT_VAR = 3, 7

        def pairs(eng, body):
            body(0, 0)
            body(1, 1)
            with eng.Fori(1, NB // 2 - 1) as i:
                body(2 * i, 0)
                body(2 * i + 1, 1)
            body(NB - 2, 0)
            body(NB - 1, 1)

        def more(b):
            return not (static(b) and b == NB - 1)

        @block.sync
        def _(sp):
            sp.dma_start(h1[:, 0, :, :], scratch["h1"][0]).then_inc(h1_in[0], 16)

            def batch(b, s):
                if more(b):
                    if not (static(b) and b == 0):
                        sp.wait_ge(summed, 4 * b)
                    sp.dma_start(h1[:, 1 - s, :, :], scratch["h1"][b + 1]).then_inc(h1_in[1 - s], 16)
                sp.wait_ge(summed, 4 * b + 4)
                sp.dma_start(out[b], o[:, :, :]).then_inc(stored, 16)

            pairs(sp, batch)
            sp.wait_ge(stored, 16 * NB)

        @block.tensor
        def _(pe):
            ones = keep["ones_d"]

            def moments(dst, src, ins_sem):
                for k in range(KT):
                    ins = nc.tensor.matmul(dst[:, 0:L], ones[:, :], src[:, k, :], start=k == 0, stop=k == KT - 1)
                ins.then_inc(ins_sem, 1)

            def mean(n, s):
                pe.wait_ge(h1_in[s], (n - s) * 8 + 16)
                if not (static(n) and n == 0):
                    pe.wait_ge(centered, n)
                moments(pm, h1[:, s, :, :], mean_done)

            def var(n):
                pe.wait_ge(squared, n + 1)
                if not (static(n) and n == 0):
                    pe.wait_ge(sd_done, n)
                moments(pv, sq, var_done)

            def split_mm(dst, k_tiles, w_hi, w_lo, x_hi, x_lo, done):
                for k in range(k_tiles):
                    for m, (w, x) in enumerate(((w_hi, x_hi), (w_hi, x_lo), (w_lo, x_hi))):
                        ins = nc.tensor.matmul(dst, w(k), x(k), start=k == 0 and m == 0,
                                               stop=k == k_tiles - 1 and m == 2)
                ins.then_inc(done, 1)

            def wide(dst, col, done):
                cols = slice(col, col + P)
                split_mm(dst[:, 0:L], KT, lambda k: ffn["ug_hi"][:, k, cols], lambda k: ffn["ug_lo"][:, k, cols],
                         lambda k: x2[:, 0, k, :], lambda k: x2[:, 1, k, :], done)

            pe.wait_ge(consts, 1)
            mean(0, 0)
            var(0)

            def batch(b, s):
                pe.wait_ge(x_lo, b + 1)
                pe.wait_ge(x_hi, b + 1)
                for j in range(IT):
                    n = 16 * b + j
                    if not (static(b) and b == 0 and j < 2):
                        pe.wait_ge(gate_act, n - 1)
                    wide(pgt[j % 2], INTER + j * P, gate_mm)
                    if not (static(b) and b == 0 and j < 2):
                        pe.wait_ge(product, n - 1)
                    wide(pu[j % 2], j * P, up_mm)
                    if more(b) and j == AT_MEAN:
                        mean(b + 1, 1 - s)
                    if more(b) and j == AT_VAR:
                        var(b + 1)
                for j in range(KT):
                    if not (static(b) and b == 0 and j < 2):
                        pe.wait_ge(summed, 4 * b + j - 1)
                    cols = slice(j * P, j * P + P)
                    if j == 0:
                        pe.wait_ge(mid_lo, 16 * b + 14)
                        pe.wait_ge(mid_hi, 16 * b + 14)
                    for k in range(IT):
                        if j == 0 and k >= 14:
                            pe.wait_ge(mid_lo, 16 * b + k + 1)
                            pe.wait_ge(mid_hi, 16 * b + k + 1)
                        for m, (w, x) in enumerate((("d_hi", m_hi), ("d_hi", m_lo), ("d_lo", m_hi))):
                            ins = nc.tensor.matmul(pd[j % 2][:, 0:L], ffn[w][:, k, cols], x[:, k, :],
                                                   start=k == 0 and m == 0, stop=k == IT - 1 and m == 2)
                    ins.then_inc(down_mm, 1)

            pairs(pe, batch)

        @block.scalar
        def _(act):
            A = act.activation

            def square(n):
                act.wait_ge(centered, n + 1)
                if not (static(n) and n == 0):
                    act.wait_ge(var_done, n)
                A(sq[:, :, :], xc[:, :, :], ACT.Square).then_inc(squared, 1)

            def deviation(n):
                act.wait_ge(var_done, n + 1)
                if not (static(n) and n == 0):
                    act.wait_ge(rs_done, n)
                A(sd[:, :], pv[:, 0:L], ACT.Sqrt, bias=eps[:, 0:1]).then_inc(sd_done, 1)

            def high(n, mm):
                act.wait_ge(normed, n + 1)
                if mm is not None:
                    act.wait_ge(up_mm, mm)
                A(x2[:, 0, :, :], xc[:, :, :], ACT.Identity).then_inc(x_hi, 1)

            act.wait_ge(consts, 1)
            square(0)
            deviation(0)
            high(0, None)

            def mid_high(n, j):
                act.wait_ge(product, n + 1)
                A(m_hi[:, j, :], mid[:, j % 2, :], ACT.Identity).then_inc(mid_hi, 1)

            def batch(b, s):
                for j in range(IT):
                    n = 16 * b + j
                    act.wait_ge(gate_mm, n + 1)
                    if not (static(b) and b == 0 and j < 2):
                        act.wait_ge(product, n - 1)
                    A(sg[:, j % 2, :], pgt[j % 2][:, 0:L], ACT.Silu, scale=ws_ug[:, IT + j:IT + j + 1]).then_inc(gate_act, 1)
                    if j == 0 and not (static(b) and b == 0):
                        act.wait_ge(down_mm, 4 * b)
                    if j:
                        mid_high(n - 1, j - 1)
                    if more(b) and j == AT_MEAN + 1:
                        square(b + 1)
                    if more(b) and j == AT_VAR + 1:
                        deviation(b + 1)
                mid_high(16 * b + IT - 1, IT - 1)
                if more(b):
                    high(b + 1, 16 * b + 16)

            pairs(act, batch)

        @block.vector
        def _(dve):
            TT, STT = nc.vector.tensor_tensor, nc.vector.scalar_tensor_tensor
            nc.vector.memset(eps[:, :], EPS).then_inc(consts, 1)

            def center(n, s):
                dve.wait_ge(mean_done, n + 1)
                if not (static(n) and n == 0):
                    dve.wait_ge(x_lo, n)
                    dve.wait_ge(x_hi, n)
                TT(xc[:, :, :], h1[:, s, :, :], bcast(pm[:, 0:L], 1, KT), ALU.subtract).then_inc(centered, 1)

            def normalise(n):
                dve.wait_ge(sd_done, n + 1)
                if not (static(n) and n == 0):
                    dve.wait_ge(normed, n)
                nc.vector.reciprocal(rs[:, :], sd[:, :]).then_inc(rs_done, 1)
                dve.wait_ge(rs_done, n + 1)
                dve.wait_ge(squared, n + 1)
                STT(out=xc[:, :, :], in0=xc[:, :, :], scalar=X_SCALE, in1=bcast(rs[:, :], 1, KT),
                    op0=ALU.mult, op1=ALU.mult).then_inc(normed, 1)

            dve.wait_ge(consts, 1)
            center(0, 0)
            normalise(0)

            def mid_low(n, j):
                dve.wait_ge(mid_hi, n + 1)
                TT(m_lo[:, j, :], mid[:, j % 2, :], m_hi[:, j, :], ALU.subtract).then_inc(mid_lo, 1)

            def batch(b, s):
                for j in range(IT):
                    n = 16 * b + j
                    dve.wait_ge(up_mm, n + 1)
                    dve.wait_ge(gate_act, n + 1)
                    if not (static(b) and b == 0 and j < 2):
                        dve.wait_ge(mid_lo, n - 1)
                    STT(out=mid[:, j % 2, :], in0=pu[j % 2][:, 0:L], scalar=ws_ug[:, j:j + 1], in1=sg[:, j % 2, :],
                        op0=ALU.mult, op1=ALU.mult).then_inc(product, 1)
                    if j:
                        mid_low(n - 1, j - 1)
                    if more(b) and j == AT_MEAN:
                        center(b + 1, 1 - s)
                    if more(b) and j == AT_VAR + 1:
                        normalise(b + 1)
                mid_low(16 * b + IT - 1, IT - 1)
                for j in range(KT):
                    dve.wait_ge(down_mm, 4 * b + j + 1)
                    if j == 0 and not (static(b) and b == 0):
                        dve.wait_ge(stored, 16 * b)
                    STT(out=o[:, j, :], in0=pd[j % 2][:, 0:L], scalar=ws_dp[:, j:j + 1], in1=h1[:, s, j, :],
                        op0=ALU.mult, op1=ALU.add).then_inc(summed, 1)

            pairs(dve, batch)

        @block.gpsimd
        def _(pool):
            def low(n):
                pool.wait_ge(x_hi, n + 1)
                nc.gpsimd.tensor_tensor(x2[:, 1, :, :], xc[:, :, :], x2[:, 0, :, :], ALU.subtract).then_inc(x_lo, 1)

            low(0)
            with pool.Fori(1, NB) as n:
                low(n)


def build(nc, t, out):
    def scr(name, shape, dt=F32):
        return nc.dram_tensor(f"scratch_{name}", shape, dt, kind="Internal").ap()

    scratch = {"h": scr("h", (NB, P, KT, L)), "xn": scr("xn", (NB, P, 2, KT, L), F16),
               "a": scr("a", (NB, HEADS, L)), "dt_tail": scr("dt_tail", (NB, HEADS, 1)),
               "h1": scr("h1", (NB, P, KT, L)),
               "ug_sum": scr("ug_sum", (2 * NB, P, PIECE)), "down_sum": scr("down_sum", (NB, P, PIECE))}
    s4_phase(nc, t, scratch)
    with ExitStack() as ctx:
        def sb(name, shape, dt=F32):
            return ctx.enter_context(nc.sbuf_tensor(name, shape, dt))

        keep = {"ident": sb("ident", [P, L]), "ones_d": sb("ones_d", [P, P])}
        with ExitStack() as inner:
            def sbi(name, shape, dt=F32):
                return inner.enter_context(nc.sbuf_tensor(name, shape, dt))

            keep |= {"dt_tok": sbi("dt_tok", [P, 2, NB, HEADS]), "dt_tail": sbi("dt_tail", [P, NB, HEADS]),
                     "w_hi": sbi("w_hi", [P, KT, P * PT], F16), "w_lo": sbi("w_lo", [P, KT, P * PT], F16),
                     "o_hi": sbi("o_hi", [P, ZT, D], F16), "o_lo": sbi("o_lo", [P, ZT, D], F16)}
            with nc.sbuf_tensor("a_keep", [P, 4, L], F32) as a_keep:
                keep["a"] = a_keep
                prep_phase(nc, t, scratch, keep)
            mamba_phase(nc, t, scratch, keep)
        with ExitStack() as inner:
            def sbi(name, shape, dt=F32):
                return inner.enter_context(nc.sbuf_tensor(name, shape, dt))

            ffn = {"ug_hi": sbi("ug_hi", [P, KT, 2 * INTER], F16), "ug_lo": sbi("ug_lo", [P, KT, 2 * INTER], F16),
                   "d_hi": sbi("d_hi", [P, IT, D], F16), "d_lo": sbi("d_lo", [P, IT, D], F16),
                   "ws_ug": sbi("ws_ug", [P, 2 * IT]), "ws_dp": sbi("ws_dp", [P, KT])}
            rotate_phase(nc, t, scratch, ffn)
            ffn_phase(nc, t, scratch, keep, ffn, out)


def _hadamard(n):
    h = np.ones((1, 1), np.float32)
    while h.shape[0] < n:
        h = np.block([[h, h], [h, -h]])
    return h.astype(np.float32)


def _tiles(v):
    return np.ascontiguousarray(v.reshape(-1, P).T)


def _pieces(w, cols):
    w = w.reshape(-1, P, w.shape[1] // cols, cols).transpose(2, 1, 0, 3)
    return np.ascontiguousarray(w).reshape(-1, P, PIECE)


def layout(i):
    w_in, mup = i["L0_attn_W_in"], i["L0_attn_mup_vector"]
    b_in, n = i["L0_attn_b_in"], P * PT
    return {
        "C": np.ascontiguousarray(i["x"].transpose(3, 2, 1, 0)).reshape(P, NH, NB),
        "cls": _tiles(i["cls_tok"].reshape(-1)),
        "log_dt": i["L0_tok_log_dt"],
        "B_re": np.ascontiguousarray(i["L0_tok_B_ri"][..., 0].T),
        "B_im": np.ascontiguousarray(i["L0_tok_B_ri"][..., 1].T),
        "inv_A_real": np.ascontiguousarray(i["L0_tok_inv_A_real"].T),
        "A_imag": np.ascontiguousarray(i["L0_tok_A_imag"].T),
        "W_in": w_in,
        "b_in": _tiles(b_in[:n]),
        "mup": _tiles(mup[:n]),
        "dt_vec": np.ascontiguousarray(np.stack(
            [np.tile(v, P // HEADS) for v in (b_in[n:], mup[n:], i["L0_attn_dt_bias"], i["L0_attn_A_log"])], 1)),
        "conv_w": np.ascontiguousarray(i["L0_attn_conv_w"].reshape(CT, P, 4).transpose(1, 0, 2)),
        "conv_b": _tiles(i["L0_attn_conv_b"]),
        "D": _tiles(np.repeat(i["L0_attn_D_param"], HD)),
        "norm_w": _tiles(i["L0_attn_norm_w"]),
        "W_out": i["L0_attn_W_out"],
        "b_out": _tiles(i["L0_attn_b_out"]),
        "SU_ug": _tiles(i["L0_ffn_SU_ug"]),
        "SU_dp": _tiles(i["L0_ffn_SU_dp"]),
        "Wscale_ug": _tiles(i["L0_ffn_Wscale_ug"]),
        "Wscale_dp": _tiles(i["L0_ffn_Wscale_dp"]),
        "W_ug": _pieces(np.concatenate([i["L0_ffn_W_up"], i["L0_ffn_W_gate"]]).T, UCOLS),
        "W_down": _pieces(i["L0_ffn_W_down"].T, DCOLS),
        "hadamard": _hadamard(P),
        "ident": np.eye(P, L, dtype=np.float32),
    }


def kernel(**inputs):
    import concourse.bacc as bacc
    from concourse.bass_utils import run_bass_kernel_spmd

    arrays = {f"in_{k}": np.ascontiguousarray(v)
              for k, v in layout({k: np.asarray(v) for k, v in inputs.items()}).items()}
    nc = bacc.Bacc("TRN2", target_bir_lowering=False, num_devices=1)
    t = {k[3:]: nc.dram_tensor(k, a.shape, F32, kind="ExternalInput").ap() for k, a in arrays.items()}
    out = nc.dram_tensor("out", (NB, P, KT, L), F32, kind="ExternalOutput").ap()
    build(nc, t, out)
    r = run_bass_kernel_spmd(nc, [arrays], core_ids=[0])
    got = r.results[0]["out"]
    return np.ascontiguousarray(got.transpose(0, 3, 2, 1)).reshape(NB, L, D)
```

```python
from contextlib import ExitStack

import numpy as np

import concourse.bass as bass
from concourse import mybir

F32 = mybir.dt.float32
F16 = mybir.dt.float16
ALU = mybir.AluOpType
ACT = mybir.ActivationFunctionType

P = 128
NB = 16
NH = 256
NS = 64
D = 512
L = NH + 1
KT = D // P
HEADS = 32
HD = 64
GROUPS = 8
GH = HEADS // GROUPS
SD = 32
DS = HEADS * HD
ZT = DS // P
CT = (DS + 2 * GROUPS * SD) // P
PT = ZT + CT
PROJ = 2 * DS + 2 * GROUPS * SD + HEADS
INTER = 2048
IT = INTER // P
EPS = 1e-5
UNITS = NB * GROUPS

X_SCALE = 16.0
W_SCALE = 256.0
O_SCALE = 16.0

UCOLS = 2 * INTER // (2 * NB)
DCOLS = D // NB
PIECE = KT * UCOLS
assert PIECE == IT * DCOLS

HC = 8
CHUNKS = NH // HC


class Link:

    def __init__(self, eng, sem):
        self.eng, self.sem, self.n = eng, sem, 0

    def __call__(self, ins):
        ins.then_inc(self.sem, 1)
        self.n += 1
        self.eng.wait_ge(self.sem, self.n)


def bcast(ap, axis, n):
    u = ap.unsqueeze(axis)
    shape = list(u.shape)
    shape[axis] = n
    return u.broadcast_to(shape)


def static(v):
    return isinstance(v, int)


def peeled(eng, first, stop, body):
    body(first)
    with eng.Fori(first + 1, stop) as i:
        body(i)


def s4_phase(nc, t, scratch):
    with ExitStack() as ctx:
        def sb(name, shape, dt=F32):
            return ctx.enter_context(nc.sbuf_tensor(name, shape, dt))

        def sem(name):
            return ctx.enter_context(nc.semaphore(name))

        inv, aim, bre, bim, ldt = (sb(n, [P, NH]) for n in ("s4_inv", "s4_aim", "s4_bre", "s4_bim", "s4_ldt"))
        cp = sb("s4_cp", [P, NH, NB])
        cq = sb("s4_cq", [P, NH, NB])
        tmp = [sb(f"s4_tmp{i}", [P, NH]) for i in range(6)]
        er, ei = sb("s4_er", [P, 9, NH]), sb("s4_ei", [P, 9, NH])
        xj, yj = sb("s4_xj", [P, 16, NH]), sb("s4_yj", [P, 16, NH])
        cr, ci = sb("s4_cr", [P, 8, NH]), sb("s4_ci", [P, 8, NH])
        gr, gi = sb("s4_gr", [P, 4, NH]), sb("s4_gi", [P, 4, NH])
        sgn = sb("s4_sgn", [P, 3])
        v = sb("s4_v", [P, 2, HC, P])
        vt = sb("s4_vt", [P, 2, HC, P])
        big, big_pool = (x[:, :, :, :].rearrange("p s h l -> p (s h l)") for x in (v, vt))
        uu = sb("s4_u", [P, 2, HC, 64])
        ut = sb("s4_ut", [P, 2, HC, 64])
        cls = sb("s4_cls", [P, KT])
        ht = sb("s4_ht", [P, KT, NB, L])
        ps = [ctx.enter_context(nc.psum_tensor(f"s4_ps{i}", [P, 8, 4, NB], F32)) for i in range(2)]

        c_in, loaded, cls_in, stored = sem("s4_c_in"), sem("s4_loaded"), sem("s4_cls_in"), sem("s4_stored")
        exps, chain, params = sem("s4_exps"), sem("s4_chain"), sem("s4_params")
        powers, pool_chain = sem("s4_powers"), sem("s4_pool_chain")
        pool_part, v_step, uv_ready = sem("s4_pool_part"), sem("s4_v_step"), sem("s4_uv_ready")
        mm_done, evac, cls_done = sem("s4_mm_done"), sem("s4_evac"), sem("s4_cls_done")

        def double(link, TT, room, re, im, k, e, conj):
            tb = room[:, 0:k * NH].rearrange("p (k h) -> p k h", k=k)
            c, s = bcast(er[:, e, :], 1, k), bcast(ei[:, e, :], 1, k)
            r0, i0, r1, i1 = re[:, 0:k, :], im[:, 0:k, :], re[:, k:2 * k, :], im[:, k:2 * k, :]
            link(TT(tb, i0, s, ALU.mult))
            link(TT(r1, r0, c, ALU.mult))
            link(TT(r1, r1, tb, ALU.add if conj else ALU.subtract))
            link(TT(tb, r0, s, ALU.mult))
            link(TT(i1, i0, c, ALU.mult))
            link(TT(i1, i1, tb, ALU.subtract if conj else ALU.add))

        block = ctx.enter_context(nc.Block())

        @block.sync
        def _(sp):
            for dst, src in ((inv, t["inv_A_real"]), (aim, t["A_imag"]), (bre, t["B_re"]), (bim, t["B_im"])):
                for h in range(2):
                    sp.dma_start(dst[NS * h:NS * h + NS, :], src).then_inc(loaded, 16)
            sp.dma_start(ldt[:, :], t["log_dt"].partition_broadcast(P)).then_inc(loaded, 16)
            sp.dma_start(cp[:, :, :], t["C"]).then_inc(c_in, 16)
            for h in range(2):
                sp.dma_start(cq[NS * h:NS * h + NS, :, :],
                             t["C"][NS * (1 - h):NS * (1 - h) + NS]).then_inc(c_in, 16)
            sp.dma_start(cls[:, :], t["cls"]).then_inc(cls_in, 16)
            sp.wait_ge(cls_done, 1)
            for part, tokens in enumerate((slice(0, 1 + NH // 2), slice(1 + NH // 2, L))):
                sp.wait_ge(evac, CHUNKS // 2 * (part + 1))
                for b in range(NB):
                    sp.dma_start(scratch["h"][b][:, :, tokens], ht[:, :, b, tokens]).then_inc(stored, 16)
            sp.wait_ge(stored, 16 * 2 * NB)

        @block.scalar
        def _(act):
            act.wait_ge(cls_in, 16)
            act.activation(ht[:, :, :, 0], bcast(cls[:, :], 2, NB), ACT.Identity).then_inc(cls_done, 1)
            act.wait_ge(loaded, 16 * 9)
            act.activation(inv[:, :], inv[:, :], ACT.Exp).then_inc(exps, 1)
            act.activation(ldt[:, :], ldt[:, :], ACT.Exp).then_inc(exps, 1)

            def evacuate(i):
                for s in range(2):
                    act.wait_ge(mm_done, 2 * i + s + 1)
                    act.activation(ht[:, :, :, bass.ds(2 * HC * i + (1 + HC * s), HC)],
                                   ps[s][:, :, :, :].rearrange("p h a c -> p a c h"),
                                   ACT.Identity).then_inc(evac, 1)

            peeled(act, 0, CHUNKS // 2, evacuate)

        @block.vector
        def _(dve):
            link = Link(dve, chain)
            TT, TS, STT = nc.vector.tensor_tensor, nc.vector.tensor_scalar, nc.vector.scalar_tensor_tensor
            link(nc.vector.memset(sgn[:, :], 0.0))
            for half, vals in ((0, (1.0, 0.0, 2.0)), (1, (0.0, 1.0, -2.0))):
                for c, val in enumerate(vals):
                    link(nc.vector.memset(sgn[NS * half:NS * half + NS, c:c + 1], val))
            dve.wait_ge(exps, 2)
            t0, t1, t2, t3, t4, t5 = (x[:, :] for x in tmp)
            dt, a = ldt[:, :], inv[:, :]
            link(TS(t5, dt, 0.5, None, ALU.mult))
            link(STT(out=t0, in0=a, scalar=-1.0, in1=t5, op0=ALU.mult, op1=ALU.mult))
            link(TT(t1, aim[:, :], t5, ALU.mult))
            link(TS(t2, t0, -1.0, 1.0, ALU.mult, ALU.add))
            link(TT(t3, t2, t2, ALU.mult))
            link(TT(t4, t1, t1, ALU.mult))
            link(TT(t3, t3, t4, ALU.add))
            link(nc.vector.reciprocal(t3, t3))
            link(TT(t5, t0, t0, ALU.mult))
            link(TT(t5, t5, t4, ALU.add))
            link(TS(t5, t5, -1.0, 1.0, ALU.mult, ALU.add))
            link(TT(er[:, 0, :], t5, t3, ALU.mult))
            link(STT(out=ei[:, 0, :], in0=t1, scalar=2.0, in1=t3, op0=ALU.mult, op1=ALU.mult))
            link(TT(t3, t3, dt, ALU.mult))
            link(TT(t2, t2, t3, ALU.mult))
            link(TT(t1, t1, t3, ALU.mult))
            link(TT(gr[:, 0, :], bre[:, :], t2, ALU.mult))
            link(TT(t0, bim[:, :], t1, ALU.mult))
            link(TT(gr[:, 0, :], gr[:, 0, :], t0, ALU.subtract))
            link(TT(gi[:, 0, :], bre[:, :], t1, ALU.mult))
            link(TT(t0, bim[:, :], t2, ALU.mult))
            link(TT(gi[:, 0, :], gi[:, 0, :], t0, ALU.add))
            for k in range(8):
                r, i = er[:, k, :], ei[:, k, :]
                link(TT(t0, i, i, ALU.mult))
                link(TT(t1, r, r, ALU.mult))
                link(TT(er[:, k + 1, :], t1, t0, ALU.subtract))
                link(STT(out=ei[:, k + 1, :], in0=r, scalar=2.0, in1=i, op0=ALU.mult, op1=ALU.mult))
                if k == 5:
                    nc.vector.memset(xj[:, 0, :], 0.0).then_inc(powers, 1)

            dve.wait_ge(powers, 1)
            link(nc.vector.memset(yj[:, 0, :], 0.0))
            link(TS(xj[:, 0, :], xj[:, 0, :], sgn[:, 0:1], None, ALU.add))
            link(TS(yj[:, 0, :], yj[:, 0, :], sgn[:, 1:2], None, ALU.add))
            for e in range(4):
                double(link, TT, big, xj, yj, 1 << e, e, True)
            for e in range(2):
                double(link, TT, big, gr, gi, 1 << e, 7 + e, False)
            link(TS(gr[:, :, :], gr[:, :, :], sgn[:, 2:3], None, ALU.mult))
            link(TS(gi[:, :, :], gi[:, :, :], -2.0, None, ALU.mult))
            nc.vector.memset(sgn[:, 0:1], 1.0).then_inc(params, 1)

            def form(i):
                for s in range(2):
                    hs = bass.ds(2 * HC * i + HC * s, HC)
                    n = 2 * i + s
                    c3 = bcast(cr[:, :, hs].rearrange("p i h -> p h i"), 3, 16)
                    x3 = bcast(xj[:, :, hs].rearrange("p j h -> p h j"), 2, 8)
                    if not static(i):
                        dve.wait_ge(mm_done, n - 1)
                    TT(v[:, s, :, :].rearrange("p h (i j) -> p h i j", i=8), c3, x3, ALU.mult).then_inc(v_step, 1)
                    g3 = bcast(gr[:, :, hs].rearrange("p a h -> p h a"), 3, NB)
                    p3 = bcast(cp[:, hs, :], 2, 4)
                    TT(uu[:, s, :, :].rearrange("p h (a c) -> p h a c", a=4), g3, p3, ALU.mult).then_inc(v_step, 1)
                    dve.wait_ge(v_step, 2 * n + 2)
                    dve.wait_ge(pool_part, 2 * n + 2)
                    TT(v[:, s, :, :], v[:, s, :, :], vt[:, s, :, :], ALU.add).then_inc(uv_ready, 1)
                    TT(uu[:, s, :, :], uu[:, s, :, :], ut[:, s, :, :], ALU.add).then_inc(uv_ready, 1)

            dve.wait_ge(pool_chain, 2 + 6 * 3)
            dve.wait_ge(c_in, 16 * 3)
            peeled(dve, 0, CHUNKS // 2, form)

        @block.gpsimd
        def _(pool):
            pool.wait_ge(powers, 1)
            link = Link(pool, pool_chain)
            link(nc.gpsimd.memset(cr[:, 0, :], 1.0))
            link(nc.gpsimd.memset(ci[:, 0, :], 0.0))
            for e in range(3):
                double(link, nc.gpsimd.tensor_tensor, big_pool, cr, ci, 1 << e, 4 + e, False)
            pool.wait_ge(params, 1)
            pool.wait_ge(c_in, 16 * 3)

            def partners(i):
                for s in range(2):
                    hs = bass.ds(2 * HC * i + HC * s, HC)
                    s3 = bcast(ci[:, :, hs].rearrange("p i h -> p h i"), 3, 16)
                    y3 = bcast(yj[:, :, hs].rearrange("p j h -> p h j"), 2, 8)
                    if not static(i):
                        pool.wait_ge(uv_ready, 4 * i + 2 * s - 2)
                    nc.gpsimd.tensor_tensor(vt[:, s, :, :].rearrange("p h (i j) -> p h i j", i=8), s3, y3,
                                            ALU.mult).then_inc(pool_part, 1)
                    g3 = bcast(gi[:, :, hs].rearrange("p a h -> p h a"), 3, NB)
                    q3 = bcast(cq[:, hs, :], 2, 4)
                    nc.gpsimd.tensor_tensor(ut[:, s, :, :].rearrange("p h (a c) -> p h a c", a=4), g3, q3,
                                            ALU.mult).then_inc(pool_part, 1)

            peeled(pool, 0, CHUNKS // 2, partners)

        @block.tensor
        def _(pe):
            def multiply(i):
                for s in range(2):
                    n = 2 * i + s
                    pe.wait_ge(uv_ready, 2 * n + 2)
                    if not static(i):
                        pe.wait_ge(evac, n - 1)
                    for h in range(HC):
                        last = nc.tensor.matmul(ps[s][:, h, :, :], v[:, s, h, :], uu[:, s, h, :],
                                                start=True, stop=True)
                    last.then_inc(mm_done, 1)

            peeled(pe, 0, CHUNKS // 2, multiply)


def prep_phase(nc, t, scratch, keep):
    with ExitStack() as ctx:
        def sb(name, shape, dt=F32):
            return ctx.enter_context(nc.sbuf_tensor(name, shape, dt))

        def sem(name):
            return ctx.enter_context(nc.semaphore(name))

        WC = P * PT // 4
        hb, xc, sq = sb("p_hb", [P, 4, KT, L]), sb("p_xc", [P, 2, KT, L]), sb("p_sq", [P, 2, KT, L])
        sd, rs = sb("p_sd", [P, 2, L]), sb("p_rs", [P, 2, L])
        xsp = sb("p_xsp", [P, 2, 2, KT, L], F16)
        wst = sb("p_wst", [P, 2, WC])
        ost = sb("p_ost", [P, 2, D])
        wdt = sb("p_wdt", [P, KT, HEADS])
        wdt_hi, wdt_lo = sb("p_wdt_hi", [P, KT, HEADS], F16), sb("p_wdt_lo", [P, KT, HEADS], F16)
        dtv = sb("p_dtv", [P, 4])
        nw = sb("p_nw", [P, ZT])
        eps = sb("p_eps", [P, 1])
        vec = sb("p_vec", [P, 3])
        dtr = sb("p_dtr", [P, 4, L])
        mean_ps = [ctx.enter_context(nc.psum_tensor(f"p_mean{i}", [P, 512], F32)) for i in range(2)]
        var_ps = [ctx.enter_context(nc.psum_tensor(f"p_var{i}", [P, 512], F32)) for i in range(2)]
        dt_ps = [ctx.enter_context(nc.psum_tensor(f"p_dt{i}", [P, 512], F32)) for i in range(2)]
        tr_ps = [ctx.enter_context(nc.psum_tensor(f"p_tr{i}", [P, P], F32)) for i in range(2)]

        small_in = sem("p_small_in")
        h_in = [sem(f"p_h_in{i}") for i in range(4)]
        w_in = [sem(f"p_w_in{i}") for i in range(2)]
        o_in = [sem(f"p_o_in{i}") for i in range(2)]
        setup, setup_act, consts = sem("p_setup"), sem("p_setup_act"), sem("p_consts")
        mean_done, centered, squared, var_done = sem("p_mean_done"), sem("p_centered"), sem("p_squared"), sem("p_var_done")
        sd_done, rs_done, normed, hi_done, lo_done = sem("p_sd_done"), sem("p_rs_done"), sem("p_normed"), sem("p_hi_done"), sem("p_lo_done")
        w_hi_done, w_lo_done, o_hi_done, o_lo_done = sem("p_w_hi_done"), sem("p_w_lo_done"), sem("p_o_hi_done"), sem("p_o_lo_done")
        dt_mm, dt_out = sem("p_dt_mm"), sem("p_dt_out")
        x_out = [sem(f"p_x_out{i}") for i in range(2)]
        chain, soft_act, dt_ready, tr_done, a_ready = sem("p_chain"), sem("p_soft_act"), sem("p_dt_ready"), sem("p_tr_done"), sem("p_a_ready")
        tr_out, stored, tail_in = sem("p_tr_out"), sem("p_stored"), sem("p_tail_in")

        block = ctx.enter_context(nc.Block())

        @block.sync
        def _(sp):
            sp.dma_start(wdt[:, :, :], t["W_in"][:, P * PT:].rearrange("(k p) n -> p k n", p=P)).then_inc(small_in, 16)
            sp.dma_start(dtv[:, :], t["dt_vec"]).then_inc(small_in, 16)
            sp.dma_start(nw[:, :], t["norm_w"]).then_inc(small_in, 16)
            sp.dma_start(keep["ident"][:, :], t["ident"]).then_inc(small_in, 16)

            def load_h(i, g):
                if not (static(i) and i == 0):
                    sp.wait_ge(centered, 4 * i + g - 3)
                sp.dma_start(hb[:, g, :, :], scratch["h"][4 * i + g]).then_inc(h_in[g], 16)

            def load_weights(i, g):
                n, s = 4 * i + g, g % 2
                if not (static(i) and i == 0 and g < 2):
                    sp.wait_ge(w_lo_done, n - 1)
                    sp.wait_ge(o_lo_done, n - 1)
                sp.dma_start(wst[:, s, :], t["W_in"][bass.ds(i * P, P), g * WC:g * WC + WC]).then_inc(w_in[s], 16)
                sp.dma_start(ost[:, s, :], t["W_out"][bass.ds(n * P, P), :]).then_inc(o_in[s], 16)

            for g in range(2):
                load_h(0, g)

            def four(i):
                for g in range(4):
                    if g < 2:
                        load_h(i, g + 2)
                    elif not (static(i) and i == 3):
                        load_h(i + 1, g - 2)
                    load_weights(i, g)

            four(0)
            with sp.Fori(1, 3) as i:
                four(i)
            four(3)
            sp.wait_ge(a_ready, 1)
            for g in range(4):
                rows = slice(HEADS * g, HEADS * g + HEADS)
                sp.dma_start(scratch["a"].rearrange("(i g) h l -> g h i l", g=4)[g], keep["a"][rows, :, :]).then_inc(stored, 16)
                sp.dma_start(scratch["dt_tail"].rearrange("(i g) h o -> g h i o", g=4)[g],
                             dtr[rows, :, L - 1:L], allow_slow_non_contiguous=True).then_inc(stored, 16)
            sp.wait_ge(stored, 16 * 8)
            sp.dma_start(keep["dt_tail"][:, :, :], scratch["dt_tail"].rearrange("b h o -> (b h o)").partition_broadcast(P)
                         .rearrange("p (b h) -> p b h", b=NB)).then_inc(tail_in, 16)
            sp.wait_ge(tail_in, 16)
            for q in range(2):
                sp.wait_ge(x_out[q], 16 * 8)

        @block.tensor
        def _(pe):
            ones = keep["ones_d"]

            def mean(i, g):
                n, s = 4 * i + g, g % 2
                pe.wait_ge(h_in[g], 16 * i + 16)
                if not (static(i) and i == 0 and g < 2):
                    pe.wait_ge(centered, n - 1)
                for k in range(KT):
                    last = nc.tensor.matmul(mean_ps[s][:, 0:L], ones[:, :], hb[:, g, k, :], start=k == 0, stop=k == KT - 1)
                last.then_inc(mean_done, 1)

            def var(n, s):
                pe.wait_ge(squared, n + 1)
                if not (static(n) and n < 2):
                    pe.wait_ge(sd_done, n - 1)
                for k in range(KT):
                    last = nc.tensor.matmul(var_ps[s][:, 0:L], ones[:, :], sq[:, s, k, :], start=k == 0, stop=k == KT - 1)
                last.then_inc(var_done, 1)

            def dts(n, s, g):
                pe.wait_ge(lo_done, n + 1)
                pe.wait_ge(hi_done, n + 1)
                if not (static(n) and n < 2):
                    pe.wait_ge(dt_out, n - 1)
                rows = slice(HEADS * g, HEADS * g + HEADS)
                for k in range(KT):
                    for m, (w, x) in enumerate(((wdt_hi, 0), (wdt_hi, 1), (wdt_lo, 0))):
                        last = nc.tensor.matmul(dt_ps[s][rows, 0:L], w[:, k, :], xsp[:, s, x, k, :],
                                                start=k == 0 and m == 0, stop=k == KT - 1 and m == 2)
                last.then_inc(dt_mm, 1)

            pe.wait_ge(consts, 2)
            pe.wait_ge(setup, 5)
            mean(0, 0)

            def four(i):
                for g in range(4):
                    n = 4 * i + g
                    var(n, g % 2)
                    if g < 3:
                        mean(i, g + 1)
                    elif not (static(i) and i == 3):
                        mean(i + 1, 0)
                    if not (g == 0 and static(i) and i == 0):
                        dts(n - 1, (g - 1) % 2, (g - 1) % 4)

            four(0)
            with pe.Fori(1, 3) as i:
                four(i)
            four(3)
            dts(NB - 1, 1, 3)
            pe.wait_ge(dt_ready, 1)
            for m in range(2):
                for i in range(4):
                    n = 4 * m + i
                    if n >= 2:
                        pe.wait_ge(tr_out, n - 1)
                    nc.tensor.transpose(tr_ps[n % 2][:, :], dtr[:, i, P * m:P * m + P], keep["ident"][:, 0:P]).then_inc(tr_done, 1)

        @block.scalar
        def _(act):
            A = act.activation
            act.wait_ge(consts, 2)
            act.wait_ge(small_in, 64)
            A(wdt_hi[:, :, :], wdt[:, :, :], ACT.Identity, scale=W_SCALE).then_inc(setup_act, 1)
            act.wait_ge(setup, 1)
            A(vec[:, 2:3], vec[:, 2:3], ACT.Exp).then_inc(setup_act, 1)
            act.wait_ge(setup, 5)

            def square(n, s):
                act.wait_ge(centered, n + 1)
                if not (static(n) and n < 2):
                    act.wait_ge(var_done, n - 1)
                A(sq[:, s, :, :], xc[:, s, :, :], ACT.Square).then_inc(squared, 1)

            square(0, 0)

            def four(i):
                for g in range(4):
                    n, s = 4 * i + g, g % 2
                    nws = nw[:, n:n + 1] if static(n) else nw[:, bass.ds(n, 1)]
                    act.wait_ge(var_done, n + 1)
                    if not (static(n) and n < 2):
                        act.wait_ge(rs_done, n - 1)
                    A(sd[:, s, :], var_ps[s][:, 0:L], ACT.Sqrt, bias=eps[:, 0:1]).then_inc(sd_done, 1)
                    if not (static(n) and n == 0):
                        act.wait_ge(lo_done, n)
                        act.dma_start(scratch["xn"][n - 1], xsp[:, 1 - s, :, :, :]).then_inc(x_out[1 - s], 16)
                    act.wait_ge(w_in[s], 16 * (2 * i + g // 2 + 1))
                    A(keep["w_hi"][:, i, g * WC:g * WC + WC], wst[:, s, :], ACT.Identity, scale=W_SCALE).then_inc(w_hi_done, 1)
                    act.wait_ge(o_in[s], 16 * (2 * i + g // 2 + 1))
                    A(keep["o_hi"][:, n, :], ost[:, s, :], ACT.Identity, scale=nws).then_inc(o_hi_done, 1)
                    act.wait_ge(normed, n + 1)
                    if not (static(n) and n < 2):
                        act.wait_ge(x_out[s], 16 * (2 * i + g // 2))
                    A(xsp[:, s, 0, :, :], xc[:, s, :, :], ACT.Identity).then_inc(hi_done, 1)
                    if not (g == 3 and static(i) and i == 3):
                        square(n + 1, (g + 1) % 2)
                    if not (g == 0 and static(i) and i == 0):
                        dt_evac(n - 1, (g - 1) % 2, (g - 1) % 4, i if g else i - 1)

            def dt_evac(n, s, g, i):
                act.wait_ge(dt_mm, n + 1)
                rows = slice(HEADS * g, HEADS * g + HEADS)
                A(dtr[rows, i, :], dt_ps[s][rows, 0:L], ACT.Identity, scale=vec[rows, 0:1],
                  bias=vec[rows, 1:2]).then_inc(dt_out, 1)

            four(0)
            with act.Fori(1, 3) as i:
                four(i)
            four(3)
            act.wait_ge(lo_done, NB)
            act.dma_start(scratch["xn"][NB - 1], xsp[:, 1, :, :, :]).then_inc(x_out[1], 16)
            dt_evac(NB - 1, 1, 3, 3)
            act.wait_ge(dt_out, NB)
            A(sq[:, 0, :, :], dtr[:, :, :], ACT.Abs).then_inc(soft_act, 1)
            act.wait_ge(soft_act, 1)
            A(sq[:, 1, :, :], sq[:, 0, :, :], ACT.Exp, scale=-1.0).then_inc(soft_act, 1)
            act.wait_ge(dt_ready, 2)
            A(keep["a"][:, :, :], sq[:, 0, :, :], ACT.Exp).then_inc(soft_act, 1)

        @block.vector
        def _(dve):
            TT, TS, STT = nc.vector.tensor_tensor, nc.vector.tensor_scalar, nc.vector.scalar_tensor_tensor
            dve.wait_ge(small_in, 64)
            TS(vec[:, 2:3], dtv[:, 3:4], 88.0, None, ALU.min).then_inc(setup, 1)
            TS(vec[:, 0:1], dtv[:, 1:2], 1.0 / (X_SCALE * W_SCALE), None, ALU.mult).then_inc(setup, 1)
            STT(out=vec[:, 1:2], in0=dtv[:, 0:1], scalar=dtv[:, 1:2], in1=dtv[:, 2:3], op0=ALU.mult, op1=ALU.add).then_inc(setup, 1)
            TS(nw[:, :], nw[:, :], O_SCALE, None, ALU.mult).then_inc(setup, 1)
            dve.wait_ge(setup_act, 1)
            STT(out=wdt_lo[:, :, :], in0=wdt[:, :, :], scalar=W_SCALE, in1=wdt_hi[:, :, :],
                op0=ALU.mult, op1=ALU.subtract).then_inc(setup, 1)
            dve.wait_ge(setup_act, 2)
            dve.wait_ge(setup, 5)
            TS(vec[:, 2:3], vec[:, 2:3], -1.0, None, ALU.mult).then_inc(setup, 1)

            def center(n, s, g):
                dve.wait_ge(mean_done, n + 1)
                if not (static(n) and n < 2):
                    dve.wait_ge(lo_done, n - 1)
                TT(xc[:, s, :, :], hb[:, g, :, :], bcast(mean_ps[s][:, 0:L], 1, KT), ALU.subtract).then_inc(centered, 1)

            center(0, 0, 0)

            def four(i):
                for g in range(4):
                    n, s = 4 * i + g, g % 2
                    nws = nw[:, n:n + 1] if static(n) else nw[:, bass.ds(n, 1)]
                    dve.wait_ge(sd_done, n + 1)
                    if not (static(n) and n < 2):
                        dve.wait_ge(normed, n - 1)
                    nc.vector.reciprocal(rs[:, s, :], sd[:, s, :]).then_inc(rs_done, 1)
                    dve.wait_ge(rs_done, n + 1)
                    STT(out=xc[:, s, :, :], in0=xc[:, s, :, :], scalar=X_SCALE, in1=bcast(rs[:, s, :], 1, KT),
                        op0=ALU.mult, op1=ALU.mult).then_inc(normed, 1)
                    if not (g == 3 and static(i) and i == 3):
                        center(n + 1, (g + 1) % 2, (g + 1) % 4)
                    dve.wait_ge(w_hi_done, n + 1)
                    cols = slice(g * WC, g * WC + WC)
                    STT(out=keep["w_lo"][:, i, cols], in0=wst[:, s, :], scalar=W_SCALE, in1=keep["w_hi"][:, i, cols],
                        op0=ALU.mult, op1=ALU.subtract).then_inc(w_lo_done, 1)
                    dve.wait_ge(o_hi_done, n + 1)
                    STT(out=keep["o_lo"][:, n, :], in0=ost[:, s, :], scalar=nws,
                        in1=keep["o_hi"][:, n, :], op0=ALU.mult, op1=ALU.subtract).then_inc(o_lo_done, 1)

            four(0)
            with dve.Fori(1, 3) as i:
                four(i)
            four(3)
            link = Link(dve, chain)
            dve.wait_ge(soft_act, 2)
            u, q, q2, w = sq[:, 1, :, :], sq[:, 0, :, :], xc[:, 0, :, :], xc[:, 1, :, :]
            link(TS(q, u, 2.0, None, ALU.add))
            link(nc.vector.reciprocal(q, q))
            link(TT(q, q, u, ALU.mult))
            link(TT(q2, q, q, ALU.mult))
            link(TS(w, q2, 1.0 / 13, None, ALU.mult))
            for k in range(5, 0, -1):
                link(STT(out=w, in0=w, scalar=1.0 / (2 * k + 1), in1=q2, op0=ALU.add, op1=ALU.mult))
            link(STT(out=w, in0=w, scalar=1.0, in1=q, op0=ALU.add, op1=ALU.mult))
            link(TS(w, w, 2.0, None, ALU.mult))
            STT(out=dtr[:, :, :], in0=dtr[:, :, :], scalar=0.0, in1=w, op0=ALU.max, op1=ALU.add).then_inc(dt_ready, 1)
            dve.wait_ge(dt_ready, 1)
            TS(sq[:, 0, :, :], dtr[:, :, :], vec[:, 2:3], -200.0, ALU.mult, ALU.max).then_inc(dt_ready, 1)
            dve.wait_ge(soft_act, 3)
            nc.vector.memset(keep["a"][:, :, 0:1], 0.0).then_inc(a_ready, 1)
            for m in range(2):
                for i in range(4):
                    n = 4 * m + i
                    dve.wait_ge(tr_done, n + 1)
                    nc.vector.tensor_copy(keep["dt_tok"][:, m, 4 * i:4 * i + 4, :].rearrange("p b h -> p (b h)"),
                                          tr_ps[n % 2][:, :]).then_inc(tr_out, 1)

        @block.gpsimd
        def _(pool):
            nc.gpsimd.memset(keep["ones_d"][:, :], 1.0 / D).then_inc(consts, 1)
            nc.gpsimd.memset(eps[:, :], EPS).then_inc(consts, 1)

            def four(i):
                for g in range(4):
                    n, s = 4 * i + g, g % 2
                    pool.wait_ge(hi_done, n + 1)
                    if not (static(n) and n < 2):
                        pool.wait_ge(x_out[s], 16 * (2 * i + g // 2))
                    nc.gpsimd.tensor_tensor(xsp[:, s, 1, :, :], xc[:, s, :, :], xsp[:, s, 0, :, :], ALU.subtract).then_inc(lo_done, 1)

            peeled(pool, 0, 4, four)


class Mamba:

    STEP = 5 * GROUPS + 8

    @staticmethod
    def starts(b, g):
        return static(b) and b == 0 and g < 2

    @staticmethod
    def base(b, g):
        if static(b) and b == 0:
            return 8 + 4 * g if g < 3 else 6 + 5 * g
        return 2 + Mamba.STEP * b + 5 * g + (0 if g < 3 else 2 if g == 3 else 4)

    @staticmethod
    def bank(b, g):
        return Mamba.base(0 if static(b) and b == 0 else 1, g) % 4

    @staticmethod
    def x(b, g):
        return 5 if g == GROUPS - 1 else 0

    @staticmethod
    def z(b, g):
        return 7 if g == GROUPS - 1 else 2 if Mamba.starts(b, g) else 3

    @staticmethod
    def norm(b, g):
        return 0 if g == GROUPS - 1 else 2

    OUT = 5

    @staticmethod
    def out_half(b, g):
        return g - 2 if g in (2, 3) and not (static(b) and b == 0) else None

    @staticmethod
    def pair(b, g):
        return 2 + 10 * b + g


def mamba_phase(nc, t, scratch, keep):
    with ExitStack() as ctx:
        def sb(name, shape, dt=F32):
            return ctx.enter_context(nc.sbuf_tensor(name, shape, dt))

        def sem(name):
            return ctx.enter_context(nc.semaphore("m_" + name))

        L1 = L - P
        xn = sb("m_xn", [P, 2, KT, L], F16)
        HT = KT // 2
        hb, h1 = sb("m_hb", [P, HT, L]), sb("m_h1", [P, HT, L])
        vb, vm = sb("m_vb", [P, PT]), sb("m_vm", [P, PT])
        cw, cb = sb("m_cw", [P, CT, 4]), sb("m_cb", [P, CT])
        sc3, bi3 = sb("m_sc3", [P, CT]), sb("m_bi3", [P, CT])
        dp, bo = sb("m_dp", [P, ZT]), sb("m_bo", [P, KT])
        xb, acc = sb("m_xb", [P, 2, 2, L + 3]), sb("m_acc", [P, 2, 2, L])
        xs, zs = sb("m_xs", [P, 4, 2, L]), sb("m_zs", [P, 4, 2, L])
        bz = sb("m_bz", [P, 2, 4, L])
        cs = sb("m_cs", [P, 2, L])
        xt = sb("m_xt", [P, 2, 2, 2 * P])
        dec = sb("m_dec", [P, 2, GH, L])
        dec1 = sb("m_dec1", [P, 2, GH, L1])
        yg = sb("m_yg", [P, 4, 2, L])
        sq = sb("m_sq", [P, 2, L])
        sd, rs = sb("m_sd", [P, L]), sb("m_rs", [P, L])
        yn_hi, yn_lo = sb("m_yn_hi", [P, ZT, L], F16), sb("m_yn_lo", [P, ZT, L], F16)
        tailp, tailw = sb("m_tailp", [P, 2, 4]), sb("m_tailw", [P, GROUPS, 2])
        tailx = sb("m_tailx", [P, 2])
        ones_g, ones = sb("m_ones_g", [P, P]), sb("m_ones", [P, P])
        cb1 = sb("m_cb1", [P, L1])
        eps, silu_eps = sb("m_eps", [P, 1]), sb("m_silu_eps", [P, 1])
        rot_in, rot_mid = sb("m_rot_in", [P, 2, PIECE]), sb("m_rot_mid", [P, PIECE])
        ident = keep["ident"]
        pi = [ctx.enter_context(nc.psum_tensor(f"m_pi{i}", [P, 512], F32)) for i in range(4)]
        pt = ctx.enter_context(nc.psum_tensor("m_pt", [P, 2, 2 * P], F32))
        pg = ctx.enter_context(nc.psum_tensor("m_pg", [P, 512], F32))
        py = [ctx.enter_context(nc.psum_tensor(f"m_py{i}", [P, 512], F32)) for i in range(2)]

        small_in, consts, setup = sem("small_in"), sem("consts"), sem("setup")
        xn_in, h_in, h1_out = sem("xn_in"), sem("h_in"), sem("h1_out")
        dec_in = [sem(f"dec_in{i}") for i in range(2)]
        piece_in, piece_out = ([sem(f"piece_{x}{j}") for j in range(3)] for x in ("in", "out"))
        piece_step = sem("piece_step")
        load_at, store_at = {0: 0, 1: 1, 4: 2}, {3: (0, 1), 6: (2,)}
        tile_full, tile_free = sem("tile_full"), sem("tile_free")
        transposed, cb_done, heads_done = sem("transposed"), sem("cb_done"), sem("heads_done")
        convolved, activated = sem("convolved"), sem("activated")
        cb_copied, table_back, sq_summed = sem("cb_copied"), sem("table_back"), sem("sq_summed")
        squared, hi_done, lo_done, h1_done = sem("squared"), sem("hi_done"), sem("lo_done"), sem("h1_done")
        xt_done, scanned, weighted, weighted1 = sem("xt_done"), sem("scanned"), sem("weighted"), sem("weighted1")
        tailp_done, tailw_done, tail_step = sem("tailp_done"), sem("tailw_done"), sem("tail_step")
        y_step, gated, rs_done, normed = sem("y_step"), sem("gated"), sem("rs_done"), sem("normed")

        block = ctx.enter_context(nc.Block())

        def batches(eng, body):
            body(0)
            body(1)
            with eng.Fori(2, NB - 1) as b:
                body(b)
            body(NB - 1)

        def last(b):
            return static(b) and b == NB - 1

        @block.sync
        def _(sp):
            sp.dma_start(xn[:, :, :, :], scratch["xn"][0]).then_inc(xn_in, 16)
            for dst, src in ((vb, "b_in"), (vm, "mup"), (cb, "conv_b"), (dp, "D"), (bo, "b_out")):
                sp.dma_start(dst[:, :], t[src]).then_inc(small_in, 16)
            sp.dma_start(cw[:, :, :], t["conv_w"]).then_inc(small_in, 16)

            def decays(n, b, g, s):
                sp.dma_start(dec[:, s, :, :].rearrange("p h l -> p (h l)"),
                             scratch["a"].rearrange("b (g h) l -> b g (h l)", h=GH)[b, g].partition_broadcast(P)
                             ).then_inc(dec_in[s], 16)

            decays(0, 0, 0, 0)

            def load_h(b, half):
                if not (static(b) and b == 0 and half == 0):
                    sp.wait_ge(h1_done, 2 * b + half)
                sp.dma_start(hb[:, :, :], scratch["h"][b][:, HT * half:HT * half + HT, :]).then_inc(h_in, 16)

            def store_h1(b, half):
                sp.wait_ge(h1_done, 2 * b + half + 1)
                sp.dma_start(scratch["h1"][b][:, HT * half:HT * half + HT, :], h1[:, :, :]).then_inc(h1_out, 16)

            def piece(b, j):
                if j:
                    return t["W_ug"][2 * b + j - 1], scratch["ug_sum"][2 * b + j - 1]
                return t["W_down"][b], scratch["down_sum"][b]

            def load_piece(b, j):
                if j == 2:
                    sp.wait_ge(piece_out[0], 16 * b + 16)
                elif not (static(b) and b == 0):
                    sp.wait_ge(piece_out[(2, 1)[j]], 16 * b)
                sp.dma_start(rot_in[:, j % 2, :], piece(b, j)[0]).then_inc(piece_in[j], 16)

            def store_piece(b, j):
                sp.wait_ge(piece_step, 16 * b + (8, 12, 16)[j])
                sp.dma_start(piece(b, j)[1], rot_in[:, j % 2, :]).then_inc(piece_out[j], 16)

            def batch(b):
                for g in range(GROUPS):
                    u = 8 * b + g
                    if g == 0:
                        if not (static(b) and b == 0):
                            load_h(b - 1, 0)
                    if g == 3 and not (static(b) and b == 0):
                        load_h(b - 1, 1)
                        store_h1(b - 1, 0)
                    if g == 4 and not (static(b) and b == 0):
                        store_h1(b - 1, 1)
                    if g == GROUPS - 1 and not last(b):
                        sp.wait_ge(tile_full, Mamba.base(b, g - 1) + Mamba.z(b, g - 1) + 2)
                        sp.dma_start(xn[:, :, :, :], scratch["xn"][b + 1]).then_inc(xn_in, 16)
                    if not (last(b) and g == GROUPS - 1):
                        if not (static(b) and b == 0 and g == 0):
                            sp.wait_ge(heads_done, u)
                        if g < GROUPS - 1:
                            decays(u + 1, b, g + 1, (g + 1) % 2)
                        else:
                            decays(u + 1, b + 1, 0, 0)
                    if g in store_at:
                        for j in store_at[g]:
                            store_piece(b, j)
                    if g in load_at:
                        load_piece(b, load_at[g])

            batches(sp, batch)
            for half in range(2):
                load_h(NB - 1, half)
                if half:
                    store_h1(NB - 1, 0)
            store_h1(NB - 1, 1)
            sp.wait_ge(h1_out, 16 * 2 * NB)
            for j in range(3):
                sp.wait_ge(piece_out[j], 16 * NB)

        @block.tensor
        def _(pe):
            def split_mm(dst, k_tiles, w_hi, w_lo, x_hi, x_lo):
                for k in range(k_tiles):
                    for m, (w, x) in enumerate(((w_hi, x_hi), (w_hi, x_lo), (w_lo, x_hi))):
                        ins = nc.tensor.matmul(dst, w(k), x(k), start=k == 0 and m == 0,
                                               stop=k == k_tiles - 1 and m == 2)
                ins.then_inc(tile_full, 1)

            def project(tile, q, cols):
                if not static(tile) or tile >= 4:
                    pe.wait_ge(tile_free, tile - 3)
                cols = slice(cols * P, cols * P + P)
                split_mm(pi[q][:, 0:L], KT, lambda k: keep["w_hi"][:, k, cols], lambda k: keep["w_lo"][:, k, cols],
                         lambda k: xn[:, 0, k, :], lambda k: xn[:, 1, k, :])

            def project_bc(tile, q):
                for j, col in enumerate((2, 3, 0, 1)):
                    project(tile + j, (q + j) % 4, 2 * ZT + col)

            def project_x(tile, q, g):
                for j in range(2):
                    project(tile + j, (q + j) % 4, ZT + 2 * g + j)

            def project_z(tile, q, g):
                for j in range(2):
                    project(tile + j, (q + j) % 4, 2 * g + j)

            def heads(n, s):
                pe.wait_ge(weighted, n + 1)
                pe.wait_ge(weighted1, n + 1)
                pe.wait_ge(xt_done, n + 1)
                if not (static(n) and n == 0):
                    pe.wait_ge(y_step, 2 * n)
                for q in range(2):
                    for hh in range(2):
                        h = 2 * q + hh
                        rows, cols = slice(HD * hh, HD * hh + HD), slice(HD * h, HD * h + HD)
                        nc.tensor.matmul(py[q][rows, 0:L], xt[:, s, 0, cols], dec[:, s, h, :], start=True, stop=False)
                        ins = nc.tensor.matmul(py[q][rows, P:L], xt[:, s, 1, cols], dec1[:, s, h, :], start=False, stop=True)
                ins.then_inc(heads_done, 1)

            def norm(tile, q, n):
                pe.wait_ge(sq_summed, n + 1)
                pe.wait_ge(tile_free, tile - 3)
                nc.tensor.matmul(pi[q][:, 0:L], ones_g[:, :], sq[:, 0, :], start=True, stop=True).then_inc(tile_full, 1)

            def out_project(tile, q, b, half):
                pe.wait_ge(lo_done, 8 * b + 8)
                pe.wait_ge(hi_done, 8 * b + 8)
                for j in range(HT):
                    pe.wait_ge(tile_free, tile + j - 3)
                    cols = slice((HT * half + j) * P, (HT * half + j + 1) * P)
                    split_mm(pi[(q + j) % 4][:, 0:L], ZT, lambda k: keep["o_hi"][:, k, cols],
                             lambda k: keep["o_lo"][:, k, cols], lambda k: yn_hi[:, k, :], lambda k: yn_lo[:, k, :])

            pe.wait_ge(consts, 8)
            pe.wait_ge(xn_in, 16)
            project_bc(0, 0)
            project_x(4, 0, 0)
            project_z(6, 2, 0)

            def batch(b):
                for g in range(GROUPS):
                    u = 8 * b + g
                    tile, q = Mamba.base(b, g), Mamba.bank(b, g)
                    x, z, nt = Mamba.x(b, g), Mamba.z(b, g), Mamba.norm(b, g)
                    def transpose():
                        pe.wait_ge(activated, Mamba.pair(b, g) + 1)
                        if not (static(b) and b == 0 and g == 0):
                            pe.wait_ge(xt_done, u)
                        for m in range(2):
                            for j in range(2):
                                ins = nc.tensor.transpose(pt[:, m, j * P:j * P + P], xs[:, g % 4, j, m * P:m * P + P], ident[:, 0:P])
                        ins.then_inc(transposed, 1)

                    def c_times_b():
                        if not (static(b) and b == 0 and g == 0):
                            pe.wait_ge(weighted, u)
                        if g == 0:
                            pe.wait_ge(tailp_done, b + 1)
                            nc.tensor.matmul(pg[:, 400:408], ones[:, :], tailp[:, :, :].rearrange("p t r -> p (t r)"),
                                             start=True, stop=True)
                        if g == 1:
                            pe.wait_ge(tailw_done, 2 * b + 2)
                        nc.tensor.matmul(pg[:, 0:L], bz[:, g // 4, g % 4, 0:P], cs[:, g // 4, :], start=True, stop=True)
                        nc.tensor.matmul(pg[:, L:L + L1], bz[:, g // 4, g % 4, P:2 * P], cs[:, g // 4, P:L],
                                         start=True, stop=True).then_inc(cb_done, 1)

                    if g == 0:
                        pe.wait_ge(activated, 10 * b + 2)
                        c_times_b()
                        transpose()
                    else:
                        transpose()
                        c_times_b()

                    def sums():
                        if not Mamba.starts(b, g):
                            norm(tile + nt, (q + nt) % 4, u - 2)

                    def previous():
                        if not (static(b) and b == 0 and g == 0):
                            heads(u - 1, (g - 1) % 2)

                    if g == GROUPS - 1:
                        previous()
                        sums()
                        if not last(b):
                            pe.wait_ge(xn_in, 16 * (b + 2))
                            project_bc(tile + 1, q + 1)
                            project_x(tile + x, q + x, 0)
                            project_z(tile + z, q + z, 0)
                    else:
                        project_x(tile + x, q + x, g + 1)
                        sums()
                        previous()
                        project_z(tile + z, q + z, g + 1)
                        if Mamba.out_half(b, g) is not None:
                            out_project(tile + Mamba.OUT, q + Mamba.OUT, b - 1, Mamba.out_half(b, g))

            batches(pe, batch)
            end = Mamba.base(NB - 1, 7) + 1
            heads(UNITS - 1, 1)
            norm(end, end % 4, UNITS - 2)
            norm(end + 1, (end + 1) % 4, UNITS - 1)
            for half in range(2):
                out_project(end + 2 + HT * half, (end + 2 + HT * half) % 4, NB - 1, half)

        @block.scalar
        def _(act):
            A = act.activation

            def pair(tile, q, p, c, g_slot):
                for j in range(2):
                    act.wait_ge(tile_full, tile + j + 1)
                    ps = pi[(q + j) % 4][:, 0:L]
                    A(xb[:, g_slot, j, 3:L + 3], ps, ACT.Identity, scale=vm[:, ZT + c + j:ZT + c + j + 1],
                      bias=vb[:, ZT + c + j:ZT + c + j + 1])
                    A(acc[:, g_slot, j, :], ps, ACT.Identity, scale=sc3[:, c + j:c + j + 1],
                      bias=bi3[:, c + j:c + j + 1]).then_inc(tile_free, 1)

            def project_pair(tile, q, p, c, slot):
                if not (static(p) and p < 2):
                    act.wait_ge(activated, p - 1)
                pair(tile, q, p, c, slot)

            def silu_x(p, slot, b, g):
                act.wait_ge(convolved, 6 * p + 6)
                u = 8 * b + g
                if not (static(b) and b == 0 and g < 4):
                    act.wait_ge(gated, u - 3)
                A(xs[:, g % 4, :, :], acc[:, slot, :, :], ACT.Silu).then_inc(activated, 1)

            def silu_c(b):
                act.wait_ge(convolved, 6 * (10 * b) + 6)
                if not (static(b) and b == 0):
                    act.wait_ge(cb_done, 8 * b)
                A(cs[:, :, :], acc[:, 0, :, :], ACT.Silu).then_inc(activated, 1)

            def silu_b(b):
                act.wait_ge(convolved, 6 * (10 * b) + 12)
                if not (static(b) and b == 0):
                    act.wait_ge(cb_done, 8 * b)
                for r in range(4):
                    rows = slice(SD * r, SD * r + SD)
                    ins = A(bz[rows, :, r, :], acc[rows, 1, :, :], ACT.Silu)
                ins.then_inc(activated, 1)

            def copy_cb(n):
                act.wait_ge(cb_done, n + 1)
                if not (static(n) and n == 0):
                    act.wait_ge(weighted1, n)
                A(cb1[:, :], pg[:, L:L + L1], ACT.Identity).then_inc(cb_copied, 1)

            def gates(tile, q, b, g):
                u = 8 * b + g
                if not (static(b) and b == 0 and g < 4):
                    act.wait_ge(gated, u - 3)
                for j in range(2):
                    act.wait_ge(tile_full, tile + j + 1)
                    c = 2 * g + j
                    A(zs[:, g % 4, j, :], pi[(q + j) % 4][:, 0:L], ACT.Silu, scale=vm[:, c:c + 1],
                      bias=vb[:, c:c + 1]).then_inc(tile_free, 1)

            def pair_x(tile, q, b, g):
                project_pair(tile, q, Mamba.pair(b, g), 2 * g, g % 2)

            def pair_bc(tile, q, b, j):
                project_pair(tile + 2 * j, q + 2 * j, 10 * b + j, ZT + 2 * (1 - j), j)

            def deviation(tile, q, n):
                act.wait_ge(tile_full, tile + 1)
                if not (static(n) and n == 0):
                    act.wait_ge(rs_done, n)
                A(sd[:, :], pi[q % 4][:, 0:L], ACT.Sqrt, bias=eps[:, 0:1]).then_inc(tile_free, 1)
                if not (static(n) and n == 0):
                    act.wait_ge(table_back, n)
                A(silu_eps[:, :], eps[:, :], ACT.Silu).then_inc(table_back, 1)

            def square(n, s, norm_tile):
                act.wait_ge(gated, n + 1)
                if norm_tile is not None:
                    act.wait_ge(tile_full, norm_tile + 1)
                A(sq[:, :, :], yg[:, s, :, :], ACT.Square).then_inc(squared, 1)

            def high(n, s, g):
                act.wait_ge(normed, n + 1)
                A(yn_hi[:, 2 * g:2 * g + 2, :], yg[:, s, :, :], ACT.Identity).then_inc(hi_done, 1)

            def residual(tile, q, b, half):
                if not (static(b) and b == 0 and half == 0):
                    act.wait_ge(h1_out, 16 * (2 * b + half))
                for j in range(HT):
                    act.wait_ge(tile_full, tile + j + 1)
                    k = HT * half + j
                    A(h1[:, j, :], pi[(q + j) % 4][:, 0:L], ACT.Identity, scale=1.0 / (X_SCALE * O_SCALE),
                      bias=bo[:, k:k + 1]).then_inc(tile_free, 1)

            act.wait_ge(consts, 8)
            act.wait_ge(setup, 5)
            pair_bc(0, 0, 0, 0)
            pair_bc(0, 0, 0, 1)
            silu_c(0)
            silu_b(0)
            pair_x(4, 0, 0, 0)
            silu_x(2, 0, 0, 0)
            gates(6, 2, 0, 0)

            def batch(b):
                for g in range(GROUPS):
                    u = 8 * b + g
                    tile, q = Mamba.base(b, g), Mamba.bank(b, g)
                    x, z, nt = Mamba.x(b, g), Mamba.z(b, g), Mamba.norm(b, g)
                    starts, first = Mamba.starts(b, g), static(b) and b == 0 and g == 0
                    half = Mamba.out_half(b, g)
                    copy_cb(u)

                    if g == GROUPS - 1:
                        deviation(tile + nt, q + nt, u - 2)
                        if not last(b):
                            pair_bc(tile + 1, q + 1, b + 1, 0)
                        square(u - 1, (g - 1) % 4, tile + nt)
                        high(u - 2, (g - 2) % 4, (g - 2) % 8)
                        if not last(b):
                            pair_bc(tile + 1, q + 1, b + 1, 1)
                            silu_c(b + 1)
                            pair_x(tile + x, q + x, b + 1, 0)
                            silu_b(b + 1)
                            silu_x(Mamba.pair(b + 1, 0), 0, b + 1, 0)
                            gates(tile + z, q + z, b + 1, 0)
                    else:
                        pair_x(tile + x, q + x, b, g + 1)
                        if not starts:
                            deviation(tile + nt, q + nt, u - 2)
                        silu_x(Mamba.pair(b, g + 1), (g + 1) % 2, b, g + 1)
                        gates(tile + z, q + z, b, g + 1)
                        if not first:
                            square(u - 1, (g - 1) % 4, None if starts else tile + nt)
                        if half is not None:
                            residual(tile + Mamba.OUT, q + Mamba.OUT, b - 1, half)
                        if half == 1:
                            high(u - 3, (g - 3) % 4, (g - 3) % 8)
                        if not (starts or half == 0):
                            high(u - 2, (g - 2) % 4, (g - 2) % 8)

            batches(act, batch)
            end = Mamba.base(NB - 1, 7) + 1
            deviation(end, end, UNITS - 2)
            square(UNITS - 1, 3, end)
            high(UNITS - 2, 2, 6)
            deviation(end + 1, end + 1, UNITS - 1)
            high(UNITS - 1, 3, 7)
            for half in range(2):
                residual(end + 2 + HT * half, end + 2 + HT * half, NB - 1, half)

        @block.vector
        def _(dve):
            TT, TS, STT = nc.vector.tensor_tensor, nc.vector.tensor_scalar, nc.vector.scalar_tensor_tensor
            nc.vector.memset(xb[:, :, :, 0:3], 0.0).then_inc(consts, 1)
            nc.vector.memset(ones[:, :], 1.0).then_inc(consts, 1)
            nc.vector.memset(ones_g[:, :], float(GROUPS) / DS / X_SCALE ** 2).then_inc(consts, 1)
            nc.vector.memset(eps[:, :], EPS / X_SCALE ** 2).then_inc(consts, 1)
            for r in range(4):
                nc.vector.memset(bz[:, :, r, :], 0.0).then_inc(consts, 1)
            dve.wait_ge(small_in, 16 * 6)
            TT(vb[:, :], vb[:, :], vm[:, :], ALU.mult).then_inc(setup, 1)
            dve.wait_ge(setup, 1)
            TS(vm[:, :], vm[:, :], 1.0 / (X_SCALE * W_SCALE), None, ALU.mult).then_inc(setup, 1)
            dve.wait_ge(setup, 2)
            TT(sc3[:, :], vm[:, ZT:], cw[:, :, 3], ALU.mult).then_inc(setup, 1)
            TT(bi3[:, :], vb[:, ZT:], cw[:, :, 3], ALU.mult).then_inc(setup, 1)
            dve.wait_ge(setup, 4)
            TT(bi3[:, :], bi3[:, :], cb[:, :], ALU.add).then_inc(setup, 1)

            def convolve(p, slot, c, tile):
                dve.wait_ge(tile_free, tile + 2)
                for k in (2, 1, 0):
                    for j in range(2):
                        if k < 2:
                            dve.wait_ge(convolved, 6 * p + 2 * (1 - k) + j + 1)
                        STT(out=acc[:, slot, j, :], in0=xb[:, slot, j, k:k + L], scalar=cw[:, c + j, k:k + 1],
                            in1=acc[:, slot, j, :], op0=ALU.mult, op1=ALU.add).then_inc(convolved, 1)

            def tokens(n, s, b, g):
                dve.wait_ge(transposed, n + 1)
                if not (static(n) and n < 2):
                    dve.wait_ge(heads_done, n - 1)
                dt = keep["dt_tok"][:, :, b, GH * g:GH * g + GH]
                TT(xt[:, s, :, :].rearrange("p m (h f) -> p m h f", h=GH),
                   pt[:, :, :].rearrange("p m (h f) -> p m h f", h=GH), bcast(dt, 3, HD), ALU.mult).then_inc(xt_done, 1)

            def scan(n, s, count):
                dve.wait_ge(dec_in[s], count)
                if not (static(n) and n < 2):
                    dve.wait_ge(heads_done, n - 1)
                for h in range(GH):
                    nc.vector.tensor_tensor_scan(dec1[:, s, h, :], dec[:, s, h, P:L], ident[:, 0:L1], 0.0,
                                                 ALU.mult, ALU.add).then_inc(scanned, 1)
                dve.wait_ge(scanned, 8 * n + 4)
                for h in range(GH):
                    nc.vector.tensor_tensor_scan(dec[:, s, h, :], dec[:, s, h, :], ident[:, :], 0.0,
                                                 ALU.mult, ALU.add).then_inc(scanned, 1)

            def weigh(n, s):
                dve.wait_ge(cb_copied, n + 1)
                dve.wait_ge(scanned, 8 * n + 8)
                TT(dec[:, s, :, :], dec[:, s, :, :], bcast(pg[:, 0:L], 1, GH), ALU.mult).then_inc(weighted, 1)

            def tail_products(b):
                dve.wait_ge(activated, 10 * b + 2)
                if not (static(b) and b == 0):
                    dve.wait_ge(cb_done, 8 * b)
                TT(tailp[:, :, :], bz[:, :, :, L - 1], bcast(cs[:, :, L - 1], 2, 4), ALU.mult).then_inc(tailp_done, 1)

            def tail_weights(b):
                if not (static(b) and b == 0):
                    dve.wait_ge(gated, 8 * b)
                for hh in range(2):
                    rows = slice(HD * hh, HD * hh + HD)
                    dt = keep["dt_tail"][rows, b, :].rearrange("p (g q e) -> p g q e", q=2, e=2)[:, :, :, hh]
                    TT(tailw[rows, :, :], dt, bcast(pg[rows, 400:408], 2, 2), ALU.mult).then_inc(tailw_done, 1)

            def output(n, s, g):
                dve.wait_ge(heads_done, n + 1)
                if not (static(n) and n < 4):
                    dve.wait_ge(lo_done, n - 3)
                    dve.wait_ge(hi_done, n - 3)
                for j in range(2):
                    c = 2 * g + j
                    STT(out=yg[:, s, j, :], in0=xs[:, g % 4, j, :], scalar=dp[:, c:c + 1], in1=py[j][:, 0:L],
                        op0=ALU.mult, op1=ALU.add).then_inc(y_step, 1)

            def invert(n, tile):
                dve.wait_ge(tile_free, tile + 1)
                if not (static(n) and n == 0):
                    dve.wait_ge(normed, n)
                nc.vector.reciprocal(rs[:, :], sd[:, :]).then_inc(rs_done, 1)

            dve.wait_ge(consts, 8)
            convolve(0, 0, ZT + 2, 0)
            convolve(1, 1, ZT, 2)
            convolve(2, 0, 0, 4)
            tail_products(0)
            scan(0, 0, 16)

            def batch(b):
                for g in range(GROUPS):
                    u = 8 * b + g
                    tokens(u, g % 2, b, g)
                    weigh(u, g % 2)
                    tile, nt = Mamba.base(b, g), Mamba.norm(b, g)
                    if g < GROUPS - 1:
                        convolve(Mamba.pair(b, g + 1), (g + 1) % 2, 2 * (g + 1), tile)
                    if not (static(b) and b == 0 and g == 0):
                        output(u - 1, (g - 1) % 4, (g - 1) % 8)
                    if not Mamba.starts(b, g):
                        invert(u - 2, tile + nt)
                    if g == GROUPS - 1 and not last(b):
                        p = 10 * b + 10
                        convolve(p, 0, ZT + 2, tile + 1)
                        convolve(p + 1, 1, ZT, tile + 3)
                        convolve(p + 2, 0, 0, tile + Mamba.x(b, g))
                        tail_products(b + 1)
                    if g == 0:
                        tail_weights(b)
                    if not (last(b) and g == GROUPS - 1):
                        scan(u + 1, (g + 1) % 2, 16 * (4 * b + (g + 1) // 2 + 1))

            batches(dve, batch)
            end = Mamba.base(NB - 1, 7) + 1
            output(UNITS - 1, 3, 7)
            invert(UNITS - 2, end)
            invert(UNITS - 1, end + 1)

        @block.gpsimd
        def _(pool):
            TT = nc.gpsimd.tensor_tensor

            def weigh1(n, s):
                pool.wait_ge(cb_copied, n + 1)
                pool.wait_ge(scanned, 8 * n + 4)
                TT(dec1[:, s, :, :], dec1[:, s, :, :], bcast(cb1[:, :], 1, GH), ALU.mult).then_inc(weighted1, 1)

            def gate(n, s, g, b1):
                pool.wait_ge(tailw_done, 2 * b1)
                pool.wait_ge(y_step, 2 * n + 2)
                if not (static(n) and n == 0):
                    pool.wait_ge(tail_step, 2 * n)
                TT(tailx[:, :], xs[:, g % 4, :, L - 1], tailw[:, g, :], ALU.mult).then_inc(tail_step, 1)
                pool.wait_ge(tail_step, 2 * n + 1)
                TT(yg[:, s, :, L - 1], yg[:, s, :, L - 1], tailx[:, :], ALU.add).then_inc(tail_step, 1)
                pool.wait_ge(tail_step, 2 * n + 2)
                TT(yg[:, s, :, :], yg[:, s, :, :], zs[:, g % 4, :, :], ALU.mult).then_inc(gated, 1)

            def normalise(n, s):
                pool.wait_ge(rs_done, n + 1)
                pool.wait_ge(squared, n + 1)
                TT(yg[:, s, :, :], yg[:, s, :, :], bcast(rs[:, :], 1, 2), ALU.mult).then_inc(normed, 1)

            def sum_squares(n):
                pool.wait_ge(squared, n + 1)
                TT(sq[:, 0, :], sq[:, 0, :], sq[:, 1, :], ALU.add).then_inc(sq_summed, 1)

            def low(n, s, g):
                pool.wait_ge(hi_done, n + 1)
                TT(yn_lo[:, 2 * g:2 * g + 2, :], yg[:, s, :, :], yn_hi[:, 2 * g:2 * g + 2, :],
                   ALU.subtract).then_inc(lo_done, 1)

            def add_residual(b, half, tile):
                pool.wait_ge(tile_free, tile + HT)
                pool.wait_ge(h_in, 16 * (2 * b + half + 1))
                TT(h1[:, :, :], h1[:, :, :], hb[:, :, :], ALU.add).then_inc(h1_done, 1)

            def sum_tiles(b, j, tiles, before):
                pool.wait_ge(piece_in[j], 16 * b + 16)
                if not (static(b) and b == 0 and before == 0):
                    pool.wait_ge(piece_step, 16 * b + before)
                bufs = [rot_in[:, j % 2, :], rot_mid[:, :]]
                for level in range(tiles.bit_length() - 1):
                    src, dst = (x.rearrange("p (a two b) -> p a two b", two=2, b=(1 << level) * PIECE // tiles)
                                for x in (bufs[level % 2], bufs[1 - level % 2]))
                    TT(dst[:, :, 0, :], src[:, :, 0, :], src[:, :, 1, :], ALU.add).then_inc(piece_step, 1)
                    TT(dst[:, :, 1, :], src[:, :, 0, :], src[:, :, 1, :], ALU.subtract).then_inc(piece_step, 1)
                    before += 2
                    pool.wait_ge(piece_step, 16 * b + before)

            def batch(b):
                for g in range(GROUPS):
                    u = 8 * b + g
                    weigh1(u, g % 2)
                    if not (static(b) and b == 0 and g == 0):
                        gate(u - 1, (g - 1) % 4, (g - 1) % 8, b if g == 0 else b + 1)
                    if not Mamba.starts(b, g):
                        normalise(u - 2, (g - 2) % 4)
                    if not (static(b) and b == 0 and g == 0):
                        sum_squares(u - 1)
                    if g == 2:
                        sum_tiles(b, 0, IT, 0)
                        sum_tiles(b, 1, KT, 8)
                    half = Mamba.out_half(b, g)
                    if half is not None:
                        add_residual(b - 1, half, Mamba.base(b, g) + Mamba.OUT)
                    if half == 1:
                        low(u - 3, (g - 3) % 4, (g - 3) % 8)
                    if not (Mamba.starts(b, g) or half == 0):
                        low(u - 2, (g - 2) % 4, (g - 2) % 8)
                    if g == 5:
                        sum_tiles(b, 2, KT, 12)

            batches(pool, batch)
            end = Mamba.base(NB - 1, 7) + 1
            gate(UNITS - 1, 3, 7, NB)
            normalise(UNITS - 2, 2)
            sum_squares(UNITS - 1)
            low(UNITS - 2, 2, 6)
            normalise(UNITS - 1, 3)
            low(UNITS - 1, 3, 7)
            for half in range(2):
                add_residual(NB - 1, half, end + 2 + HT * half)


def rotate_phase(nc, t, scratch, ffn):
    with ExitStack() as ctx:
        def sb(name, shape, dt=F32):
            return ctx.enter_context(nc.sbuf_tensor(name, shape, dt))

        def sem(name):
            return ctx.enter_context(nc.semaphore("r_" + name))

        SLOTS = 4
        NU, ND = 2 * NB // 4, NB // 4
        had = sb("r_had", [P, P])
        wst = sb("r_wst", [P, SLOTS, 4, PIECE])
        su, sd = sb("r_su", [P, KT]), sb("r_sd", [P, IT])
        ps = [ctx.enter_context(nc.psum_tensor(f"r_ps{i}", [P, 512], F32)) for i in range(8)]
        small_in, scales = sem("small_in"), sem("scales")
        w_in = [sem(f"w_in{i}") for i in range(SLOTS)]
        rotated, hi_done, lo_done = sem("rotated"), sem("hi_done"), sem("lo_done")
        block = ctx.enter_context(nc.Block())
        turns = [("ug", c) for c in range(NU)] + [("down", c) for c in range(ND)]

        @block.sync
        def _(sp):
            for dst, src in ((had, "hadamard"), (su, "SU_ug"), (sd, "SU_dp"),
                             (ffn["ws_ug"], "Wscale_ug"), (ffn["ws_dp"], "Wscale_dp")):
                sp.dma_start(dst[:, :], t[src]).then_inc(small_in, 16)
            for n, (kind, c) in enumerate(turns):
                if n >= SLOTS:
                    sp.wait_ge(rotated, 4 * (n - SLOTS + 1))
                sp.dma_start(wst[:, n % SLOTS, :, :], scratch[kind + "_sum"][4 * c:4 * c + 4]
                             .rearrange("c p n -> p c n")).then_inc(w_in[n % SLOTS], 16)

        def target(n, q, which):
            kind, c = turns[n]
            bank = ps[4 * (n % 2) + q]
            if kind == "ug":
                return [(ffn["ug_" + which][:, q, 4 * c * UCOLS:4 * (c + 1) * UCOLS], bank[:, :], su[:, q:q + 1])]
            v = bank[:, :].rearrange("p (c k n) -> p c k n", c=4, k=4)
            return [(ffn["d_" + which][:, 4 * q + j, 4 * c * DCOLS:4 * (c + 1) * DCOLS].rearrange("p (c n) -> p c n", c=4),
                     v[:, :, j, :], sd[:, 4 * q + j:4 * q + j + 1]) for j in range(4)]

        @block.vector
        def _(dve):
            TS = nc.vector.tensor_scalar
            dve.wait_ge(small_in, 16 * 5)
            TS(su[:, :], su[:, :], W_SCALE / float(np.sqrt(D)), None, ALU.mult).then_inc(scales, 1)
            TS(sd[:, :], sd[:, :], W_SCALE / float(np.sqrt(INTER)), None, ALU.mult).then_inc(scales, 1)
            TS(ffn["ws_ug"][:, :], ffn["ws_ug"][:, :], 1.0 / (X_SCALE * W_SCALE), None, ALU.mult).then_inc(scales, 1)
            TS(ffn["ws_dp"][:, :], ffn["ws_dp"][:, :], 1.0 / W_SCALE, None, ALU.mult).then_inc(scales, 1)
            dve.wait_ge(scales, 4)
            for n in range(len(turns)):
                for q in range(4):
                    dve.wait_ge(hi_done, 4 * n + q + 1)
                    for (lo, src, scale), (hi, _, _) in zip(target(n, q, "lo"), target(n, q, "hi")):
                        ins = nc.vector.scalar_tensor_tensor(out=lo, in0=src, scalar=scale, in1=hi,
                                                             op0=ALU.mult, op1=ALU.subtract)
                    ins.then_inc(lo_done, 1)

        @block.scalar
        def _(act):
            act.wait_ge(scales, 4)
            for n in range(len(turns)):
                for q in range(4):
                    act.wait_ge(rotated, 4 * n + q + 1)
                    for hi, src, scale in target(n, q, "hi"):
                        ins = act.activation(hi, src, ACT.Identity, scale=scale)
                    ins.then_inc(hi_done, 1)

        @block.tensor
        def _(pe):
            pe.wait_ge(small_in, 16 * 5)
            for n, (kind, c) in enumerate(turns):
                s = n % SLOTS
                pe.wait_ge(w_in[s], 16 * (n // SLOTS + 1))
                for q in range(4):
                    if n >= 2:
                        pe.wait_ge(lo_done, 4 * (n - 2) + q + 1)
                    width = (UCOLS if kind == "ug" else 4 * DCOLS)
                    nc.tensor.matmul(ps[4 * (n % 2) + q][:, :], had[:, :], wst[:, s, :, width * q:width * (q + 1)],
                                     start=True, stop=True).then_inc(rotated, 1)


def ffn_phase(nc, t, scratch, keep, ffn, out):
    with ExitStack() as ctx:
        def sb(name, shape, dt=F32):
            return ctx.enter_context(nc.sbuf_tensor(name, shape, dt))

        def sem(name):
            return ctx.enter_context(nc.semaphore("f_" + name))

        h1 = sb("f_h1", [P, 2, KT, L])
        xc, sq = sb("f_xc", [P, KT, L]), sb("f_sq", [P, KT, L])
        sd, rs = sb("f_sd", [P, L]), sb("f_rs", [P, L])
        x2 = sb("f_x2", [P, 2, KT, L], F16)
        sg = sb("f_sg", [P, 2, L])
        mid = sb("f_mid", [P, 2, L])
        m_hi, m_lo = sb("f_m_hi", [P, IT, L], F16), sb("f_m_lo", [P, IT, L], F16)
        o = sb("f_o", [P, KT, L])
        eps = sb("f_eps", [P, 1])
        ws_ug, ws_dp = ffn["ws_ug"], ffn["ws_dp"]
        pu = [ctx.enter_context(nc.psum_tensor(f"f_pu{i}", [P, 512], F32)) for i in range(2)]
        pgt = [ctx.enter_context(nc.psum_tensor(f"f_pg{i}", [P, 512], F32)) for i in range(2)]
        pd = [ctx.enter_context(nc.psum_tensor(f"f_pd{i}", [P, 512], F32)) for i in range(2)]
        pm = ctx.enter_context(nc.psum_tensor("f_pm", [P, 512], F32))
        pv = ctx.enter_context(nc.psum_tensor("f_pv", [P, 512], F32))
        consts = sem("consts")
        h1_in = [sem(f"h1_in{i}") for i in range(2)]
        mean_done, centered, squared, var_done, sd_done, rs_done, normed = (sem(x) for x in (
            "mean_done", "centered", "squared", "var_done", "sd_done", "rs_done", "normed"))
        x_hi, x_lo = sem("x_hi"), sem("x_lo")
        gate_mm, up_mm, gate_act, product, mid_hi, mid_lo = (sem(x) for x in (
            "gate_mm", "up_mm", "gate_act", "product", "mid_hi", "mid_lo"))
        down_mm, summed, stored = sem("down_mm"), sem("summed"), sem("stored")
        block = ctx.enter_context(nc.Block())
        AT_MEAN, AT_VAR = 3, 7

        def pairs(eng, body):
            body(0, 0)
            body(1, 1)
            with eng.Fori(1, NB // 2 - 1) as i:
                body(2 * i, 0)
                body(2 * i + 1, 1)
            body(NB - 2, 0)
            body(NB - 1, 1)

        def more(b):
            return not (static(b) and b == NB - 1)

        @block.sync
        def _(sp):
            sp.dma_start(h1[:, 0, :, :], scratch["h1"][0]).then_inc(h1_in[0], 16)

            def batch(b, s):
                if more(b):
                    if not (static(b) and b == 0):
                        sp.wait_ge(summed, 4 * b)
                    sp.dma_start(h1[:, 1 - s, :, :], scratch["h1"][b + 1]).then_inc(h1_in[1 - s], 16)
                sp.wait_ge(summed, 4 * b + 4)
                sp.dma_start(out[b], o[:, :, :]).then_inc(stored, 16)

            pairs(sp, batch)
            sp.wait_ge(stored, 16 * NB)

        @block.tensor
        def _(pe):
            ones = keep["ones_d"]

            def moments(dst, src, ins_sem):
                for k in range(KT):
                    ins = nc.tensor.matmul(dst[:, 0:L], ones[:, :], src[:, k, :], start=k == 0, stop=k == KT - 1)
                ins.then_inc(ins_sem, 1)

            def mean(n, s):
                pe.wait_ge(h1_in[s], (n - s) * 8 + 16)
                if not (static(n) and n == 0):
                    pe.wait_ge(centered, n)
                moments(pm, h1[:, s, :, :], mean_done)

            def var(n):
                pe.wait_ge(squared, n + 1)
                if not (static(n) and n == 0):
                    pe.wait_ge(sd_done, n)
                moments(pv, sq, var_done)

            def split_mm(dst, k_tiles, w_hi, w_lo, x_hi, x_lo, done):
                for k in range(k_tiles):
                    for m, (w, x) in enumerate(((w_hi, x_hi), (w_hi, x_lo), (w_lo, x_hi))):
                        ins = nc.tensor.matmul(dst, w(k), x(k), start=k == 0 and m == 0,
                                               stop=k == k_tiles - 1 and m == 2)
                ins.then_inc(done, 1)

            def wide(dst, col, done):
                cols = slice(col, col + P)
                split_mm(dst[:, 0:L], KT, lambda k: ffn["ug_hi"][:, k, cols], lambda k: ffn["ug_lo"][:, k, cols],
                         lambda k: x2[:, 0, k, :], lambda k: x2[:, 1, k, :], done)

            pe.wait_ge(consts, 1)
            mean(0, 0)
            var(0)

            def batch(b, s):
                pe.wait_ge(x_lo, b + 1)
                pe.wait_ge(x_hi, b + 1)
                for j in range(IT):
                    n = 16 * b + j
                    if not (static(b) and b == 0 and j < 2):
                        pe.wait_ge(gate_act, n - 1)
                    wide(pgt[j % 2], INTER + j * P, gate_mm)
                    if not (static(b) and b == 0 and j < 2):
                        pe.wait_ge(product, n - 1)
                    wide(pu[j % 2], j * P, up_mm)
                    if more(b) and j == AT_MEAN:
                        mean(b + 1, 1 - s)
                    if more(b) and j == AT_VAR:
                        var(b + 1)
                for j in range(KT):
                    if not (static(b) and b == 0 and j < 2):
                        pe.wait_ge(summed, 4 * b + j - 1)
                    cols = slice(j * P, j * P + P)
                    if j == 0:
                        pe.wait_ge(mid_lo, 16 * b + 14)
                        pe.wait_ge(mid_hi, 16 * b + 14)
                    for k in range(IT):
                        if j == 0 and k >= 14:
                            pe.wait_ge(mid_lo, 16 * b + k + 1)
                            pe.wait_ge(mid_hi, 16 * b + k + 1)
                        for m, (w, x) in enumerate((("d_hi", m_hi), ("d_hi", m_lo), ("d_lo", m_hi))):
                            ins = nc.tensor.matmul(pd[j % 2][:, 0:L], ffn[w][:, k, cols], x[:, k, :],
                                                   start=k == 0 and m == 0, stop=k == IT - 1 and m == 2)
                    ins.then_inc(down_mm, 1)

            pairs(pe, batch)

        @block.scalar
        def _(act):
            A = act.activation

            def square(n):
                act.wait_ge(centered, n + 1)
                if not (static(n) and n == 0):
                    act.wait_ge(var_done, n)
                A(sq[:, :, :], xc[:, :, :], ACT.Square).then_inc(squared, 1)

            def deviation(n):
                act.wait_ge(var_done, n + 1)
                if not (static(n) and n == 0):
                    act.wait_ge(rs_done, n)
                A(sd[:, :], pv[:, 0:L], ACT.Sqrt, bias=eps[:, 0:1]).then_inc(sd_done, 1)

            def high(n, mm):
                act.wait_ge(normed, n + 1)
                if mm is not None:
                    act.wait_ge(up_mm, mm)
                A(x2[:, 0, :, :], xc[:, :, :], ACT.Identity).then_inc(x_hi, 1)

            act.wait_ge(consts, 1)
            square(0)
            deviation(0)
            high(0, None)

            def mid_high(n, j):
                act.wait_ge(product, n + 1)
                A(m_hi[:, j, :], mid[:, j % 2, :], ACT.Identity).then_inc(mid_hi, 1)

            def batch(b, s):
                for j in range(IT):
                    n = 16 * b + j
                    act.wait_ge(gate_mm, n + 1)
                    if not (static(b) and b == 0 and j < 2):
                        act.wait_ge(product, n - 1)
                    A(sg[:, j % 2, :], pgt[j % 2][:, 0:L], ACT.Silu, scale=ws_ug[:, IT + j:IT + j + 1]).then_inc(gate_act, 1)
                    if j == 0 and not (static(b) and b == 0):
                        act.wait_ge(down_mm, 4 * b)
                    if j:
                        mid_high(n - 1, j - 1)
                    if more(b) and j == AT_MEAN + 1:
                        square(b + 1)
                    if more(b) and j == AT_VAR + 1:
                        deviation(b + 1)
                mid_high(16 * b + IT - 1, IT - 1)
                if more(b):
                    high(b + 1, 16 * b + 16)

            pairs(act, batch)

        @block.vector
        def _(dve):
            TT, STT = nc.vector.tensor_tensor, nc.vector.scalar_tensor_tensor
            nc.vector.memset(eps[:, :], EPS).then_inc(consts, 1)

            def center(n, s):
                dve.wait_ge(mean_done, n + 1)
                if not (static(n) and n == 0):
                    dve.wait_ge(x_lo, n)
                    dve.wait_ge(x_hi, n)
                TT(xc[:, :, :], h1[:, s, :, :], bcast(pm[:, 0:L], 1, KT), ALU.subtract).then_inc(centered, 1)

            def normalise(n):
                dve.wait_ge(sd_done, n + 1)
                if not (static(n) and n == 0):
                    dve.wait_ge(normed, n)
                nc.vector.reciprocal(rs[:, :], sd[:, :]).then_inc(rs_done, 1)
                dve.wait_ge(rs_done, n + 1)
                dve.wait_ge(squared, n + 1)
                STT(out=xc[:, :, :], in0=xc[:, :, :], scalar=X_SCALE, in1=bcast(rs[:, :], 1, KT),
                    op0=ALU.mult, op1=ALU.mult).then_inc(normed, 1)

            dve.wait_ge(consts, 1)
            center(0, 0)
            normalise(0)

            def mid_low(n, j):
                dve.wait_ge(mid_hi, n + 1)
                TT(m_lo[:, j, :], mid[:, j % 2, :], m_hi[:, j, :], ALU.subtract).then_inc(mid_lo, 1)

            def batch(b, s):
                for j in range(IT):
                    n = 16 * b + j
                    dve.wait_ge(up_mm, n + 1)
                    dve.wait_ge(gate_act, n + 1)
                    if not (static(b) and b == 0 and j < 2):
                        dve.wait_ge(mid_lo, n - 1)
                    STT(out=mid[:, j % 2, :], in0=pu[j % 2][:, 0:L], scalar=ws_ug[:, j:j + 1], in1=sg[:, j % 2, :],
                        op0=ALU.mult, op1=ALU.mult).then_inc(product, 1)
                    if j:
                        mid_low(n - 1, j - 1)
                    if more(b) and j == AT_MEAN:
                        center(b + 1, 1 - s)
                    if more(b) and j == AT_VAR + 1:
                        normalise(b + 1)
                mid_low(16 * b + IT - 1, IT - 1)
                for j in range(KT):
                    dve.wait_ge(down_mm, 4 * b + j + 1)
                    if j == 0 and not (static(b) and b == 0):
                        dve.wait_ge(stored, 16 * b)
                    STT(out=o[:, j, :], in0=pd[j % 2][:, 0:L], scalar=ws_dp[:, j:j + 1], in1=h1[:, s, j, :],
                        op0=ALU.mult, op1=ALU.add).then_inc(summed, 1)

            pairs(dve, batch)

        @block.gpsimd
        def _(pool):
            def low(n):
                pool.wait_ge(x_hi, n + 1)
                nc.gpsimd.tensor_tensor(x2[:, 1, :, :], xc[:, :, :], x2[:, 0, :, :], ALU.subtract).then_inc(x_lo, 1)

            low(0)
            with pool.Fori(1, NB) as n:
                low(n)


def build(nc, t, out):
    def scr(name, shape, dt=F32):
        return nc.dram_tensor(f"scratch_{name}", shape, dt, kind="Internal").ap()

    scratch = {"h": scr("h", (NB, P, KT, L)), "xn": scr("xn", (NB, P, 2, KT, L), F16),
               "a": scr("a", (NB, HEADS, L)), "dt_tail": scr("dt_tail", (NB, HEADS, 1)),
               "h1": scr("h1", (NB, P, KT, L)),
               "ug_sum": scr("ug_sum", (2 * NB, P, PIECE)), "down_sum": scr("down_sum", (NB, P, PIECE))}
    s4_phase(nc, t, scratch)
    with ExitStack() as ctx:
        def sb(name, shape, dt=F32):
            return ctx.enter_context(nc.sbuf_tensor(name, shape, dt))

        keep = {"ident": sb("ident", [P, L]), "ones_d": sb("ones_d", [P, P])}
        with ExitStack() as inner:
            def sbi(name, shape, dt=F32):
                return inner.enter_context(nc.sbuf_tensor(name, shape, dt))

            keep |= {"dt_tok": sbi("dt_tok", [P, 2, NB, HEADS]), "dt_tail": sbi("dt_tail", [P, NB, HEADS]),
                     "w_hi": sbi("w_hi", [P, KT, P * PT], F16), "w_lo": sbi("w_lo", [P, KT, P * PT], F16),
                     "o_hi": sbi("o_hi", [P, ZT, D], F16), "o_lo": sbi("o_lo", [P, ZT, D], F16)}
            with nc.sbuf_tensor("a_keep", [P, 4, L], F32) as a_keep:
                keep["a"] = a_keep
                prep_phase(nc, t, scratch, keep)
            mamba_phase(nc, t, scratch, keep)
        with ExitStack() as inner:
            def sbi(name, shape, dt=F32):
                return inner.enter_context(nc.sbuf_tensor(name, shape, dt))

            ffn = {"ug_hi": sbi("ug_hi", [P, KT, 2 * INTER], F16), "ug_lo": sbi("ug_lo", [P, KT, 2 * INTER], F16),
                   "d_hi": sbi("d_hi", [P, IT, D], F16), "d_lo": sbi("d_lo", [P, IT, D], F16),
                   "ws_ug": sbi("ws_ug", [P, 2 * IT]), "ws_dp": sbi("ws_dp", [P, KT])}
            rotate_phase(nc, t, scratch, ffn)
            ffn_phase(nc, t, scratch, keep, ffn, out)


def _hadamard(n):
    h = np.ones((1, 1), np.float32)
    while h.shape[0] < n:
        h = np.block([[h, h], [h, -h]])
    return h.astype(np.float32)


def _tiles(v):
    return np.ascontiguousarray(v.reshape(-1, P).T)


def _pieces(w, cols):
    w = w.reshape(-1, P, w.shape[1] // cols, cols).transpose(2, 1, 0, 3)
    return np.ascontiguousarray(w).reshape(-1, P, PIECE)


def layout(i):
    w_in, mup = i["L0_attn_W_in"], i["L0_attn_mup_vector"]
    b_in, n = i["L0_attn_b_in"], P * PT
    return {
        "C": np.ascontiguousarray(i["x"].transpose(3, 2, 1, 0)).reshape(P, NH, NB),
        "cls": _tiles(i["cls_tok"].reshape(-1)),
        "log_dt": i["L0_tok_log_dt"],
        "B_re": np.ascontiguousarray(i["L0_tok_B_ri"][..., 0].T),
        "B_im": np.ascontiguousarray(i["L0_tok_B_ri"][..., 1].T),
        "inv_A_real": np.ascontiguousarray(i["L0_tok_inv_A_real"].T),
        "A_imag": np.ascontiguousarray(i["L0_tok_A_imag"].T),
        "W_in": w_in,
        "b_in": _tiles(b_in[:n]),
        "mup": _tiles(mup[:n]),
        "dt_vec": np.ascontiguousarray(np.stack(
            [np.tile(v, P // HEADS) for v in (b_in[n:], mup[n:], i["L0_attn_dt_bias"], i["L0_attn_A_log"])], 1)),
        "conv_w": np.ascontiguousarray(i["L0_attn_conv_w"].reshape(CT, P, 4).transpose(1, 0, 2)),
        "conv_b": _tiles(i["L0_attn_conv_b"]),
        "D": _tiles(np.repeat(i["L0_attn_D_param"], HD)),
        "norm_w": _tiles(i["L0_attn_norm_w"]),
        "W_out": i["L0_attn_W_out"],
        "b_out": _tiles(i["L0_attn_b_out"]),
        "SU_ug": _tiles(i["L0_ffn_SU_ug"]),
        "SU_dp": _tiles(i["L0_ffn_SU_dp"]),
        "Wscale_ug": _tiles(i["L0_ffn_Wscale_ug"]),
        "Wscale_dp": _tiles(i["L0_ffn_Wscale_dp"]),
        "W_ug": _pieces(np.concatenate([i["L0_ffn_W_up"], i["L0_ffn_W_gate"]]).T, UCOLS),
        "W_down": _pieces(i["L0_ffn_W_down"].T, DCOLS),
        "hadamard": _hadamard(P),
        "ident": np.eye(P, L, dtype=np.float32),
    }


def kernel(**inputs):
    import concourse.bacc as bacc
    from concourse.bass_utils import run_bass_kernel_spmd

    arrays = {f"in_{k}": np.ascontiguousarray(v)
              for k, v in layout({k: np.asarray(v) for k, v in inputs.items()}).items()}
    nc = bacc.Bacc("TRN2", target_bir_lowering=False, num_devices=1)
    t = {k[3:]: nc.dram_tensor(k, a.shape, F32, kind="ExternalInput").ap() for k, a in arrays.items()}
    out = nc.dram_tensor("out", (NB, P, KT, L), F32, kind="ExternalOutput").ap()
    build(nc, t, out)
    r = run_bass_kernel_spmd(nc, [arrays], core_ids=[0])
    got = r.results[0]["out"]
    return np.ascontiguousarray(got.transpose(0, 3, 2, 1)).reshape(NB, L, D)
```
